# Optimizing a Trainium2 kernel written in Bass

```python
import numpy as np
import jax
import jax.numpy as jnp

def _softmax(x, axis=-1):
    return jax.nn.softmax(x, axis=axis)

def _gelu(x):
    return jax.nn.gelu(x, approximate=True)

def _silu(x):
    return jax.nn.silu(x)

def _sigmoid(x):
    return jax.nn.sigmoid(x)

def _layernorm(x, axis=-1, eps=1e-05):
    m = jnp.mean(x, axis=axis, keepdims=True)
    v = jnp.var(x, axis=axis, keepdims=True)
    return (x - m) / jnp.sqrt(v + eps)

def _scatter_add(tgt, idx, src, axis=0):
    return tgt.at[idx].add(src)

def _segment_sum(src, seg, n):
    return jax.ops.segment_sum(src, seg, n)
kernel_name = 'mk_early_fusion_d4_tok_img768_r4_2c52f2'

def setup_inputs(seed: int=0):
    np.random.seed(seed)
    _w = jnp.asarray

    def _rec_inputs():
        import jax
        import jax.numpy as jnp
        _rk = jax.random.key(seed)
        x = -0.000222058 + 0.999998 * jax.random.normal(jax.random.fold_in(_rk, 1), (16, 3, 84, 84), jnp.float32)
        txt = 0.000626447 + 0.554253 * jax.random.normal(jax.random.fold_in(_rk, 2), (16, 77, 192), jnp.float32)
        return (x, txt)
    x, txt = _rec_inputs()

    def _L0_tok_setup():
        import jax, jax.numpy as jnp
        import numpy as np
        from jax import lax
        HIDDEN = 192
        C_IN = 3
        PATCH = 16
        SIDE = 32
        NUM_PATCHES = SIDE * SIDE

        def _position_ids(nb_h, nb_w):
            boundaries = np.arange(1.0 / SIDE, 1.0, 1.0 / SIDE, dtype=np.float32)
            frac_h = np.arange(0.0, 1.0 - 1e-06, 1.0 / nb_h, dtype=np.float32)
            frac_w = np.arange(0.0, 1.0 - 1e-06, 1.0 / nb_w, dtype=np.float32)
            bh = np.searchsorted(boundaries, frac_h, side='right')
            bw = np.searchsorted(boundaries, frac_w, side='right')
            return jnp.asarray((bh[:, None] * SIDE + bw).reshape(-1), dtype=jnp.int32)
        key = jax.random.key(seed)
        k1, k2, k3 = jax.random.split(key, 3)
        pixel_values = jax.random.normal(k1, (32, C_IN, 128, 128), dtype=jnp.float32)
        conv_w = jax.random.normal(k2, (HIDDEN, C_IN, PATCH, PATCH), dtype=jnp.float32) * 0.02
        conv_b = jnp.zeros((HIDDEN,), dtype=jnp.float32)
        pos_table = jax.random.normal(k3, (NUM_PATCHES, HIDDEN), dtype=jnp.float32) * 0.02
        return {'pixel_values': pixel_values, 'conv_w': conv_w, 'conv_b': conv_b, 'pos_table': pos_table}
    _L0_tok_all = _L0_tok_setup()
    _L0_tok_in = {k: v for k, v in _L0_tok_all.items() if k in ('conv_w', 'conv_b', 'pos_table')}
    del _L0_tok_all

    def _L0_attn_setup():
        import jax, jax.numpy as jnp
        import numpy as np
        EMBED_DIM = 192
        SEQ_LEN = 256
        BATCH = 16
        ALPHA = 0.99
        key = jax.random.key(seed)
        k_x, k_w, k_b = jax.random.split(key, 3)
        d = EMBED_DIM
        x = jax.random.normal(k_x, (BATCH, SEQ_LEN, d), dtype=jnp.float32)
        lim = 1.0 / np.sqrt(d)
        W_qkv = jax.random.uniform(k_w, (3 * d, d), dtype=jnp.float32, minval=-lim, maxval=lim)
        b_qkv = jax.random.uniform(k_b, (3 * d,), dtype=jnp.float32, minval=-lim, maxval=lim)
        return {'x': x, 'W_qkv': W_qkv, 'b_qkv': b_qkv}
    _L0_attn_all = _L0_attn_setup()
    _L0_attn_in = {k: v for k, v in _L0_attn_all.items() if k in ('W_qkv', 'b_qkv')}
    del _L0_attn_all

    def _L0_ffn_setup():
        import jax, jax.numpy as jnp
        import numpy as np
        DIM = 192
        HEADS = 12
        EXPERTS = 8
        HID = 768
        TOP_K = 2
        LN_EPS = 1e-05

        def _layer_norm(x, g, b):
            mu = x.mean(-1, keepdims=True)
            var = ((x - mu) ** 2).mean(-1, keepdims=True)
            return (x - mu) * jax.lax.rsqrt(var + LN_EPS) * g + b

        def _attention(x, qkv_w, qkv_b, proj_w, proj_b):
            B, N, C = x.shape
            hd = C // HEADS
            qkv = (x @ qkv_w + qkv_b).reshape(B, N, 3, HEADS, hd).transpose(2, 0, 3, 1, 4)
            q, k, v = (qkv[0], qkv[1], qkv[2])
            attn = jax.nn.softmax(jnp.einsum('bhnd,bhmd->bhnm', q, k) * hd ** (-0.5), axis=-1)
            o = jnp.einsum('bhnm,bhmd->bhnd', attn, v).transpose(0, 2, 1, 3).reshape(B, N, C)
            return o @ proj_w + proj_b

        def _moe_mlp(xn, gate_w, w1, b1, w2, b2):
            T = xn.shape[0]
            logits = xn @ gate_w
            top_logits, top_idx = jax.lax.top_k(logits, TOP_K)
            top_gates = jax.nn.softmax(top_logits, axis=-1)
            gates = jnp.zeros((T, EXPERTS), xn.dtype).at[jnp.arange(T)[:, None], top_idx].set(top_gates)
            h = jax.nn.gelu(jnp.einsum('td,edh->teh', xn, w1) + b1, approximate=False)
            y = jnp.einsum('teh,ehd->ted', h, w2) + b2
            return jnp.einsum('ted,te->td', y, gates)
        key = jax.random.key(seed)
        ks = jax.random.split(key, 16)
        s = 0.02
        return {'x': jax.random.normal(ks[0], (8, 196, DIM), jnp.float32), 'ln1_g': jnp.ones((DIM,), jnp.float32), 'ln1_b': jnp.zeros((DIM,), jnp.float32), 'qkv_w': jax.random.normal(ks[1], (DIM, 3 * DIM), jnp.float32) * s, 'qkv_b': jnp.zeros((3 * DIM,), jnp.float32), 'proj_w': jax.random.normal(ks[2], (DIM, DIM), jnp.float32) * s, 'proj_b': jnp.zeros((DIM,), jnp.float32), 'ln2_g': jnp.ones((DIM,), jnp.float32), 'ln2_b': jnp.zeros((DIM,), jnp.float32), 'gate_w': jax.random.normal(ks[3], (DIM, EXPERTS), jnp.float32) * s, 'w1': jax.random.normal(ks[4], (EXPERTS, DIM, HID), jnp.float32) * s, 'b1': jnp.zeros((EXPERTS, HID), jnp.float32), 'w2': jax.random.normal(ks[5], (EXPERTS, HID, DIM), jnp.float32) * s, 'b2': jnp.zeros((EXPERTS, DIM), jnp.float32)}
    _L0_ffn_all = _L0_ffn_setup()
    _L0_ffn_in = {k: v for k, v in _L0_ffn_all.items() if k in ('ln1_g', 'ln1_b', 'qkv_w', 'qkv_b', 'proj_w', 'proj_b', 'ln2_g', 'ln2_b', 'gate_w', 'w1', 'b1', 'w2', 'b2')}
    del _L0_ffn_all

    def _L1_attn_setup():
        import jax, jax.numpy as jnp
        import numpy as np
        from jax import lax
        NUM_HEADS = 12
        BETA = 0.2
        KS = 3
        LN_EPS = 1e-05
        key = jax.random.key(seed)
        k1, k2 = jax.random.split(key)
        B, N, C = (4, 256, 192)
        x = jax.random.normal(k1, (B, N, C), dtype=jnp.float32)
        qkv_w = jax.random.normal(k2, (3 * C, C), dtype=jnp.float32) * 0.02
        qkv_b = jnp.zeros((3 * C,), dtype=jnp.float32)
        ln_g = jnp.ones((C,), dtype=jnp.float32)
        ln_b = jnp.zeros((C,), dtype=jnp.float32)
        return {'x': x, 'qkv_w': qkv_w, 'qkv_b': qkv_b, 'ln_g': ln_g, 'ln_b': ln_b}
    _L1_attn_all = _L1_attn_setup()
    _L1_attn_in = {k: v for k, v in _L1_attn_all.items() if k in ('qkv_w', 'qkv_b', 'ln_g', 'ln_b')}
    del _L1_attn_all

    def _L1_ffn_setup():
        import jax, jax.numpy as jnp
        import numpy as np
        D_MODEL, D_FF, N_EXPERTS, TOP_K = (192, 768, 8, 2)
        B, S = (2, 256)
        LN_EPS = 1e-05

        def _layernorm(x, gamma, beta):
            mu = jnp.mean(x, axis=-1, keepdims=True)
            var = jnp.mean(jnp.square(x - mu), axis=-1, keepdims=True)
            return (x - mu) * jax.lax.rsqrt(var + LN_EPS) * gamma + beta
        key = jax.random.key(seed)
        k1, k2, k3, k4 = jax.random.split(key, 4)
        return {'hidden_states': jax.random.normal(k1, (B, S, D_MODEL), dtype=jnp.float32), 'ln_gamma': jnp.ones((D_MODEL,), dtype=jnp.float32), 'ln_beta': jnp.zeros((D_MODEL,), dtype=jnp.float32), 'router_w': jax.random.normal(k2, (D_MODEL, N_EXPERTS), dtype=jnp.float32) * 0.02, 'w1': jax.random.normal(k3, (N_EXPERTS, D_MODEL, D_FF), dtype=jnp.float32) * 0.02, 'w2': jax.random.normal(k4, (N_EXPERTS, D_FF, D_MODEL), dtype=jnp.float32) * 0.02}
    _L1_ffn_all = _L1_ffn_setup()
    _L1_ffn_in = {k: v for k, v in _L1_ffn_all.items() if k in ('ln_gamma', 'ln_beta', 'router_w', 'w1', 'w2')}
    del _L1_ffn_all

    def _L2_attn_setup():
        import jax, jax.numpy as jnp
        import numpy as np
        D, H, WIN, B, S = (192, 12, 64, 2, 256)
        Dh = D // H
        HALF = WIN // 2

        def _layernorm(x, g, b):
            m = jnp.mean(x, axis=-1, keepdims=True)
            v = jnp.mean((x - m) ** 2, axis=-1, keepdims=True)
            return (x - m) / jnp.sqrt(v + 1e-05) * g + b
        key = jax.random.key(seed)
        ks = jax.random.split(key, 16)

        def lin(k, din, dout):
            return jax.random.normal(k, (din, dout), jnp.float32) * 0.02
        inp = {'x': jax.random.normal(ks[0], (B, S, D), jnp.float32)}
        names = ['q_lin', 'k_lin', 'v_lin', 'q_loc', 'k_loc', 'v_loc', 'out']
        for i, n in enumerate(names):
            inp[f'W_{n}'] = lin(ks[i + 1], D, D)
            inp[f'b_{n}'] = jnp.zeros((D,), jnp.float32)
        inp['W_g1'] = lin(ks[8], 3 * D, D)
        inp['b_g1'] = jnp.zeros((D,), jnp.float32)
        inp['W_g2'] = lin(ks[9], D, D)
        inp['b_g2'] = jnp.zeros((D,), jnp.float32)
        inp['gamma1'] = jnp.ones((D,), jnp.float32)
        inp['beta1'] = jnp.zeros((D,), jnp.float32)
        return inp
    _L2_attn_all = _L2_attn_setup()
    _L2_attn_in = {k: v for k, v in _L2_attn_all.items() if k in ('W_q_lin', 'b_q_lin', 'W_k_lin', 'b_k_lin', 'W_v_lin', 'b_v_lin', 'W_q_loc', 'b_q_loc', 'W_k_loc', 'b_k_loc', 'W_v_loc', 'b_v_loc', 'W_out', 'b_out', 'W_g1', 'b_g1', 'W_g2', 'b_g2', 'gamma1', 'beta1')}
    del _L2_attn_all

    def _L2_ffn_setup():
        import jax, jax.numpy as jnp
        import numpy as np
        B, T, D = (2, 512, 192)
        S, R, M, K = (8, 16, 64, 4)
        H, G = (32, 64)

        def _ssinf3(x, P, C, W1, b1, W2, b2, G1, g1b, G2, g2b):
            shp = x.shape
            xf = x.reshape(-1, shp[-1])
            z = jnp.einsum('nd,sdr->nsr', xf, P)
            scores = jnp.einsum('nsr,smr->nsm', z, C)
            topv, topi = jax.lax.top_k(scores, K)
            w = jax.nn.softmax(topv, axis=-1)
            sidx = jnp.arange(S)[None, :, None]
            W1g = W1[sidx, topi]
            b1g = b1[sidx, topi]
            W2g = W2[sidx, topi]
            b2g = b2[sidx, topi]
            h = jax.nn.gelu(jnp.einsum('nsr,nskrh->nskh', z, W1g) + b1g)
            yl = jnp.einsum('nskh,nskhr->nskr', h, W2g) + b2g
            comb = jnp.einsum('nskr,nsk->nsr', yl, w)
            comb = comb.reshape(xf.shape[0], S * R)
            out = jax.nn.gelu(comb @ G1 + g1b) @ G2 + g2b
            return out.reshape(shp)
        key = jax.random.key(seed)
        k = jax.random.split(key, 8)
        rn = lambda kk, shape, s: jax.random.normal(kk, shape, dtype=jnp.float32) * s
        return {'x': rn(k[0], (B, T, D), 1.0), 'P': rn(k[1], (S, D, R), D ** (-0.5)), 'C': rn(k[2], (S, M, R), R ** (-0.5)), 'W1': rn(k[3], (S, M, R, H), R ** (-0.5)), 'b1': jnp.zeros((S, M, H), jnp.float32), 'W2': rn(k[4], (S, M, H, R), H ** (-0.5)), 'b2': jnp.zeros((S, M, R), jnp.float32), 'G1': rn(k[5], (S * R, G), (S * R) ** (-0.5)), 'g1b': jnp.zeros((G,), jnp.float32), 'G2': rn(k[6], (G, D), G ** (-0.5)), 'g2b': jnp.zeros((D,), jnp.float32)}
    _L2_ffn_all = _L2_ffn_setup()
    _L2_ffn_in = {k: v for k, v in _L2_ffn_all.items() if k in ('P', 'C', 'W1', 'b1', 'W2', 'b2', 'G1', 'g1b', 'G2', 'g2b')}
    del _L2_ffn_all

    def _L3_attn_setup():
        import jax, jax.numpy as jnp
        import numpy as np
        N_HEAD = 12
        key = jax.random.key(seed)
        k1, k2, k3 = jax.random.split(key, 3)
        B, L, D = (4, 512, 192)
        x = jax.random.normal(k1, (B, L, D), dtype=jnp.float32)
        w_attn = jax.random.normal(k2, (D, 3 * D), dtype=jnp.float32) * 0.02
        w_proj = jax.random.normal(k3, (D, D), dtype=jnp.float32) * 0.02
        b_proj = jnp.zeros((D,), dtype=jnp.float32)
        return {'x': x, 'w_attn': w_attn, 'w_proj': w_proj, 'b_proj': b_proj}
    _L3_attn_all = _L3_attn_setup()
    _L3_attn_in = {k: v for k, v in _L3_attn_all.items() if k in ('w_attn', 'w_proj', 'b_proj')}
    del _L3_attn_all

    def _L3_ffn_setup():
        import math
        import jax, jax.numpy as jnp
        import numpy as np
        B, L, D = (8, 1024, 192)
        E = 16
        TOP_K = 2
        F_EXP = 4 * D
        F_SH = F_EXP * 2 // 4
        key = jax.random.key(seed)
        ks = jax.random.split(key, 8)
        s = lambda fan_in: 1.0 / math.sqrt(fan_in)
        return {'hidden_states': jax.random.normal(ks[0], (B, L, D), jnp.float32), 'gate_weight': jax.random.uniform(ks[1], (E, D), jnp.float32, -s(D), s(D)), 'Wg': jax.random.uniform(ks[2], (E, F_EXP, D), jnp.float32, -s(D), s(D)), 'Wu': jax.random.uniform(ks[3], (E, F_EXP, D), jnp.float32, -s(D), s(D)), 'Wd': jax.random.uniform(ks[4], (E, D, F_EXP), jnp.float32, -s(F_EXP), s(F_EXP)), 'Ws_g': jax.random.uniform(ks[5], (F_SH, D), jnp.float32, -s(D), s(D)), 'Ws_u': jax.random.uniform(ks[6], (F_SH, D), jnp.float32, -s(D), s(D)), 'Ws_d': jax.random.uniform(ks[7], (D, F_SH), jnp.float32, -s(F_SH), s(F_SH))}
    _L3_ffn_all = _L3_ffn_setup()
    _L3_ffn_in = {k: v for k, v in _L3_ffn_all.items() if k in ('gate_weight', 'Wg', 'Wu', 'Wd', 'Ws_g', 'Ws_u', 'Ws_d')}
    del _L3_ffn_all
    return {'x': x, 'txt': txt, 'L0_tok_conv_w': _L0_tok_in['conv_w'], 'L0_tok_conv_b': _L0_tok_in['conv_b'], 'L0_tok_pos_table': _L0_tok_in['pos_table'], 'L0_attn_W_qkv': _L0_attn_in['W_qkv'], 'L0_attn_b_qkv': _L0_attn_in['b_qkv'], 'L0_ffn_ln1_g': _L0_ffn_in['ln1_g'], 'L0_ffn_ln1_b': _L0_ffn_in['ln1_b'], 'L0_ffn_qkv_w': _L0_ffn_in['qkv_w'], 'L0_ffn_qkv_b': _L0_ffn_in['qkv_b'], 'L0_ffn_proj_w': _L0_ffn_in['proj_w'], 'L0_ffn_proj_b': _L0_ffn_in['proj_b'], 'L0_ffn_ln2_g': _L0_ffn_in['ln2_g'], 'L0_ffn_ln2_b': _L0_ffn_in['ln2_b'], 'L0_ffn_gate_w': _L0_ffn_in['gate_w'], 'L0_ffn_w1': _L0_ffn_in['w1'], 'L0_ffn_b1': _L0_ffn_in['b1'], 'L0_ffn_w2': _L0_ffn_in['w2'], 'L0_ffn_b2': _L0_ffn_in['b2'], 'L1_attn_qkv_w': _L1_attn_in['qkv_w'], 'L1_attn_qkv_b': _L1_attn_in['qkv_b'], 'L1_attn_ln_g': _L1_attn_in['ln_g'], 'L1_attn_ln_b': _L1_attn_in['ln_b'], 'L1_ffn_ln_gamma': _L1_ffn_in['ln_gamma'], 'L1_ffn_ln_beta': _L1_ffn_in['ln_beta'], 'L1_ffn_router_w': _L1_ffn_in['router_w'], 'L1_ffn_w1': _L1_ffn_in['w1'], 'L1_ffn_w2': _L1_ffn_in['w2'], 'L2_attn_W_q_lin': _L2_attn_in['W_q_lin'], 'L2_attn_b_q_lin': _L2_attn_in['b_q_lin'], 'L2_attn_W_k_lin': _L2_attn_in['W_k_lin'], 'L2_attn_b_k_lin': _L2_attn_in['b_k_lin'], 'L2_attn_W_v_lin': _L2_attn_in['W_v_lin'], 'L2_attn_b_v_lin': _L2_attn_in['b_v_lin'], 'L2_attn_W_q_loc': _L2_attn_in['W_q_loc'], 'L2_attn_b_q_loc': _L2_attn_in['b_q_loc'], 'L2_attn_W_k_loc': _L2_attn_in['W_k_loc'], 'L2_attn_b_k_loc': _L2_attn_in['b_k_loc'], 'L2_attn_W_v_loc': _L2_attn_in['W_v_loc'], 'L2_attn_b_v_loc': _L2_attn_in['b_v_loc'], 'L2_attn_W_out': _L2_attn_in['W_out'], 'L2_attn_b_out': _L2_attn_in['b_out'], 'L2_attn_W_g1': _L2_attn_in['W_g1'], 'L2_attn_b_g1': _L2_attn_in['b_g1'], 'L2_attn_W_g2': _L2_attn_in['W_g2'], 'L2_attn_b_g2': _L2_attn_in['b_g2'], 'L2_attn_gamma1': _L2_attn_in['gamma1'], 'L2_attn_beta1': _L2_attn_in['beta1'], 'L2_ffn_P': _L2_ffn_in['P'], 'L2_ffn_C': _L2_ffn_in['C'], 'L2_ffn_W1': _L2_ffn_in['W1'], 'L2_ffn_b1': _L2_ffn_in['b1'], 'L2_ffn_W2': _L2_ffn_in['W2'], 'L2_ffn_b2': _L2_ffn_in['b2'], 'L2_ffn_G1': _L2_ffn_in['G1'], 'L2_ffn_g1b': _L2_ffn_in['g1b'], 'L2_ffn_G2': _L2_ffn_in['G2'], 'L2_ffn_g2b': _L2_ffn_in['g2b'], 'L3_attn_w_attn': _L3_attn_in['w_attn'], 'L3_attn_w_proj': _L3_attn_in['w_proj'], 'L3_attn_b_proj': _L3_attn_in['b_proj'], 'L3_ffn_gate_weight': _L3_ffn_in['gate_weight'], 'L3_ffn_Wg': _L3_ffn_in['Wg'], 'L3_ffn_Wu': _L3_ffn_in['Wu'], 'L3_ffn_Wd': _L3_ffn_in['Wd'], 'L3_ffn_Ws_g': _L3_ffn_in['Ws_g'], 'L3_ffn_Ws_u': _L3_ffn_in['Ws_u'], 'L3_ffn_Ws_d': _L3_ffn_in['Ws_d']}

def reference(x, txt, L0_tok_conv_w, L0_tok_conv_b, L0_tok_pos_table, L0_attn_W_qkv, L0_attn_b_qkv, L0_ffn_ln1_g, L0_ffn_ln1_b, L0_ffn_qkv_w, L0_ffn_qkv_b, L0_ffn_proj_w, L0_ffn_proj_b, L0_ffn_ln2_g, L0_ffn_ln2_b, L0_ffn_gate_w, L0_ffn_w1, L0_ffn_b1, L0_ffn_w2, L0_ffn_b2, L1_attn_qkv_w, L1_attn_qkv_b, L1_attn_ln_g, L1_attn_ln_b, L1_ffn_ln_gamma, L1_ffn_ln_beta, L1_ffn_router_w, L1_ffn_w1, L1_ffn_w2, L2_attn_W_q_lin, L2_attn_b_q_lin, L2_attn_W_k_lin, L2_attn_b_k_lin, L2_attn_W_v_lin, L2_attn_b_v_lin, L2_attn_W_q_loc, L2_attn_b_q_loc, L2_attn_W_k_loc, L2_attn_b_k_loc, L2_attn_W_v_loc, L2_attn_b_v_loc, L2_attn_W_out, L2_attn_b_out, L2_attn_W_g1, L2_attn_b_g1, L2_attn_W_g2, L2_attn_b_g2, L2_attn_gamma1, L2_attn_beta1, L2_ffn_P, L2_ffn_C, L2_ffn_W1, L2_ffn_b1, L2_ffn_W2, L2_ffn_b2, L2_ffn_G1, L2_ffn_g1b, L2_ffn_G2, L2_ffn_g2b, L3_attn_w_attn, L3_attn_w_proj, L3_attn_b_proj, L3_ffn_gate_weight, L3_ffn_Wg, L3_ffn_Wu, L3_ffn_Wd, L3_ffn_Ws_g, L3_ffn_Ws_u, L3_ffn_Ws_d):
    import jax
    import jax.numpy as jnp

    def _L0_tok_ref(pixel_values, conv_w, conv_b, pos_table):
        import jax, jax.numpy as jnp
        import numpy as np
        from jax import lax
        HIDDEN = 192
        C_IN = 3
        PATCH = 16
        SIDE = 32
        NUM_PATCHES = SIDE * SIDE

        def _position_ids(nb_h, nb_w):
            boundaries = np.arange(1.0 / SIDE, 1.0, 1.0 / SIDE, dtype=np.float32)
            frac_h = np.arange(0.0, 1.0 - 1e-06, 1.0 / nb_h, dtype=np.float32)
            frac_w = np.arange(0.0, 1.0 - 1e-06, 1.0 / nb_w, dtype=np.float32)
            bh = np.searchsorted(boundaries, frac_h, side='right')
            bw = np.searchsorted(boundaries, frac_w, side='right')
            return jnp.asarray((bh[:, None] * SIDE + bw).reshape(-1), dtype=jnp.int32)
        B, _, H, W = pixel_values.shape
        nb_h, nb_w = (H // PATCH, W // PATCH)
        patches = lax.conv_general_dilated(pixel_values, conv_w, window_strides=(PATCH, PATCH), padding='VALID', dimension_numbers=('NCHW', 'OIHW', 'NCHW'))
        patches = patches + conv_b[None, :, None, None]
        embeddings = patches.reshape(B, HIDDEN, nb_h * nb_w).transpose(0, 2, 1)
        pos_ids = _position_ids(nb_h, nb_w)
        pos_emb = pos_table[pos_ids]
        return embeddings + pos_emb[None, :, :]

    def _L0_attn_ref(x, W_qkv, b_qkv):
        import jax, jax.numpy as jnp
        import numpy as np
        EMBED_DIM = 192
        SEQ_LEN = 256
        BATCH = 16
        ALPHA = 0.99
        bs, sl, d = x.shape
        qkv = x @ W_qkv.T + b_qkv
        q, k, v = jnp.split(qkv, 3, axis=-1)
        idx = jnp.arange(sl)
        diff = idx[:, None] - idx[None, :]
        M = jnp.where(diff >= 0, jnp.float32(ALPHA) ** diff.astype(jnp.float32), 0.0)
        dim_sqrt = jnp.asarray(d, jnp.float32) ** 0.5
        scores = jnp.einsum('bsd,btd->bst', q, k) / dim_sqrt * M
        out = jnp.einsum('bst,btd->bsd', scores, v)
        return out

    def _L0_ffn_ref(x, ln1_g, ln1_b, qkv_w, qkv_b, proj_w, proj_b, ln2_g, ln2_b, gate_w, w1, b1, w2, b2):
        import jax, jax.numpy as jnp
        import numpy as np
        DIM = 192
        HEADS = 12
        EXPERTS = 8
        HID = 768
        TOP_K = 2
        LN_EPS = 1e-05

        def _layer_norm(x, g, b):
            mu = x.mean(-1, keepdims=True)
            var = ((x - mu) ** 2).mean(-1, keepdims=True)
            return (x - mu) * jax.lax.rsqrt(var + LN_EPS) * g + b

        def _attention(x, qkv_w, qkv_b, proj_w, proj_b):
            B, N, C = x.shape
            hd = C // HEADS
            qkv = (x @ qkv_w + qkv_b).reshape(B, N, 3, HEADS, hd).transpose(2, 0, 3, 1, 4)
            q, k, v = (qkv[0], qkv[1], qkv[2])
            attn = jax.nn.softmax(jnp.einsum('bhnd,bhmd->bhnm', q, k) * hd ** (-0.5), axis=-1)
            o = jnp.einsum('bhnm,bhmd->bhnd', attn, v).transpose(0, 2, 1, 3).reshape(B, N, C)
            return o @ proj_w + proj_b

        def _moe_mlp(xn, gate_w, w1, b1, w2, b2):
            T = xn.shape[0]
            logits = xn @ gate_w
            top_logits, top_idx = jax.lax.top_k(logits, TOP_K)
            top_gates = jax.nn.softmax(top_logits, axis=-1)
            gates = jnp.zeros((T, EXPERTS), xn.dtype).at[jnp.arange(T)[:, None], top_idx].set(top_gates)
            h = jax.nn.gelu(jnp.einsum('td,edh->teh', xn, w1) + b1, approximate=False)
            y = jnp.einsum('teh,ehd->ted', h, w2) + b2
            return jnp.einsum('ted,te->td', y, gates)
        B, N, C = x.shape
        x = x + _attention(_layer_norm(x, ln1_g, ln1_b), qkv_w, qkv_b, proj_w, proj_b)
        xn = _layer_norm(x, ln2_g, ln2_b).reshape(B * N, C)
        moe_out = _moe_mlp(xn, gate_w, w1, b1, w2, b2).reshape(B, N, C)
        return x + moe_out

    def _L1_attn_ref(x, qkv_w, qkv_b, ln_g, ln_b):
        import jax, jax.numpy as jnp
        import numpy as np
        from jax import lax
        NUM_HEADS = 12
        BETA = 0.2
        KS = 3
        LN_EPS = 1e-05
        B, N, C = x.shape
        H = NUM_HEADS
        D = C // H
        mu = jnp.mean(x, axis=-1, keepdims=True)
        var = jnp.mean(jnp.square(x - mu), axis=-1, keepdims=True)
        xn = (x - mu) * lax.rsqrt(var + LN_EPS) * ln_g + ln_b
        qkv = xn @ qkv_w.T + qkv_b
        qkv = qkv.reshape(B, N, 3, H, D).transpose(2, 0, 3, 1, 4)
        q, k, v = (qkv[0], qkv[1], qkv[2])
        attn = jnp.einsum('bhnd,bhmd->bhnm', q, k) * D ** (-0.5)
        kernel = jnp.ones((KS, KS), dtype=attn.dtype).at[KS // 2, KS // 2].set(0.0)
        kernel = kernel.reshape(1, 1, KS, KS)
        neigh = lax.conv_general_dilated(attn.reshape(B * H, 1, N, N), kernel, window_strides=(1, 1), padding='SAME', dimension_numbers=('NCHW', 'OIHW', 'NCHW'))
        attn = attn - BETA * neigh.reshape(B, H, N, N)
        attn = jax.nn.softmax(attn - jnp.max(attn, axis=-1, keepdims=True), axis=-1)
        out = jnp.einsum('bhnm,bhmd->bhnd', attn, v)
        return out.transpose(0, 2, 1, 3).reshape(B, N, C)

    def _L1_ffn_ref(hidden_states, ln_gamma, ln_beta, router_w, w1, w2):
        import jax, jax.numpy as jnp
        import numpy as np
        D_MODEL, D_FF, N_EXPERTS, TOP_K = (192, 768, 8, 2)
        B, S = (2, 256)
        LN_EPS = 1e-05

        def _layernorm(x, gamma, beta):
            mu = jnp.mean(x, axis=-1, keepdims=True)
            var = jnp.mean(jnp.square(x - mu), axis=-1, keepdims=True)
            return (x - mu) * jax.lax.rsqrt(var + LN_EPS) * gamma + beta
        Bz, Sz, D = hidden_states.shape
        residual = hidden_states
        x = _layernorm(hidden_states, ln_gamma, ln_beta)
        tokens = x.reshape(-1, D)
        T = tokens.shape[0]
        logits = tokens @ router_w
        probs = jax.nn.softmax(logits, axis=-1)
        topw, topi = jax.lax.top_k(probs, TOP_K)
        topw = topw / jnp.sum(topw, axis=-1, keepdims=True)
        gates = jnp.zeros((T, N_EXPERTS), dtype=tokens.dtype)
        gates = gates.at[jnp.arange(T)[:, None], topi].set(topw)
        h = jnp.einsum('td,edf->etf', tokens, w1)
        h = jax.nn.silu(h)
        y = jnp.einsum('etf,efd->etd', h, w2)
        out = jnp.einsum('te,etd->td', gates, y)
        return residual + out.reshape(Bz, Sz, D)

    def _L2_attn_ref(x, W_q_lin, b_q_lin, W_k_lin, b_k_lin, W_v_lin, b_v_lin, W_q_loc, b_q_loc, W_k_loc, b_k_loc, W_v_loc, b_v_loc, W_out, b_out, W_g1, b_g1, W_g2, b_g2, gamma1, beta1):
        import jax, jax.numpy as jnp
        import numpy as np
        D, H, WIN, B, S = (192, 12, 64, 2, 256)
        Dh = D // H
        HALF = WIN // 2

        def _layernorm(x, g, b):
            m = jnp.mean(x, axis=-1, keepdims=True)
            v = jnp.mean((x - m) ** 2, axis=-1, keepdims=True)
            return (x - m) / jnp.sqrt(v + 1e-05) * g + b
        Bc, Sc, Dc = x.shape
        residual = x
        xn = _layernorm(x, gamma1, beta1)
        qf = jax.nn.elu(xn @ W_q_lin + b_q_lin) + 1.0
        kf = jax.nn.elu(xn @ W_k_lin + b_k_lin) + 1.0
        vl = xn @ W_v_lin + b_v_lin
        kv = jnp.einsum('bsd,bse->bde', kf, vl)
        lin_out = jnp.einsum('bsd,bde->bse', qf, kv)
        normalizer = jnp.einsum('bsd,bd->bs', qf, kf.sum(axis=1))
        lin_out = lin_out / (normalizer[..., None] + 1e-06)
        qo = (xn @ W_q_loc + b_q_loc).reshape(Bc, Sc, H, Dh)
        ko = (xn @ W_k_loc + b_k_loc).reshape(Bc, Sc, H, Dh)
        vo = (xn @ W_v_loc + b_v_loc).reshape(Bc, Sc, H, Dh)
        offsets = jnp.arange(-HALF, HALF + 1)
        idx = jnp.arange(Sc)[:, None] + offsets
        valid = (idx >= 0) & (idx < Sc)
        idxc = jnp.clip(idx, 0, Sc - 1)
        kwin = ko[:, idxc]
        vwin = vo[:, idxc]
        scores = jnp.einsum('bshd,bswhd->bshw', qo, kwin) / np.sqrt(Dh).astype(np.float32)
        scores = jnp.where(valid[None, :, None, :], scores, -jnp.inf)
        attn = jax.nn.softmax(scores, axis=-1)
        win_out = jnp.einsum('bshw,bswhd->bshd', attn, vwin).reshape(Bc, Sc, Dc)
        gate_in = jnp.concatenate([lin_out, win_out, xn], axis=-1)
        gate = jax.nn.sigmoid(jax.nn.relu(gate_in @ W_g1 + b_g1) @ W_g2 + b_g2)
        fused = gate * lin_out + (1.0 - gate) * win_out
        return fused @ W_out + b_out + residual

    def _L2_ffn_ref(x, P, C, W1, b1, W2, b2, G1, g1b, G2, g2b):
        import jax, jax.numpy as jnp
        import numpy as np
        B, T, D = (2, 512, 192)
        S, R, M, K = (8, 16, 64, 4)
        H, G = (32, 64)

        def _ssinf3(x, P, C, W1, b1, W2, b2, G1, g1b, G2, g2b):
            shp = x.shape
            xf = x.reshape(-1, shp[-1])
            z = jnp.einsum('nd,sdr->nsr', xf, P)
            scores = jnp.einsum('nsr,smr->nsm', z, C)
            topv, topi = jax.lax.top_k(scores, K)
            w = jax.nn.softmax(topv, axis=-1)
            sidx = jnp.arange(S)[None, :, None]
            W1g = W1[sidx, topi]
            b1g = b1[sidx, topi]
            W2g = W2[sidx, topi]
            b2g = b2[sidx, topi]
            h = jax.nn.gelu(jnp.einsum('nsr,nskrh->nskh', z, W1g) + b1g)
            yl = jnp.einsum('nskh,nskhr->nskr', h, W2g) + b2g
            comb = jnp.einsum('nskr,nsk->nsr', yl, w)
            comb = comb.reshape(xf.shape[0], S * R)
            out = jax.nn.gelu(comb @ G1 + g1b) @ G2 + g2b
            return out.reshape(shp)
        return _ssinf3(x, P, C, W1, b1, W2, b2, G1, g1b, G2, g2b)

    def _L3_attn_ref(x, w_attn, w_proj, b_proj):
        import jax, jax.numpy as jnp
        import numpy as np
        N_HEAD = 12
        B, L, D = x.shape
        hd = D // N_HEAD
        qkv = x @ w_attn
        q, k, v = jnp.split(qkv, 3, axis=-1)
        q = q.reshape(B, L, N_HEAD, hd).transpose(0, 2, 1, 3)
        k = k.reshape(B, L, N_HEAD, hd).transpose(0, 2, 1, 3)
        v = v.reshape(B, L, N_HEAD, hd).transpose(0, 2, 1, 3)
        scores = jnp.einsum('bhqd,bhkd->bhqk', q, k) * (1.0 / jnp.sqrt(jnp.float32(hd)))
        causal = jnp.tril(jnp.ones((L, L), dtype=bool))
        scores = jnp.where(causal[None, None, :, :], scores, -jnp.inf)
        attn = jax.nn.softmax(scores, axis=-1)
        out = jnp.einsum('bhqk,bhkd->bhqd', attn, v)
        out = out.transpose(0, 2, 1, 3).reshape(B, L, D)
        return out @ w_proj + b_proj

    def _L3_ffn_ref(hidden_states, gate_weight, Wg, Wu, Wd, Ws_g, Ws_u, Ws_d):
        import math
        import jax, jax.numpy as jnp
        import numpy as np
        B, L, D = (8, 1024, 192)
        E = 16
        TOP_K = 2
        F_EXP = 4 * D
        F_SH = F_EXP * 2 // 4
        b, l, d = hidden_states.shape
        n = b * l
        x = hidden_states.reshape(n, d)
        scores = jax.nn.sigmoid(x @ gate_weight.T)
        capacity = math.ceil(n / E * TOP_K)
        topk_score, topk_ids = jax.lax.top_k(scores.T, capacity)
        xg = x[topk_ids]
        gate = jax.nn.silu(jnp.einsum('ecd,efd->ecf', xg, Wg))
        up = jnp.einsum('ecd,efd->ecf', xg, Wu)
        out = jnp.einsum('ecf,edf->ecd', gate * up, Wd)
        out = out * topk_score[..., None]
        y = jnp.zeros((n, d), x.dtype).at[topk_ids.reshape(-1)].add(out.reshape(-1, d))
        y = y.reshape(b, l, d)
        shared = jax.nn.silu(hidden_states @ Ws_g.T) * (hidden_states @ Ws_u.T) @ Ws_d.T
        return y + shared
    h = _L0_tok_ref(x, L0_tok_conv_w, L0_tok_conv_b, L0_tok_pos_table)
    h = jnp.concatenate([h, txt], axis=1)
    h = h + _L0_attn_ref(_layernorm(h, axis=-1), L0_attn_W_qkv, L0_attn_b_qkv)
    h = h + _L0_ffn_ref(_layernorm(h, axis=-1), L0_ffn_ln1_g, L0_ffn_ln1_b, L0_ffn_qkv_w, L0_ffn_qkv_b, L0_ffn_proj_w, L0_ffn_proj_b, L0_ffn_ln2_g, L0_ffn_ln2_b, L0_ffn_gate_w, L0_ffn_w1, L0_ffn_b1, L0_ffn_w2, L0_ffn_b2)
    h = h + _L1_attn_ref(_layernorm(h, axis=-1), L1_attn_qkv_w, L1_attn_qkv_b, L1_attn_ln_g, L1_attn_ln_b)
    h = h + _L1_ffn_ref(_layernorm(h, axis=-1), L1_ffn_ln_gamma, L1_ffn_ln_beta, L1_ffn_router_w, L1_ffn_w1, L1_ffn_w2)
    h = h + _L2_attn_ref(_layernorm(h, axis=-1), L2_attn_W_q_lin, L2_attn_b_q_lin, L2_attn_W_k_lin, L2_attn_b_k_lin, L2_attn_W_v_lin, L2_attn_b_v_lin, L2_attn_W_q_loc, L2_attn_b_q_loc, L2_attn_W_k_loc, L2_attn_b_k_loc, L2_attn_W_v_loc, L2_attn_b_v_loc, L2_attn_W_out, L2_attn_b_out, L2_attn_W_g1, L2_attn_b_g1, L2_attn_W_g2, L2_attn_b_g2, L2_attn_gamma1, L2_attn_beta1)
    h = h + _L2_ffn_ref(_layernorm(h, axis=-1), L2_ffn_P, L2_ffn_C, L2_ffn_W1, L2_ffn_b1, L2_ffn_W2, L2_ffn_b2, L2_ffn_G1, L2_ffn_g1b, L2_ffn_G2, L2_ffn_g2b)
    h = h + _L3_attn_ref(_layernorm(h, axis=-1), L3_attn_w_attn, L3_attn_w_proj, L3_attn_b_proj)
    h = h + _L3_ffn_ref(_layernorm(h, axis=-1), L3_ffn_gate_weight, L3_ffn_Wg, L3_ffn_Wu, L3_ffn_Wd, L3_ffn_Ws_g, L3_ffn_Ws_u, L3_ffn_Ws_d)
    return h

_drawn_inputs = setup_inputs


def setup_inputs(seed=0):
    import zlib

    import numpy as np

    out = dict(_drawn_inputs(seed))
    spreads = {'L0_tok_conv_b': (0.0, 0.1),
     'L0_ffn_ln1_g': (1.0, 0.6),
     'L0_ffn_ln1_b': (0.0, 0.8),
     'L0_ffn_qkv_b': (0.0, 0.467),
     'L0_ffn_proj_b': (0.0, 0.1),
     'L0_ffn_ln2_g': (1.0, 0.6),
     'L0_ffn_ln2_b': (0.0, 0.629),
     'L0_ffn_b1': (0.0, 0.72),
     'L0_ffn_b2': (0.0, 0.1),
     'L1_attn_qkv_b': (0.0, 0.1),
     'L1_attn_ln_g': (1.0, 0.6),
     'L1_attn_ln_b': (0.0, 0.621),
     'L1_ffn_ln_gamma': (1.0, 0.6),
     'L1_ffn_ln_beta': (0.0, 0.8),
     'L2_attn_b_q_lin': (0.0, 2.0),
     'L2_attn_b_k_lin': (0.0, 2.0),
     'L2_attn_b_v_lin': (0.0, 0.8),
     'L2_attn_b_q_loc': (0.0, 0.8),
     'L2_attn_b_k_loc': (0.0, 2.0),
     'L2_attn_b_v_loc': (0.0, 0.8),
     'L2_attn_b_out': (0.0, 0.333),
     'L2_attn_b_g1': (0.0, 0.8),
     'L2_attn_b_g2': (0.0, 0.8),
     'L2_attn_gamma1': (1.0, 0.6),
     'L2_attn_beta1': (0.0, 0.8),
     'L2_ffn_b1': (0.0, 2.0),
     'L2_ffn_b2': (0.0, 0.8),
     'L2_ffn_g1b': (0.0, 0.753),
     'L2_ffn_g2b': (0.0, 0.356),
     'L3_attn_b_proj': (0.0, 0.324)}
    factors = {'L0_ffn_qkv_w': 7.54,
     'L0_ffn_proj_w': 3.284,
     'L1_attn_qkv_w': 2.867,
     'L1_ffn_router_w': 3.383,
     'L1_ffn_w1': 3.02,
     'L1_ffn_w2': 3.007,
     'L2_attn_W_q_lin': 31.649,
     'L2_attn_W_k_lin': 28.91,
     'L2_attn_W_v_lin': 8.0,
     'L2_attn_W_q_loc': 8.0,
     'L2_attn_W_k_loc': 8.0,
     'L2_attn_W_v_loc': 8.0,
     'L2_attn_W_out': 8.0,
     'L2_attn_W_g1': 8.0,
     'L2_attn_W_g2': 8.0,
     'L3_attn_w_attn': 8.0,
     'L3_attn_w_proj': 8.0,
     'L3_ffn_gate_weight': 6.673,
     'L3_ffn_Wg': 6.387,
     'L3_ffn_Wu': 6.374,
     'L3_ffn_Wd': 6.341,
     'L3_ffn_Ws_g': 5.774,
     'L3_ffn_Ws_u': 5.54,
     'L3_ffn_Ws_d': 5.701}
    for name, (base, spread) in spreads.items():
        noise = np.random.default_rng([zlib.crc32(name.encode()), seed]).standard_normal(out[name].shape)
        drawn = base * np.exp(spread * noise) if base else spread * noise
        out[name] = jnp.asarray(drawn.astype(out[name].dtype))
    for name, factor in factors.items():
        out[name] = (out[name] * factor).astype(out[name].dtype)
    return out
```

```python
from contextlib import ExitStack

import concourse.bass as bass
from concourse import mybir

STAGES = 99

B = 16
L = 102
NP = 25
D = 192
C = 2
K = D // C
H = 12
HD = D // H
RG = 4
HT = H // RG
HP = 32
T = B * L
CONV_K = 6
GB = 4
G = B // GB
NG = GB * L
EPS = 1e-5
E01 = 8
F = 768
FM = F // 128
NS = 8
NR = 16
NM = 64
KEEP = 4
NV = 16
VT = 8
E3 = 16
CAP = T * 2 // E3
ROUNDS = -(-CAP // 8)
FS = F * 2 // 4
SM = FS // 128
NEG = -1e30

F32 = mybir.dt.float32
BF16 = mybir.dt.bfloat16
U32 = mybir.dt.uint32
ALU = mybir.AluOpType
ACT = mybir.ActivationFunctionType
AX = mybir.AxisListType
ds = bass.ds

PACKS = {
    "tok": [("conv_w", 128, CONV_K * D), ("patches", 128, CONV_K * B * NP), ("pos", GB * NP, D), ("conv_b", GB * NP, D)],
    "const": [("ident", 128, 128), ("neg_half", L, 2), ("iota", L, 64)],
    "l0a": [("wq", K, C * D), ("wk", K, C * D), ("wv", K, C * D), ("bq", K, C), ("bk", K, C), ("bv", L, D),
            ("decay", L, L)],
    "l2a": [("wq", K, C * HT * 128), ("wk", K, C * HT * 128), ("wv", K, C * D), ("bq", 128, HT), ("bk", 128, HT),
            ("bv", L, D), ("g", K, C), ("b", K, C), ("band", L, L), ("lin_wq", K, C * D), ("lin_wk", K, C * D),
            ("lin_wv", K, C * D), ("lin_bq", K, C), ("lin_bk", K, C), ("lin_bv", L, D), ("wg1", K, 3 * C * D),
            ("bg1", K, C), ("wg2", K, C * D), ("bg2", L, D), ("wo", K, C * D), ("bo", L, D)],
    "l2f": [("p", K, C * 128), ("centres", 128, NS * NM), ("b2", 128, 4 * 128), ("g1", 128, 64), ("g1b", 64, 1),
            ("g2", 64, D), ("g2b", L, D)],
    "l3f": [("choose", K, C * E3), ("ws_g", K, C * FS), ("ws_u", K, C * FS), ("ws_d", 128, SM * D)],
    "l3a": [("wq", K, C * HT * 128), ("wk", K, C * HT * 128), ("wv", K, C * D), ("causal", L, L),
            ("wo", K, C * D), ("bo", L, D)],
    "l0r": [("g", K, C), ("b", K, C), ("gate", K, C * E01), ("b2", E01, D)],
    "l1r": [("g", K, C), ("b", K, C), ("gate", K, C * E01)],
    "l1a": [("wq", K, C * HT * 128), ("wk", K, C * HT * 128), ("wv", K, C * D), ("bq", 128, HT), ("bk", 128, HT),
            ("bv", L, D), ("g", K, C), ("b", K, C), ("mix", 128, 4)],
    "l0f": [("wq", K, C * HT * 128), ("wk", K, C * HT * 128), ("wv", K, C * D), ("bq", 128, HT), ("bk", 128, HT),
            ("bv", L, D), ("g", K, C), ("b", K, C), ("wo", K, C * D), ("bo", L, D)],
}


def offsets(pack):
    at, where = 0, {}
    for name, rows, cols in PACKS[pack]:
        where[name] = (rows, at, cols)
        at += cols
    return where, at


class Fields:

    def __init__(self, tile, pack):
        self.tile, self.where = tile, offsets(pack)[0]

    def at(self, name, groups=1):
        rows, start, cols = self.where[name]
        view = self.tile[0:rows, start:start + cols]
        return view if groups == 1 else view.rearrange("p (a n) -> p a n", a=groups)


class Steps:

    def __init__(self, eng, sem, before=0):
        self.eng, self.sem, self.before, self.n = eng, sem, before, 0

    def done(self, ins):
        ins.then_inc(self.sem, 1)
        self.n += 1

    def wait(self):
        self.eng.wait_ge(self.sem, self.before + self.n)


SEM_BANK = 72


class Memory:

    def __init__(self, nc, g, stack, phase):
        self.nc, self.stack, self.phase = nc, stack, phase
        self.bank = g["sem_banks"][g["phases"] % 2]
        g["phases"] += 1
        self.used = []
        stack.callback(self.retire)

    def retire(self):
        for sem in self.used:
            self.nc.release_semaphore(sem)
        self.nc.sync.sem_clear(range(self.bank[0], self.bank[0] + len(self.used)))

    def sb(self, name, shape, dt=F32):
        return self.stack.enter_context(self.nc.sbuf_tensor(f"{self.phase}_{name}", shape, dt))

    def sem(self, name):
        handle = self.nc.alloc_semaphore(f"{self.phase}_{name}", self.bank[len(self.used)])
        self.used.append(handle)
        return handle


def embed(nc, g, dram):
    with ExitStack() as stack:
        m = Memory(nc, g, stack, "tok")
        width = offsets("tok")[1]
        pack = m.sb("pack", [128, width])
        f = Fields(pack, "tok")
        emb = m.sb("emb", [GB * NP, G, D])
        bias = m.sb("bias", [GB * NP, D])
        loaded, txt_loaded, moved = m.sem("loaded"), m.sem("txt_loaded"), m.sem("moved")
        bias_ready, emb_ps, emb_ready = m.sem("bias_ready"), m.sem("emb_ps"), m.sem("emb_ready")
        w = f.at("conv_w", CONV_K)
        x = f.at("patches", CONV_K)
        ps = g["ps"]

        block = stack.enter_context(nc.Block())

        @block.sync
        def _(sp):
            sp.dma_start(pack[:, :], dram["pack_tok"]).then_inc(loaded, 16)
            sp.dma_start(g["h"][NP:L, :, :], dram["txt"].rearrange("b t d -> t b d")).then_inc(txt_loaded, 16)
            for name in PACKS:
                if name != "tok":
                    sp.dma_start(g["pack_" + name][:, :], dram["pack_" + name]).then_inc(g["packs_loaded"], 16)
            for q in range(G):
                sp.wait_ge(emb_ready, q + 1)
                for j in range(GB):
                    sp.dma_start(g["h"][0:NP, q * GB + j, :], emb[j * NP:(j + 1) * NP, q, :]).then_inc(moved, 16)
            sp.wait_ge(moved, 16 * B)
            sp.wait_ge(txt_loaded, 16)
            sp.wait_ge(g["packs_loaded"], 16 * (len(PACKS) - 1))

        @block.tensor
        def _(pe):
            pe.wait_ge(loaded, 16)
            for q in range(G):
                for k in range(CONV_K):
                    last = pe.matmul(ps[0:GB * NP, 0, q, 0:D], x[:, k, q * GB * NP:(q + 1) * GB * NP], w[:, k, :],
                                     start=(k == 0), stop=(k == CONV_K - 1))
                last.then_inc(emb_ps, 1)

        @block.vector
        def _(dve):
            dve.wait_ge(loaded, 16)
            dve.tensor_tensor(bias[:, :], f.at("pos"), f.at("conv_b"), ALU.add).then_inc(bias_ready, 1)
            dve.wait_ge(bias_ready, 1)
            for q in range(G):
                dve.wait_ge(emb_ps, q + 1)
                dve.tensor_tensor(emb[:, q, :], ps[0:GB * NP, 0, q, 0:D], bias[:, :], ALU.add).then_inc(emb_ready, 1)


class Norm:

    def __init__(self, m, g, name, per_iter=1):
        self.stats = m.sb(name + "_stats", [L, 2, 6])
        self.moments = m.sb(name + "_moments", [L, 2, 2])
        self.shifted = m.sb(name + "_shifted", [L, 2])
        self.rstd = m.sb(name + "_rstd", [L, 2])
        self.pause = m.sb(name + "_pause", [1, 1])
        self.neg_half = g["const"].at("neg_half")
        self.var_ready, self.rstd_ready = m.sem(name + "_var_ready"), m.sem(name + "_rstd_ready")

    def vector(self, dve, i, steps, src, dst):
        for j in range(2):
            steps.done(dve.bn_stats(self.stats[:, j, :], src[j]))
        steps.wait()
        dve.memset(self.pause[:, :], 0.0)
        for j in range(2):
            steps.done(dve.bn_aggr(self.moments[:, j, :], self.stats[:, j, :]))
        steps.wait()
        dve.tensor_scalar(self.shifted[:, :], self.moments[:, :, 1], EPS, None, ALU.add).then_inc(self.var_ready, 1)
        dve.wait_ge(self.rstd_ready, i + 1)
        return [dve.tensor_scalar(dst[j], src[j], self.moments[:, j, 0:1], self.rstd[:, j:j + 1],
                                  ALU.subtract, ALU.mult) for j in range(2)]

    def pool(self, pool, i):
        pool.wait_ge(self.var_ready, i + 1)
        pool.tensor_tensor(self.rstd[:, :], self.shifted[:, :], self.neg_half, ALU.pow).then_inc(self.rstd_ready, 1)


def retention(nc, g):
    w = g["l0a"]
    wq, wk, wv = w.at("wq", C), w.at("wk", C), w.at("wv", C)
    ident = g["const"].at("ident")
    ps, h = g["ps"], g["h"]
    with ExitStack() as stack:
        m = Memory(nc, g, stack, "ret")
        norm = Norm(m, g, "norm")
        z = m.sb("z", [L, 2, D])
        xT = m.sb("xT", [K, 2, C, L])
        qT = m.sb("qT", [K, 2, C, L])
        kT = m.sb("kT", [K, 2, C, L])
        v = m.sb("v", [L, 2, D])
        sT = m.sb("sT", [L, 2, L])
        dve_steps = m.sem("dve_steps")
        z_ready, xT_ps, xT_ready = m.sem("z_ready"), m.sem("xT_ps"), m.sem("xT_ready")
        qkv_ps, qk_ready, v_ready = m.sem("qkv_ps"), m.sem("qk_ready"), m.sem("v_ready")
        s_ps, s_ready, o_ps = m.sem("s_ps"), m.sem("s_ready"), m.sem("o_ps")
        block = stack.enter_context(nc.Block())

        @block.tensor
        def _(pe):
            with pe.Fori(0, B // 2) as i:
                for j in range(2):
                    pe.wait_ge(z_ready, 2 * i + j + 1)
                    for c in range(C):
                        last = pe.transpose(ps[0:K, j, 3, c * L:(c + 1) * L], z[:, j, c * K:(c + 1) * K],
                                            ident[0:L, 0:L])
                    last.then_inc(xT_ps, 1)
                for j in range(2):
                    pe.wait_ge(xT_ready, 2 * i + j + 1)
                    for bank, wt in ((0, wq), (1, wk)):
                        for co in range(C):
                            for c in range(C):
                                pe.matmul(ps[0:K, j, bank, co * L:(co + 1) * L], wt[:, c, co * K:(co + 1) * K],
                                          xT[:, j, c, :], start=(c == 0), stop=(c == C - 1))
                    for c in range(C):
                        last = pe.matmul(ps[0:L, j, 2, 0:D], xT[:, j, c, :], wv[:, c, :],
                                         start=(c == 0), stop=(c == C - 1))
                    last.then_inc(qkv_ps, 1)
                for j in range(2):
                    pe.wait_ge(qk_ready, 2 * i + j + 1)
                    for c in range(C):
                        last = pe.matmul(ps[0:L, j, 3, 0:L], kT[:, j, c, :], qT[:, j, c, :],
                                         start=(c == 0), stop=(c == C - 1))
                    last.then_inc(s_ps, 1)
                for j in range(2):
                    pe.wait_ge(s_ready, 2 * i + j + 1)
                    pe.wait_ge(v_ready, 2 * i + j + 1)
                    pe.matmul(ps[0:L, j, 0, 0:D], sT[:, j, :], v[:, j, :], start=True, stop=True).then_inc(o_ps, 1)

        @block.scalar
        def _(act):
            with act.Fori(0, B // 2) as i:
                for j in range(2):
                    act.wait_ge(xT_ps, 2 * i + j + 1)
                    act.activation(xT[:, j, :, :], ps[0:K, j, 3, 0:C * L].rearrange("p (c n) -> p c n", c=C),
                                   ACT.Copy).then_inc(xT_ready, 1)
                for j in range(2):
                    act.wait_ge(qkv_ps, 2 * i + j + 1)
                    for bank, dst, bias in ((0, qT, w.at("bq")), (1, kT, w.at("bk"))):
                        for c in range(C):
                            last = act.activation(dst[:, j, c, :], ps[0:K, j, bank, c * L:(c + 1) * L],
                                                  ACT.Identity, bias=bias[:, c:c + 1])
                    last.then_inc(qk_ready, 1)

        @block.gpsimd
        def _(pool):
            with pool.Fori(0, B // 2) as i:
                norm.pool(pool, i)

        @block.vector
        def _(dve):
            own = 4
            with dve.Fori(0, B // 2) as i:
                steps = Steps(dve, dve_steps, own * i)
                for ins in norm.vector(dve, i, steps, [h[:, ds(2 * i + j, 1), :] for j in range(2)],
                                       [z[:, j:j + 1, :] for j in range(2)]):
                    ins.then_inc(z_ready, 1)
                for j in range(2):
                    dve.wait_ge(qkv_ps, 2 * i + j + 1)
                    dve.tensor_tensor(v[:, j, :], ps[0:L, j, 2, 0:D], w.at("bv"), ALU.add).then_inc(v_ready, 1)
                for j in range(2):
                    dve.wait_ge(s_ps, 2 * i + j + 1)
                    dve.tensor_tensor(sT[:, j, :], ps[0:L, j, 3, 0:L], w.at("decay"), ALU.mult).then_inc(s_ready, 1)
                for j in range(2):
                    dve.wait_ge(o_ps, 2 * i + j + 1)
                    dve.tensor_tensor(h[:, ds(2 * i + j, 1), :], h[:, ds(2 * i + j, 1), :],
                                      ps[0:L, j, 0:1, 0:D], ALU.add)
                assert steps.n == own


def softmax_attention(nc, g, phase, residual, mask=None, conv=False, project=True):
    w = g[phase]
    wq, wk, wv = w.at("wq", C), w.at("wk", C), w.at("wv", C)
    ident = g["const"].at("ident")
    ps, h, x = g["ps"], g["h"], g["x"]
    two_norms = residual != "plain"
    gated = residual == "gated"
    VW = HD + 1
    with ExitStack() as stack:
        m = Memory(nc, g, stack, phase)
        norm = Norm(m, g, "norm")
        norm2 = Norm(m, g, "norm2") if two_norms else None
        z0 = m.sb("z0", [L, 2, D]) if two_norms else None
        z = m.sb("z", [L, 2, D])
        xT = m.sb("xT", [K, 2, C, L])
        qT = m.sb("qT", [128, 2, HT, L])
        kT = m.sb("kT", [128, 2, HT, L])
        if conv:
            side = m.sb("side", [128, 2, 2, HT, L])
            q2 = m.sb("q2", [128, 2, HT, L])
            k2 = m.sb("k2", [128, 2, HT, L])
        v = m.sb("v", [L, 2, H, VW])
        top = m.sb("top", [L, 2, H])
        p = m.sb("p", [L, 2, H, L])
        pT = m.sb("pT", [L, 2, H, L])
        rsum = m.sb("rsum", [L, 2, H])
        o = m.sb("o", [L, 2, D])
        if mask:
            mask_bf = m.sb("mask_bf", [L, HT, L], BF16)
            ident_bf = m.sb("ident_bf", [L, L], BF16)
        if project:
            oT = m.sb("oT", [K, 2, C, L])
            y = m.sb("y", [L, 2, D])
        if gated:
            lin_x = m.sb("lin_x", [K, 2, 2 * C, L])
            lin_e = m.sb("lin_e", [K, 2, 2 * C, L])
            lin_f = m.sb("lin_f", [K, 2, 2 * C, L])
            lin_v = m.sb("lin_v", [L, 2, D + 1])
            lin_s = m.sb("lin_s", [L, 2, L])
            lin_d = m.sb("lin_d", [L, 2])
            lin_o = m.sb("lin_o", [L, 2, D])
            mixT = m.sb("mixT", [K, 2, 2 * C, L])
            hidT = m.sb("hidT", [K, 2, C, L])
            gate = m.sb("gate", [L, 2, D])
            diff = m.sb("diff", [L, 2, D])
            fused = m.sb("fused", [L, 2, D])
            lin_ps, lin_x_ready, lin_m_ready = m.sem("lin_ps"), m.sem("lin_x_ready"), m.sem("lin_m_ready")
            lin_e_ready, lin_f_ready, lin_v_ready = m.sem("lin_e_ready"), m.sem("lin_f_ready"), m.sem("lin_v_ready")
            lin_s_ps, lin_s_ready, lin_o_ps = m.sem("lin_s_ps"), m.sem("lin_s_ready"), m.sem("lin_o_ps")
            lin_o_ready, mixT_ps, mixT_ready = m.sem("lin_o_ready"), m.sem("mixT_ps"), m.sem("mixT_ready")
            hid_ps, hid_ready, gate_ps = m.sem("hid_ps"), m.sem("hid_ready"), m.sem("gate_ps")
            gate_in, gate_exp, fused_ready = m.sem("gate_in"), m.sem("gate_exp"), m.sem("fused_ready")
        dve_steps, const_ready = m.sem("dve_steps"), m.sem("const_ready")
        z_ready, xT_ps, xT_ready = m.sem("z_ready"), m.sem("xT_ps"), m.sem("xT_ready")
        qkv_ps, qk_ready, v_ready = m.sem("qkv_ps"), m.sem("qk_ready"), m.sem("v_ready")
        mixed_ready, left_added = m.sem("mixed_ready"), m.sem("left_added")
        s_ps, below_ready, p_ready = m.sem("s_ps"), m.sem("below_ready"), m.sem("p_ready")
        pT_ps, pT_ready, o_ps, o_ready = m.sem("pT_ps"), m.sem("pT_ready"), m.sem("o_ps"), m.sem("o_ready")
        oT_ps, oT_ready, y_ps = m.sem("oT_ps"), m.sem("oT_ready"), m.sem("y_ps")
        block = stack.enter_context(nc.Block())

        def banked(j):
            return ps[0:L, j, :, 0:HT * L].rearrange("p r (t n) -> p r t n", t=HT)

        @block.tensor
        def _(pe):
            if mask:
                pe.wait_ge(const_ready, 3)
            with pe.Fori(0, B // 2) as i:
                for j in range(2):
                    pe.wait_ge(z_ready, 2 * i + j + 1)
                    for c in range(C):
                        last = pe.transpose(ps[0:K, j, 3, c * L:(c + 1) * L], z[:, j, c * K:(c + 1) * K],
                                            ident[0:L, 0:L])
                    last.then_inc(xT_ps, 1)
                for j in range(2):
                    pe.wait_ge(xT_ready, 2 * i + j + 1)
                    for bank, wt in ((0, wq), (1, wk)):
                        for t in range(HT):
                            for c in range(C):
                                pe.matmul(ps[:, j, bank, t * L:(t + 1) * L], wt[:, c, t * 128:(t + 1) * 128],
                                          xT[:, j, c, :], start=(c == 0), stop=(c == C - 1))
                    for c in range(C):
                        last = pe.matmul(ps[0:L, j, 2, 0:D], xT[:, j, c, :], wv[:, c, :],
                                         start=(c == 0), stop=(c == C - 1))
                    last.then_inc(qkv_ps, 1)
                qs, ks, ready = (q2, k2, mixed_ready) if conv else (qT, kT, qk_ready)
                for j in range(2):
                    pe.wait_ge(ready, 2 * i + j + 1)
                    pe.wait_ge(v_ready, 2 * i + j + 1)
                    if mask:
                        for r in range(RG):
                            pe.matmul(ps[0:L, j, r, 0:HT * L], ident_bf[:, :],
                                      mask_bf[:, :, :].rearrange("p t n -> p (t n)"),
                                      start=True, stop=False, skip_group_check=True)
                    for t in range(HT):
                        for r in range(RG):
                            last = pe.matmul(ps[0:L, j, r, t * L:(t + 1) * L], qs[HP * r:HP * (r + 1), j, t, :],
                                             ks[HP * r:HP * (r + 1), j, t, :], start=not mask, stop=True,
                                             skip_group_check=bool(mask))
                    last.then_inc(s_ps, 1)
                for j in range(2):
                    pe.wait_ge(p_ready, 2 * i + j + 1)
                    for a in range(H):
                        last = pe.transpose(ps[0:L, j, a // HT, (a % HT) * L:(a % HT + 1) * L], p[:, j, a, :],
                                            ident[0:L, 0:L])
                    last.then_inc(pT_ps, 1)
                for j in range(2):
                    pe.wait_ge(pT_ready, 2 * i + j + 1)
                    for a in range(H):
                        last = pe.matmul(ps[0:L, j, 0, a * VW:(a + 1) * VW], pT[:, j, a, :], v[:, j, a, :],
                                         start=True, stop=True)
                    last.then_inc(o_ps, 1)
                    if gated:
                        for bank, wt in ((1, "lin_wq"), (2, "lin_wk")):
                            for co in range(C):
                                for c in range(C):
                                    pe.matmul(ps[0:K, j, bank, co * L:(co + 1) * L],
                                              w.at(wt, C)[:, c, co * K:(co + 1) * K], xT[:, j, c, :],
                                              start=(c == 0), stop=(c == C - 1))
                        for c in range(C):
                            last = pe.matmul(ps[0:L, j, 3, 0:D], xT[:, j, c, :], w.at("lin_wv", C)[:, c, :],
                                             start=(c == 0), stop=(c == C - 1))
                        last.then_inc(lin_ps, 1)
                if gated:
                    for j in range(2):
                        pe.wait_ge(lin_f_ready, 2 * i + j + 1)
                        for c in range(C):
                            last = pe.matmul(ps[0:L, j, 1, 0:L], lin_f[:, j, C + c, :], lin_f[:, j, c, :],
                                             start=(c == 0), stop=(c == C - 1))
                        last.then_inc(lin_s_ps, 1)
                    for j in range(2):
                        pe.wait_ge(lin_s_ready, 2 * i + j + 1)
                        pe.wait_ge(lin_v_ready, 2 * i + j + 1)
                        pe.matmul(ps[0:L, j, 2, 0:D + 1], lin_s[:, j, :], lin_v[:, j, :], start=True, stop=True)\
                          .then_inc(lin_o_ps, 1)
                    for j in range(2):
                        pe.wait_ge(lin_o_ready, 2 * i + j + 1)
                        pe.wait_ge(o_ready, 2 * i + j + 1)
                        for n, src in ((0, lin_o), (1, o)):
                            for c in range(C):
                                last = pe.transpose(ps[0:K, j, 3, (n * C + c) * L:(n * C + c + 1) * L],
                                                    src[:, j, c * K:(c + 1) * K], ident[0:L, 0:L])
                        last.then_inc(mixT_ps, 1)
                    for j in range(2):
                        pe.wait_ge(mixT_ready, 2 * i + j + 1)
                        gate_in_T = [mixT[:, j, n, :] for n in range(2 * C)] + [xT[:, j, c, :] for c in range(C)]
                        for co in range(C):
                            for n, part in enumerate(gate_in_T):
                                last = pe.matmul(ps[0:K, j, 0, co * L:(co + 1) * L],
                                                 w.at("wg1", 3 * C)[:, n, co * K:(co + 1) * K], part,
                                                 start=(n == 0), stop=(n == 3 * C - 1))
                        last.then_inc(hid_ps, 1)
                    for j in range(2):
                        pe.wait_ge(hid_ready, 2 * i + j + 1)
                        for c in range(C):
                            last = pe.matmul(ps[0:L, j, 1, 0:D], hidT[:, j, c, :], w.at("wg2", C)[:, c, :],
                                             start=(c == 0), stop=(c == C - 1))
                        last.then_inc(gate_ps, 1)
                if project:
                    out_src, out_ready = (fused, fused_ready) if gated else (o, o_ready)
                    for j in range(2):
                        pe.wait_ge(out_ready, 2 * i + j + 1)
                        for c in range(C):
                            last = pe.transpose(ps[0:K, j, 1, c * L:(c + 1) * L], out_src[:, j, c * K:(c + 1) * K],
                                                ident[0:L, 0:L])
                        last.then_inc(oT_ps, 1)
                    for j in range(2):
                        pe.wait_ge(oT_ready, 2 * i + j + 1)
                        for c in range(C):
                            last = pe.matmul(ps[0:L, j, 2, 0:D], oT[:, j, c, :], w.at("wo", C)[:, c, :],
                                             start=(c == 0), stop=(c == C - 1))
                        last.then_inc(y_ps, 1)

        @block.scalar
        def _(act):
            with act.Fori(0, B // 2) as i:
                for j in range(2):
                    act.wait_ge(xT_ps, 2 * i + j + 1)
                    if two_norms:
                        for c in range(C):
                            last = act.activation(xT[:, j, c, :], ps[0:K, j, 3, c * L:(c + 1) * L], ACT.Identity,
                                                  scale=w.at("g")[:, c:c + 1], bias=w.at("b")[:, c:c + 1])
                    else:
                        last = act.activation(xT[:, j, :, :].rearrange("p c n -> p (c n)"),
                                              ps[0:K, j, 3, 0:C * L], ACT.Copy)
                    last.then_inc(xT_ready, 1)
                for j in range(2):
                    act.wait_ge(qkv_ps, 2 * i + j + 1)
                    for bank, dst, bias in ((0, qT, "bq"), (1, kT, "bk")):
                        if bias in w.where:
                            for t in range(HT):
                                last = act.activation(dst[:, j, t, :], ps[:, j, bank, t * L:(t + 1) * L],
                                                      ACT.Identity, bias=w.at(bias)[:, t:t + 1])
                        else:
                            last = act.activation(dst[:, j, :, :].rearrange("p t n -> p (t n)"),
                                                  ps[:, j, bank, 0:HT * L], ACT.Copy)
                    last.then_inc(qk_ready, 1)
                for j in range(2):
                    act.wait_ge(below_ready, 2 * i + j + 1)
                    act.activation(p[:, j, :, :], p[:, j, :, :], ACT.Exp, scale=HD ** -0.5).then_inc(p_ready, 1)
                for j in range(2):
                    act.wait_ge(pT_ps, 2 * i + j + 1)
                    act.activation(pT[:, j, :, :].rearrange("p (r t) n -> p r t n", r=RG), banked(j), ACT.Copy)\
                       .then_inc(pT_ready, 1)
                if gated:
                    for j in range(2):
                        act.wait_ge(lin_ps, 2 * i + j + 1)
                        for n, bias in ((0, "lin_bq"), (1, "lin_bk")):
                            for c in range(C):
                                last = act.activation(lin_x[:, j, n * C + c, :], ps[0:K, j, 1 + n, c * L:(c + 1) * L],
                                                      ACT.Identity, bias=w.at(bias)[:, c:c + 1])
                        last.then_inc(lin_x_ready, 1)
                    for j in range(2):
                        act.wait_ge(lin_m_ready, 2 * i + j + 1)
                        act.activation(lin_e[:, j, :, :], lin_e[:, j, :, :], ACT.Exp).then_inc(lin_e_ready, 1)
                    for j in range(2):
                        act.wait_ge(lin_s_ps, 2 * i + j + 1)
                        act.activation(lin_s[:, j, :], ps[0:L, j, 1, 0:L], ACT.Copy).then_inc(lin_s_ready, 1)
                    for j in range(2):
                        act.wait_ge(mixT_ps, 2 * i + j + 1)
                        act.activation(mixT[:, j, :, :].rearrange("p c n -> p (c n)"), ps[0:K, j, 3, 0:2 * C * L],
                                       ACT.Copy).then_inc(mixT_ready, 1)
                    for j in range(2):
                        act.wait_ge(hid_ps, 2 * i + j + 1)
                        for c in range(C):
                            last = act.activation(hidT[:, j, c, :], ps[0:K, j, 0, c * L:(c + 1) * L], ACT.Relu,
                                                  bias=w.at("bg1")[:, c:c + 1])
                        last.then_inc(hid_ready, 1)
                    for j in range(2):
                        act.wait_ge(gate_in, 2 * i + j + 1)
                        act.activation(gate[:, j, :], gate[:, j, :], ACT.Exp, scale=-1.0).then_inc(gate_exp, 1)
                if project:
                    for j in range(2):
                        act.wait_ge(oT_ps, 2 * i + j + 1)
                        act.activation(oT[:, j, :, :].rearrange("p c n -> p (c n)"), ps[0:K, j, 1, 0:C * L],
                                       ACT.Copy).then_inc(oT_ready, 1)

        @block.gpsimd
        def _(pool):
            if gated:
                pool.memset(lin_v[:, :, :], 1.0)
            pool.memset(v[:, :, :, :], 1.0).then_inc(const_ready, 1)
            with pool.Fori(0, B // 2) as i:
                norm.pool(pool, i)
                if two_norms:
                    norm2.pool(pool, i)

        @block.vector
        def _(dve):
            if mask:
                for t in range(HT):
                    last = dve.tensor_copy(mask_bf[:, t, :], w.at(mask))
                last.then_inc(const_ready, 1)
                dve.tensor_copy(ident_bf[:, :], ident[0:L, 0:L]).then_inc(const_ready, 1)
            dve.wait_ge(const_ready, 3 if mask else 1)
            own = 4 + 6 * two_norms + 4 * conv + 4 + 2 * project + 14 * gated
            with dve.Fori(0, B // 2) as i:
                steps = Steps(dve, dve_steps, own * i)
                tile = [ds(2 * i + j, 1) for j in range(2)]
                if two_norms:
                    for ins in norm.vector(dve, i, steps, [h[:, tile[j], :] for j in range(2)],
                                           [z0[:, j:j + 1, :] for j in range(2)]):
                        steps.done(ins)
                    steps.wait()
                    second = norm2.vector(dve, i, steps, [z0[:, j:j + 1, :] for j in range(2)],
                                          [z[:, j:j + 1, :] for j in range(2)])
                else:
                    second = norm.vector(dve, i, steps, [h[:, tile[j], :] for j in range(2)],
                                         [z[:, j:j + 1, :] for j in range(2)])
                for ins in second:
                    ins.then_inc(z_ready, 1)
                for j in range(2):
                    dve.wait_ge(qkv_ps, 2 * i + j + 1)
                    heads = ps[0:L, j, 2, 0:D].rearrange("p (a n) -> p a n", a=H)
                    if "bv" in w.where:
                        last = dve.tensor_tensor(v[:, j, :, 0:HD], heads, w.at("bv", H), ALU.add)
                    else:
                        last = dve.tensor_copy(v[:, j, :, 0:HD], heads)
                    last.then_inc(v_ready, 1)
                if conv:
                    for j in range(2):
                        dve.wait_ge(qk_ready, 2 * i + j + 1)
                        for n, src, dst, own_w, side_w in ((0, qT, q2, 0, 1), (1, kT, k2, 2, 3)):
                            mix = w.at("mix")
                            dve.tensor_scalar(side[:, j, n, :, :], src[:, j, :, :], mix[:, side_w:side_w + 1], None,
                                              ALU.mult)
                            steps.done(dve.tensor_scalar(dst[:, j, :, :], src[:, j, :, :], mix[:, own_w:own_w + 1],
                                                         None, ALU.mult))
                    for j in range(2):
                        steps.wait()
                        for n, dst in ((0, q2), (1, k2)):
                            left = dve.tensor_tensor(dst[:, j, :, 1:L], dst[:, j, :, 1:L], side[:, j, n, :, 0:L - 1],
                                                     ALU.add)
                        left.then_inc(left_added, 1)
                        dve.wait_ge(left_added, 2 * i + j + 1)
                        for n, dst in ((0, q2), (1, k2)):
                            last = dve.tensor_tensor(dst[:, j, :, 0:L - 1], dst[:, j, :, 0:L - 1],
                                                     side[:, j, n, :, 1:L], ALU.add)
                        last.then_inc(mixed_ready, 1)
                for j in range(2):
                    dve.wait_ge(s_ps, 2 * i + j + 1)
                    steps.done(dve.tensor_reduce(top[:, j, :].rearrange("p (r t) -> p r t", r=RG), banked(j),
                                                 AX.X, ALU.max))
                    steps.wait()
                    peak = top[:, j, :].rearrange("p (r t) -> p r t", r=RG).unsqueeze(3).broadcast_to([L, RG, HT, L])
                    dve.tensor_tensor(p[:, j, :, :].rearrange("p (r t) n -> p r t n", r=RG), banked(j), peak,
                                      ALU.subtract).then_inc(below_ready, 1)
                for j in range(2):
                    dve.wait_ge(o_ps, 2 * i + j + 1)
                    heads = ps[0:L, j, 0, 0:H * VW].rearrange("p (a n) -> p a n", a=H)
                    steps.done(dve.reciprocal(rsum[:, j, :].unsqueeze(2), heads[:, :, HD:VW]))
                    steps.wait()
                    dve.tensor_tensor(o[:, j, :].rearrange("p (a n) -> p a n", a=H), heads[:, :, 0:HD],
                                      rsum[:, j, :].unsqueeze(2).broadcast_to([L, H, HD]), ALU.mult)\
                       .then_inc(o_ready, 1)
                if gated:
                    for j in range(2):
                        dve.wait_ge(lin_x_ready, 2 * i + j + 1)
                        dve.tensor_scalar(lin_e[:, j, :, :], lin_x[:, j, :, :], 0.0, None, ALU.min)\
                           .then_inc(lin_m_ready, 1)
                        dve.wait_ge(lin_ps, 2 * i + j + 1)
                        dve.tensor_tensor(lin_v[:, j, 0:D], ps[0:L, j, 3, 0:D], w.at("lin_bv"), ALU.add)\
                           .then_inc(lin_v_ready, 1)
                    for j in range(2):
                        dve.wait_ge(lin_e_ready, 2 * i + j + 1)
                        dve.scalar_tensor_tensor(lin_f[:, j, :, :], lin_x[:, j, :, :], 0.0, lin_e[:, j, :, :],
                                                 ALU.max, ALU.add).then_inc(lin_f_ready, 1)
                    for j in range(2):
                        dve.wait_ge(lin_o_ps, 2 * i + j + 1)
                        steps.done(dve.tensor_scalar(lin_d[:, j:j + 1], ps[0:L, j, 2, D:D + 1], 1e-6, None, ALU.add))
                        steps.wait()
                        steps.done(dve.reciprocal(lin_d[:, j:j + 1], lin_d[:, j:j + 1]))
                        steps.wait()
                        dve.tensor_scalar(lin_o[:, j, :], ps[0:L, j, 2, 0:D], lin_d[:, j:j + 1], None, ALU.mult)\
                           .then_inc(lin_o_ready, 1)
                    for j in range(2):
                        dve.wait_ge(lin_o_ready, 2 * i + j + 1)
                        steps.done(dve.tensor_tensor(diff[:, j, :], lin_o[:, j, :], o[:, j, :], ALU.subtract))
                    for j in range(2):
                        dve.wait_ge(gate_ps, 2 * i + j + 1)
                        dve.tensor_tensor(gate[:, j, :], ps[0:L, j, 1, 0:D], w.at("bg2"), ALU.add)\
                           .then_inc(gate_in, 1)
                    for j in range(2):
                        dve.wait_ge(gate_exp, 2 * i + j + 1)
                        steps.done(dve.tensor_scalar(gate[:, j, :], gate[:, j, :], 1.0, None, ALU.add))
                        steps.wait()
                        steps.done(dve.reciprocal(gate[:, j, :], gate[:, j, :]))
                        steps.wait()
                        steps.done(dve.tensor_tensor(diff[:, j, :], diff[:, j, :], gate[:, j, :], ALU.mult))
                        steps.wait()
                        dve.tensor_tensor(fused[:, j, :], diff[:, j, :], o[:, j, :], ALU.add)\
                           .then_inc(fused_ready, 1)
                for j in range(2):
                    if project:
                        dve.wait_ge(y_ps, 2 * i + j + 1)
                        steps.done(dve.tensor_tensor(y[:, j, :], ps[0:L, j, 2, 0:D], w.at("bo"), ALU.add))
                        steps.wait()
                        add = y[:, j:j + 1, :]
                    else:
                        dve.wait_ge(o_ready, 2 * i + j + 1)
                        add = o[:, j:j + 1, :]
                    if gated:
                        steps.done(dve.tensor_tensor(y[:, j, :], y[:, j, :], z0[:, j, :], ALU.add))
                        steps.wait()
                    if residual == "normed":
                        dve.tensor_tensor(x[:, tile[j], :], z0[:, j:j + 1, :], add, ALU.add)
                    else:
                        dve.tensor_tensor(h[:, tile[j], :], h[:, tile[j], :], add, ALU.add)
                assert steps.n == own, (steps.n, own)


def route(nc, g, phase, two_norms):
    w = g[phase]
    ident, iota = g["const"].at("ident"), g["const"].at("iota")[:, 0:E01]
    bias = "b2" in w.where
    ps, h, x, xT_all, gates = g["ps"], g["h"], g["x"], g["xT"], g["gates"]
    with ExitStack() as stack:
        m = Memory(nc, g, stack, phase)
        norm = Norm(m, g, "norm")
        norm2 = Norm(m, g, "norm2") if two_norms else None
        z0 = m.sb("z0", [L, 2, D]) if two_norms else None
        z = m.sb("z", [L, 2, D])
        xT = m.sb("xT", [K, 2, C, L])
        logits = m.sb("logits", [L, 2, E01])
        best = m.sb("best", [L, 2, 8])
        place = m.sb("place", [L, 2, 8], U32)
        placef = m.sb("placef", [L, 2, 8])
        gap = m.sb("gap", [L, 2])
        ratio = m.sb("ratio", [L, 2])
        total = m.sb("total", [L, 2])
        share = m.sb("share", [L, 2, 2])
        part = m.sb("part", [L, 2, 2, E01])
        pause = m.sb("pause", [1, 1])
        if bias:
            gate_row = m.sb("gate_row", [L, 2, E01])
            gT = m.sb("gT", [E01, 2, L])
        dve_steps = m.sem("dve_steps")
        z_ready, xT_ps, xT_ready, xT_kept = m.sem("z_ready"), m.sem("xT_ps"), m.sem("xT_ready"), m.sem("xT_kept")
        logits_ps, gap_ready, ratio_ready = m.sem("logits_ps"), m.sem("gap_ready"), m.sem("ratio_ready")
        gates_ready, gT_ps, gT_ready, b2_ps = m.sem("gates_ready"), m.sem("gT_ps"), m.sem("gT_ready"), m.sem("b2_ps")
        block = stack.enter_context(nc.Block())

        @block.tensor
        def _(pe):
            with pe.Fori(0, B // 2) as i:
                for j in range(2):
                    pe.wait_ge(z_ready, 2 * i + j + 1)
                    for c in range(C):
                        last = pe.transpose(ps[0:K, j, 3, c * L:(c + 1) * L], z[:, j, c * K:(c + 1) * K],
                                            ident[0:L, 0:L])
                    last.then_inc(xT_ps, 1)
                for j in range(2):
                    pe.wait_ge(xT_ready, 2 * i + j + 1)
                    for c in range(C):
                        last = pe.matmul(ps[0:L, j, 0, 0:E01], xT[:, j, c, :], w.at("gate", C)[:, c, :],
                                         start=(c == 0), stop=(c == C - 1))
                    last.then_inc(logits_ps, 1)
                if bias:
                    for j in range(2):
                        pe.wait_ge(gates_ready, i + 1)
                        pe.transpose(ps[0:E01, j, 1, 0:L], gate_row[:, j, :], ident[0:L, 0:L]).then_inc(gT_ps, 1)
                    for j in range(2):
                        pe.wait_ge(gT_ready, 2 * i + j + 1)
                        pe.matmul(ps[0:L, j, 2, 0:D], gT[:, j, :], w.at("b2"), start=True, stop=True)\
                          .then_inc(b2_ps, 1)

        @block.scalar
        def _(act):
            with act.Fori(0, B // 2) as i:
                for j in range(2):
                    act.wait_ge(xT_ps, 2 * i + j + 1)
                    for c in range(C):
                        last = act.activation(xT[:, j, c, :], ps[0:K, j, 3, c * L:(c + 1) * L], ACT.Identity,
                                              scale=w.at("g")[:, c:c + 1], bias=w.at("b")[:, c:c + 1])
                    last.then_inc(xT_ready, 1)
                act.wait_ge(gap_ready, i + 1)
                act.activation(ratio[:, :], gap[:, :], ACT.Exp).then_inc(ratio_ready, 1)
                if bias:
                    for j in range(2):
                        act.wait_ge(gT_ps, 2 * i + j + 1)
                        act.activation(gT[:, j, :], ps[0:E01, j, 1, 0:L], ACT.Copy).then_inc(gT_ready, 1)
                act.wait_ge(xT_kept, 2 * i + 2)

        @block.gpsimd
        def _(pool):
            with pool.Fori(0, B // 2) as i:
                norm.pool(pool, i)
                if two_norms:
                    norm2.pool(pool, i)
                for j in range(2):
                    pool.wait_ge(xT_ready, 2 * i + j + 1)
                    pool.tensor_copy(xT_all[:, :, ds(2 * i + j, 1), :], xT[:, j, :, :].unsqueeze(2))\
                        .then_inc(xT_kept, 1)

        @block.vector
        def _(dve):
            own = 4 + 6 * two_norms + 2 + 2 + 3 + 1 + 1 + 2 + 2 + (2 if bias else 0)
            with dve.Fori(0, B // 2) as i:
                steps = Steps(dve, dve_steps, own * i)
                tile = [ds(2 * i + j, 1) for j in range(2)]
                if two_norms:
                    for ins in norm.vector(dve, i, steps, [h[:, tile[j], :] for j in range(2)],
                                           [z0[:, j:j + 1, :] for j in range(2)]):
                        steps.done(ins)
                    steps.wait()
                    src = [z0[:, j:j + 1, :] for j in range(2)]
                    second = norm2
                else:
                    src = [x[:, tile[j], :] for j in range(2)]
                    second = norm
                for ins in second.vector(dve, i, steps, src, [z[:, j:j + 1, :] for j in range(2)]):
                    ins.then_inc(z_ready, 1)
                for j in range(2):
                    steps.done(dve.tensor_tensor(h[:, tile[j], :], h[:, tile[j], :], src[j], ALU.add))
                for j in range(2):
                    dve.wait_ge(logits_ps, 2 * i + j + 1)
                    steps.done(dve.tensor_copy(logits[:, j, :], ps[0:L, j, 0, 0:E01]))
                steps.wait()
                dve.memset(pause[:, :], 0.0)
                for j in range(2):
                    last = dve.max(best[:, j, :], logits[:, j, :])
                steps.done(last)
                steps.wait()
                dve.tensor_tensor(gap[:, :], best[:, :, 1], best[:, :, 0], ALU.subtract).then_inc(gap_ready, 1)
                for j in range(2):
                    last = dve.max_index(place[:, j, :], best[:, j, :], logits[:, j, :])
                steps.done(last)
                steps.wait()
                steps.done(dve.tensor_copy(placef[:, :, :], place[:, :, :]))
                dve.wait_ge(ratio_ready, i + 1)
                steps.done(dve.tensor_scalar(total[:, :], ratio[:, :], 1.0, None, ALU.add))
                steps.wait()
                steps.done(dve.reciprocal(share[:, :, 0], total[:, :]))
                steps.wait()
                steps.done(dve.tensor_tensor(share[:, :, 1], share[:, :, 0], ratio[:, :], ALU.mult))
                steps.wait()
                for j in range(2):
                    for n in range(2):
                        last = dve.tensor_scalar(part[:, j, n, :], iota, placef[:, j, n:n + 1],
                                                 share[:, j, n:n + 1], ALU.is_equal, ALU.mult)
                    steps.done(last)
                steps.wait()
                if bias:
                    dve.tensor_tensor(gate_row[:, :, :], part[:, :, 0, :], part[:, :, 1, :], ALU.add)\
                       .then_inc(gates_ready, 1)
                steps.done(dve.tensor_tensor(gates[:, ds(2 * i, 2), 0:E01], part[:, :, 0, :], part[:, :, 1, :],
                                             ALU.add))
                if bias:
                    for j in range(2):
                        dve.wait_ge(b2_ps, 2 * i + j + 1)
                        steps.done(dve.tensor_tensor(h[:, tile[j], :], h[:, tile[j], :], ps[0:L, j, 2:3, 0:D],
                                                     ALU.add))
                assert steps.n == own, (steps.n, own)


def experts(nc, g, dram, phase, func):
    bias = phase == "l0"
    ps, h, xT_all, gates = g["ps"], g["h"], g["xT"], g["gates"]
    hid_banks = 4
    with ExitStack() as stack:
        m = Memory(nc, g, stack, phase)
        up = m.sb("up", [K, 2, C, F])
        down = m.sb("down", [128, 2, FM, D])
        b1 = m.sb("b1", [128, 2, FM]) if bias else None
        hidden = m.sb("hidden", [128, 2, FM, NG])
        up_loaded = [m.sem(f"up_loaded{j}") for j in range(2)]
        hid_ps, hid_ready = m.sem("hid_ps"), m.sem("hid_ready")
        y_ps, y_added = m.sem("y_ps"), m.sem("y_added")
        per_load = 16 * (3 if bias else 2)
        block = stack.enter_context(nc.Block())

        def visit(i, j, qq, jj):
            return (2 * i + j) * G + 2 * qq + jj

        @block.sync
        def _(sp):
            def load(e, j):
                sp.dma_start(up[:, j, :, :], dram[phase + "_up"][e].rearrange("e p (c n) -> p (e c) n", c=C))\
                  .then_inc(up_loaded[j], 16)
                sp.dma_start(down[:, j, :, :], dram[phase + "_down"][e].rearrange("e p (m n) -> p (e m) n", m=FM))\
                  .then_inc(up_loaded[j], 16)
                if bias:
                    sp.dma_start(b1[:, j, :], dram[phase + "_b1"][e].rearrange("e p m -> p (e m)"))\
                      .then_inc(up_loaded[j], 16)
            for j in range(2):
                load(slice(j, j + 1), j)
            with sp.Fori(1, E01 // 2) as i:
                for j in range(2):
                    sp.wait_ge(y_ps, (2 * i + j - 1) * G * GB)
                    load(ds(2 * i + j, 1), j)

        @block.tensor
        def _(pe):
            with pe.Fori(0, E01 // 2) as i:
                for j in range(2):
                    with pe.Fori(0, G // 2) as qq:
                        pe.wait_ge(up_loaded[j], per_load * (i + 1))
                        for jj in range(2):
                            n = visit(i, j, qq, jj)
                            for t in range(FM):
                                pe.wait_ge(hid_ready, n * FM + t + 1)
                                bank = (jj * FM + t) % hid_banks
                                for c in range(C):
                                    last = pe.matmul(ps[:, 0, bank, 0:NG], up[:, j, c, t * 128:(t + 1) * 128],
                                                     xT_all[:, c, ds((2 * qq + jj) * GB, GB), :],
                                                     start=(c == 0), stop=(c == C - 1))
                                last.then_inc(hid_ps, 1)
                        for jj in range(2):
                            n = visit(i, j, qq, jj)
                            pe.wait_ge(hid_ready, hid_banks + (n + 1) * FM)
                            for b in range(GB):
                                pe.wait_ge(y_added, n * GB + b + 1)
                                for t in range(FM):
                                    last = pe.matmul(ps[0:L, 1, b, 0:D], hidden[:, jj, t, b * L:(b + 1) * L],
                                                     down[:, j, t, :], start=(t == 0), stop=(t == FM - 1))
                                last.then_inc(y_ps, 1)

        @block.scalar
        def _(act):
            act.sem_inc(hid_ready, hid_banks)
            if bias:
                act.wait_ge(up_loaded[0], per_load)
            with act.Fori(0, E01 // 2) as i:
                for j in range(2):
                    with act.Fori(0, G // 2) as qq:
                        if bias:
                            act.wait_ge(up_loaded[j], per_load * (i + 1))
                        for jj in range(2):
                            n = visit(i, j, qq, jj)
                            for t in range(FM):
                                act.wait_ge(hid_ps, n * FM + t + 1)
                                bank = (jj * FM + t) % hid_banks
                                act.activation(hidden[:, jj, t, :], ps[:, 0, bank, 0:NG], func,
                                               bias=b1[:, j, t:t + 1] if bias else 0.0).then_inc(hid_ready, 1)

        @block.vector
        def _(dve):
            dve.sem_inc(y_added, GB)
            with dve.Fori(0, E01 // 2) as i:
                for j in range(2):
                    with dve.Fori(0, G // 2) as qq:
                        for jj in range(2):
                            n = visit(i, j, qq, jj)
                            for b in range(GB):
                                dve.wait_ge(y_ps, n * GB + b + 1)
                                tile = ds((2 * qq + jj) * GB + b, 1)
                                dve.scalar_tensor_tensor(h[:, tile, :], ps[0:L, 1, b:b + 1, 0:D],
                                                         gates[:, tile, ds(2 * i + j, 1)].rearrange("p a b -> p (a b)"),
                                                         h[:, tile, :], ALU.mult, ALU.add).then_inc(y_added, 1)


def sub_gates(nc, g, sub):
    w = g["l2f"]
    ident, iota = g["const"].at("ident"), g["const"].at("iota")
    ps, h = g["ps"], g["h"]
    zT, gate_all, comb = sub["zT"], sub["gates"], sub["comb"]
    with ExitStack() as stack:
        m = Memory(nc, g, stack, "l2g")
        norm = Norm(m, g, "norm")
        z = m.sb("z", [L, 2, D])
        xT = m.sb("xT", [K, 2, C, L])
        sT = m.sb("sT", [128, 2, L])
        score = m.sb("score", [L, 2, NS, NM])
        best = m.sb("best", [L, 2, NS, 8])
        place = m.sb("place", [L, 2, NS, 8], U32)
        last_place = m.sb("last_place", [L, 2, NS])
        few = m.sb("few", [L, 2, NS, KEEP])
        share = m.sb("share", [L, 2, NS])
        expo = m.sb("expo", [L, 2, NS, NM])
        above = m.sb("above", [L, 2, NS, NM])
        tied = m.sb("tied", [L, 2, NS, NM])
        early = m.sb("early", [L, 2, NS, NM])
        gate = m.sb("gate", [L, 2, NS * NM])
        gT = m.sb("gT", [128, 2, 4, L])
        pause = m.sb("pause", [1, 1])
        dve_steps = m.sem("dve_steps")
        z_ready, xT_ps, xT_ready = m.sem("z_ready"), m.sem("xT_ps"), m.sem("xT_ready")
        sT_ps, sT_ready, score_ps, score_ready = m.sem("sT_ps"), m.sem("sT_ready"), m.sem("score_ps"), m.sem("score_ready")
        few_ready, few_exp, below, below_exp = m.sem("few_ready"), m.sem("few_exp"), m.sem("below"), m.sem("below_exp")
        gate_ready, gate_kept = m.sem("gate_ready"), m.sem("gate_kept")
        gT_ps, gT_ready, b2_ps = m.sem("gT_ps"), m.sem("gT_ready"), m.sem("b2_ps")
        block = stack.enter_context(nc.Block())

        @block.tensor
        def _(pe):
            with pe.Fori(0, B // 2) as i:
                for j in range(2):
                    pe.wait_ge(z_ready, 2 * i + j + 1)
                    for c in range(C):
                        last = pe.transpose(ps[0:K, j, 3, c * L:(c + 1) * L], z[:, j, c * K:(c + 1) * K],
                                            ident[0:L, 0:L])
                    last.then_inc(xT_ps, 1)
                for j in range(2):
                    pe.wait_ge(xT_ready, 2 * i + j + 1)
                    for c in range(C):
                        last = pe.matmul(ps[:, j, 0, 0:L], w.at("p", C)[:, c, :], xT[:, j, c, :],
                                         start=(c == 0), stop=(c == C - 1))
                    last.then_inc(sT_ps, 1)
                for j in range(2):
                    pe.wait_ge(sT_ready, 2 * i + j + 1)
                    pe.matmul(ps[0:L, j, 1, :], sT[:, j, :], w.at("centres"), start=True, stop=True)\
                      .then_inc(score_ps, 1)
                for j in range(2):
                    pe.wait_ge(gate_ready, 2 * i + j + 1)
                    for n in range(4):
                        last = pe.transpose(ps[:, j, 2, n * L:(n + 1) * L], gate[:, j, n * 128:(n + 1) * 128],
                                            ident[0:L, 0:L])
                    last.then_inc(gT_ps, 1)
                for j in range(2):
                    pe.wait_ge(gT_ready, 2 * i + j + 1)
                    for n in range(4):
                        last = pe.matmul(ps[0:L, j, 0, 0:128], gT[:, j, n, :], w.at("b2", 4)[:, n, :],
                                         start=(n == 0), stop=(n == 3))
                    last.then_inc(b2_ps, 1)

        @block.scalar
        def _(act):
            with act.Fori(0, B // 2) as i:
                for j in range(2):
                    act.wait_ge(xT_ps, 2 * i + j + 1)
                    act.activation(xT[:, j, :, :].rearrange("p c n -> p (c n)"), ps[0:K, j, 3, 0:C * L],
                                   ACT.Copy).then_inc(xT_ready, 1)
                for j in range(2):
                    act.wait_ge(sT_ps, 2 * i + j + 1)
                    act.activation(sT[:, j, :], ps[:, j, 0, 0:L], ACT.Copy).then_inc(sT_ready, 1)
                for j in range(2):
                    act.activation(zT[:, ds(2 * i + j, 1), :], ps[:, j, 0:1, 0:L], ACT.Copy)
                for j in range(2):
                    act.wait_ge(score_ps, 2 * i + j + 1)
                    act.activation(score[:, j, :, :].rearrange("p s m -> p (s m)"), ps[0:L, j, 1, :], ACT.Copy)\
                       .then_inc(score_ready, 1)
                for j in range(2):
                    act.wait_ge(below, 2 * i + j + 1)
                    act.activation(expo[:, j, :, :], expo[:, j, :, :], ACT.Exp).then_inc(below_exp, 1)
                    act.wait_ge(few_ready, 2 * i + j + 1)
                    act.activation(few[:, j, :, :], few[:, j, :, :], ACT.Exp).then_inc(few_exp, 1)
                for j in range(2):
                    act.wait_ge(gT_ps, 2 * i + j + 1)
                    act.activation(gT[:, j, :, :].rearrange("p a n -> p (a n)"), ps[:, j, 2, 0:4 * L], ACT.Copy)\
                       .then_inc(gT_ready, 1)

        @block.gpsimd
        def _(pool):
            with pool.Fori(0, B // 2) as i:
                norm.pool(pool, i)
                for j in range(2):
                    pool.wait_ge(gate_ready, 2 * i + j + 1)
                    pool.tensor_copy(gate_all[:, ds(2 * i + j, 1), :], gate[:, j:j + 1, :]).then_inc(gate_kept, 1)

        @block.vector
        def _(dve):
            own = 4 + 2 * 11
            with dve.Fori(0, B // 2) as i:
                steps = Steps(dve, dve_steps, own * i)
                for ins in norm.vector(dve, i, steps, [h[:, ds(2 * i + j, 1), :] for j in range(2)],
                                       [z[:, j:j + 1, :] for j in range(2)]):
                    ins.then_inc(z_ready, 1)
                for j in range(2):
                    dve.wait_ge(score_ready, 2 * i + j + 1)
                    dve.memset(pause[:, :], 0.0)
                    for n in range(NS):
                        last = dve.max(best[:, j, n, :], score[:, j, n, :])
                    steps.done(last)
                    steps.wait()
                    dve.tensor_tensor(expo[:, j, :, :], score[:, j, :, :],
                                      best[:, j, :, 0:1].broadcast_to([L, NS, NM]), ALU.subtract).then_inc(below, 1)
                    dve.tensor_tensor(few[:, j, :, :], best[:, j, :, 0:KEEP],
                                      best[:, j, :, 0:1].broadcast_to([L, NS, KEEP]), ALU.subtract)\
                       .then_inc(few_ready, 1)
                    for n in range(NS):
                        last = dve.max_index(place[:, j, n, :], best[:, j, n, :], score[:, j, n, :])
                    steps.done(last)
                    fourth = best[:, j, :, KEEP - 1:KEEP].broadcast_to([L, NS, NM])
                    steps.done(dve.tensor_tensor(above[:, j, :, :], score[:, j, :, :], fourth, ALU.is_gt))
                    steps.done(dve.tensor_tensor(tied[:, j, :, :], score[:, j, :, :], fourth, ALU.is_equal))
                    steps.wait()
                    steps.done(dve.tensor_copy(last_place[:, j, :], place[:, j, :, KEEP - 1]))
                    steps.wait()
                    steps.done(dve.tensor_tensor(early[:, j, :, :], iota.unsqueeze(1).broadcast_to([L, NS, NM]),
                                                 last_place[:, j, :].unsqueeze(2).broadcast_to([L, NS, NM]),
                                                 ALU.is_le))
                    dve.wait_ge(few_exp, 2 * i + j + 1)
                    steps.done(dve.tensor_reduce(share[:, j, :], few[:, j, :, :], AX.X, ALU.add))
                    steps.wait()
                    steps.done(dve.tensor_tensor(tied[:, j, :, :], tied[:, j, :, :], early[:, j, :, :], ALU.mult))
                    steps.wait()
                    steps.done(dve.reciprocal(share[:, j, :], share[:, j, :]))
                    steps.done(dve.tensor_tensor(above[:, j, :, :], above[:, j, :, :], tied[:, j, :, :], ALU.add))
                    dve.wait_ge(below_exp, 2 * i + j + 1)
                    steps.wait()
                    steps.done(dve.tensor_tensor(above[:, j, :, :], above[:, j, :, :], expo[:, j, :, :], ALU.mult))
                    steps.wait()
                    for half in range(2):
                        dst = gate[:, j, half * 256:(half + 1) * 256].rearrange("p (b a m) -> p a b m", b=8, a=RG)
                        src = above[:, j, half::2, :].rearrange("p a (b m) -> p a b m", b=8)
                        rate = share[:, j, half::2].unsqueeze(2).unsqueeze(3).broadcast_to([L, RG, 8, 8])
                        last = dve.tensor_tensor(dst, src, rate, ALU.mult)
                    last.then_inc(gate_ready, 1)
                for j in range(2):
                    dve.wait_ge(b2_ps, 2 * i + j + 1)
                    dve.tensor_copy(comb[:, ds(2 * i + j, 1), :], ps[0:L, j, 0:1, 0:128])
                dve.wait_ge(gate_kept, 2 * i + 2)
                assert steps.n == own, (steps.n, own)


def sub_experts(nc, g, dram, sub):
    ps, zT, gate_all, comb = g["ps"], sub["zT"], sub["gates"], sub["comb"]
    visits = 2 * G
    with ExitStack() as stack:
        m = Memory(nc, g, stack, "l2s")
        up = m.sb("up", [128, 2, 2, 128])
        down = m.sb("down", [128, 2, VT, 64])
        b1 = m.sb("b1", [128, 2, VT])
        hidden = m.sb("hidden", [128, 2, VT, NG])
        prod = m.sb("prod", [L, 2, 32, NR])
        part = m.sb("part", [L, 2, RG, NR])
        loaded = [m.sem(f"loaded{j}") for j in range(2)]
        hid_ps, hid_ready, y_ps, y_read = m.sem("hid_ps"), m.sem("hid_ready"), m.sem("y_ps"), m.sem("y_read")
        part_ready, summed = m.sem("part_ready"), m.sem("summed")
        block = stack.enter_context(nc.Block())

        @block.sync
        def _(sp):
            def load(v, j):
                sp.dma_start(up[:, j, :, :], dram["sub_up"][v].rearrange("v p (u n) -> p (v u) n", u=2))\
                  .then_inc(loaded[j], 16)
                sp.dma_start(down[:, j, :, :], dram["sub_down"][v].rearrange("v p (t n) -> p (v t) n", t=VT))\
                  .then_inc(loaded[j], 16)
                sp.dma_start(b1[:, j, :], dram["sub_b1"][v].rearrange("v p t -> p (v t)")).then_inc(loaded[j], 16)
            for j in range(2):
                load(slice(j, j + 1), j)
            with sp.Fori(1, NV // 2) as i:
                for j in range(2):
                    sp.wait_ge(y_ps, (2 * i + j - 1) * B)
                    load(ds(2 * i + j, 1), j)

        @block.tensor
        def _(pe):
            with pe.Fori(0, NV // 2) as i:
                for j in range(2):
                    pe.wait_ge(loaded[j], 48 * (i + 1))
                    for qq in range(G // 2):
                        for jj in range(2):
                            q = 2 * qq + jj
                            n = visits * i + G * j + q
                            for u in range(2):
                                for r in range(RG):
                                    t = 2 * r + u
                                    pe.wait_ge(hid_ready, n * VT + u * RG + r + 1)
                                    pe.matmul(ps[:, 0, r, 0:NG], up[HP * r:HP * (r + 1), j, u, :],
                                              zT[HP * r:HP * (r + 1), q * GB:(q + 1) * GB, :],
                                              start=True, stop=True).then_inc(hid_ps, 1)
                        for jj in range(2):
                            q = 2 * qq + jj
                            n = visits * i + G * j + q
                            pe.wait_ge(hid_ready, RG + (n + 1) * VT)
                            for b in range(GB):
                                pe.wait_ge(y_read, n * GB + b + 1)
                                for t in range(VT):
                                    last = pe.matmul(ps[0:L, 1, b, t * 64:(t + 1) * 64],
                                                     hidden[:, jj, t, b * L:(b + 1) * L], down[:, j, t, :],
                                                     start=True, stop=True)
                                last.then_inc(y_ps, 1)

        @block.scalar
        def _(act):
            act.sem_inc(hid_ready, RG)
            with act.Fori(0, NV // 2) as i:
                for j in range(2):
                    act.wait_ge(loaded[j], 48 * (i + 1))
                    for q in range(G):
                        n = visits * i + G * j + q
                        for u in range(2):
                            for r in range(RG):
                                t = 2 * r + u
                                act.wait_ge(hid_ps, n * VT + u * RG + r + 1)
                                act.activation(hidden[:, q % 2, t, :], ps[:, 0, r, 0:NG], ACT.Gelu_apprx_tanh,
                                               bias=b1[:, j, t:t + 1]).then_inc(hid_ready, 1)

        @block.vector
        def _(dve):
            dve.sem_inc(y_read, GB)
            with dve.Fori(0, NV // 2) as i:
                half = i // (NV // 4)
                for j in range(2):
                    for q in range(G):
                        n = visits * i + G * j + q
                        for b in range(GB):
                            a = b % 2
                            tile = q * GB + b
                            dve.wait_ge(y_ps, n * GB + b + 1)
                            dve.tensor_tensor(prod[:, a, :, :], ps[0:L, 1, b, :].rearrange("p (m r) -> p m r", r=NR),
                                              gate_all[:, tile, ds((2 * i + j) * 32, 32)].unsqueeze(2)
                                              .broadcast_to([L, 32, NR]), ALU.mult).then_inc(y_read, 1)
                            dve.wait_ge(y_read, GB + n * GB + b + 1)
                            dve.tensor_reduce(part[:, a, :, :],
                                              prod[:, a, :, :].rearrange("p (g m) r -> p g r m", g=RG),
                                              AX.X, ALU.add).then_inc(part_ready, 1)
                            dve.wait_ge(part_ready, n * GB + b + 1)
                            dst = comb[:, tile, ds(half * 64, 64)].rearrange("p (g r) -> p g r", g=RG)
                            dve.tensor_tensor(dst, dst, part[:, a, :, :], ALU.add)


def sub_output(nc, g, sub):
    w = g["l2f"]
    ident = g["const"].at("ident")
    ps, h, comb = g["ps"], g["h"], sub["comb"]
    with ExitStack() as stack:
        m = Memory(nc, g, stack, "l2o")
        c0 = m.sb("c0", [L, 2, 128])
        cT = m.sb("cT", [128, 2, L])
        hT = m.sb("hT", [64, 2, L])
        y = m.sb("y", [L, 2, D])
        c0_ready, cT_ps, cT_ready, h_ps = m.sem("c0_ready"), m.sem("cT_ps"), m.sem("cT_ready"), m.sem("h_ps")
        h_ready, y_ps, y_ready, added = m.sem("h_ready"), m.sem("y_ps"), m.sem("y_ready"), m.sem("added")
        block = stack.enter_context(nc.Block())

        @block.tensor
        def _(pe):
            with pe.Fori(0, B // 2) as i:
                for j in range(2):
                    pe.wait_ge(c0_ready, 2 * i + j + 1)
                    pe.transpose(ps[:, j, 0, 0:L], c0[:, j, :], ident[0:L, 0:L]).then_inc(cT_ps, 1)
                for j in range(2):
                    pe.wait_ge(cT_ready, 2 * i + j + 1)
                    pe.matmul(ps[0:64, j, 1, 0:L], w.at("g1"), cT[:, j, :], start=True, stop=True).then_inc(h_ps, 1)
                for j in range(2):
                    pe.wait_ge(h_ready, 2 * i + j + 1)
                    pe.matmul(ps[0:L, j, 2, 0:D], hT[:, j, :], w.at("g2"), start=True, stop=True).then_inc(y_ps, 1)

        @block.scalar
        def _(act):
            with act.Fori(0, B // 2) as i:
                for j in range(2):
                    act.wait_ge(cT_ps, 2 * i + j + 1)
                    act.activation(cT[:, j, :], ps[:, j, 0, 0:L], ACT.Copy).then_inc(cT_ready, 1)
                for j in range(2):
                    act.wait_ge(h_ps, 2 * i + j + 1)
                    act.activation(hT[:, j, :], ps[0:64, j, 1, 0:L], ACT.Gelu_apprx_tanh, bias=w.at("g1b"))\
                       .then_inc(h_ready, 1)

        @block.gpsimd
        def _(pool):
            with pool.Fori(0, B // 2) as i:
                for j in range(2):
                    if j == 0:
                        pool.wait_ge(y_ready, 2 * i + 1)
                    else:
                        pool.wait_ge(y_ready, 2 * i + 2)
                    pool.tensor_copy(c0[:, j:j + 1, :], comb[:, ds(2 * i + j, 1), :]).then_inc(c0_ready, 1)

        @block.vector
        def _(dve):
            dve.sem_inc(y_ready, 2)
            with dve.Fori(0, B // 2) as i:
                for j in range(2):
                    dve.wait_ge(y_ps, 2 * i + j + 1)
                    dve.tensor_tensor(y[:, j, :], ps[0:L, j, 2, 0:D], w.at("g2b"), ALU.add).then_inc(y_ready, 1)
                for j in range(2):
                    tile = ds(2 * i + j, 1)
                    dve.wait_ge(y_ready, 2 + 2 * i + j + 1)
                    dve.tensor_tensor(h[:, tile, :], h[:, tile, :], y[:, j:j + 1, :], ALU.add).then_inc(added, 1)
                dve.wait_ge(added, 2 * i + 2)


def sub_feed_forward(nc, g, dram):
    with ExitStack() as stack:
        sub = {"zT": stack.enter_context(nc.sbuf_tensor("sub_zT", [128, B, L], F32)),
               "gates": stack.enter_context(nc.sbuf_tensor("sub_gates", [L, B, NS * NM], F32)),
               "comb": stack.enter_context(nc.sbuf_tensor("sub_comb", [L, B, 128], F32))}
        sub_gates(nc, g, sub)
        sub_experts(nc, g, dram, sub)
        sub_output(nc, g, sub)


def normalise(nc, g):
    ident = g["const"].at("ident")
    ps, h, x, xT_all = g["ps"], g["h"], g["x"], g["xT"]
    with ExitStack() as stack:
        m = Memory(nc, g, stack, "l3n")
        norm = Norm(m, g, "norm")
        z = m.sb("z", [L, 2, D])
        dve_steps = m.sem("dve_steps")
        z_ready, z_kept, xT_ps, xT_ready = m.sem("z_ready"), m.sem("z_kept"), m.sem("xT_ps"), m.sem("xT_ready")
        block = stack.enter_context(nc.Block())

        @block.tensor
        def _(pe):
            with pe.Fori(0, B // 2) as i:
                for j in range(2):
                    pe.wait_ge(z_ready, 2 * i + j + 1)
                    pe.wait_ge(xT_ready, 2 * i + j + 1)
                    for c in range(C):
                        last = pe.transpose(ps[0:K, j, 3, c * L:(c + 1) * L], z[:, j, c * K:(c + 1) * K],
                                            ident[0:L, 0:L])
                    last.then_inc(xT_ps, 1)

        @block.scalar
        def _(act):
            act.sem_inc(xT_ready, 2)
            with act.Fori(0, B // 2) as i:
                for j in range(2):
                    act.wait_ge(xT_ps, 2 * i + j + 1)
                    act.activation(xT_all[:, :, ds(2 * i + j, 1), :],
                                   ps[0:K, j, 3, 0:C * L].rearrange("p (c a n) -> p c a n", c=C, a=1),
                                   ACT.Copy).then_inc(xT_ready, 1)

        @block.gpsimd
        def _(pool):
            with pool.Fori(0, B // 2) as i:
                norm.pool(pool, i)
                for j in range(2):
                    pool.wait_ge(z_ready, 2 * i + j + 1)
                    pool.tensor_copy(x[:, ds(2 * i + j, 1), :], z[:, j:j + 1, :]).then_inc(z_kept, 1)

        @block.vector
        def _(dve):
            with dve.Fori(0, B // 2) as i:
                steps = Steps(dve, dve_steps, 4 * i)
                for ins in norm.vector(dve, i, steps, [h[:, ds(2 * i + j, 1), :] for j in range(2)],
                                       [z[:, j:j + 1, :] for j in range(2)]):
                    ins.then_inc(z_ready, 1)
                dve.wait_ge(z_kept, 2 * i + 2)
                dve.wait_ge(xT_ps, 2 * i + 2)


def choose(nc, g, dram, chosen, xln, out):
    w = g["l3f"]
    ident = g["const"].at("ident")
    ps, h, xT_all = g["ps"], g["h"], g["xT"]
    with ExitStack() as stack:
        m = Memory(nc, g, stack, "l3c")
        score = m.sb("score", [E3, T])
        value = m.sb("value", [E3, ROUNDS * 8])
        place = m.sb("place", [E3, ROUNDS * 8], U32)
        placef = m.sb("placef", [E3, ROUNDS * 8])
        act_gate = m.sb("act_gate", [128, 2, SM, NG])
        act_up = m.sb("act_up", [128, 2, SM, NG])
        hidden = m.sb("hidden", [128, 2, SM, NG])
        y = m.sb("y", [L, B, D])
        x_stored, out_stored = m.sem("x_stored"), m.sem("out_stored")
        score_ps, score_ready, rounds, placef_ready = m.sem("score_ps"), m.sem("score_ready"), m.sem("rounds"), m.sem("placef_ready")
        list_ps = m.sem("list_ps")
        gu_ps, gu_ready, hidden_ready, y_ps, y_ready, h_ready = (
            m.sem("gu_ps"), m.sem("gu_ready"), m.sem("hidden_ready"), m.sem("y_ps"), m.sem("y_ready"), m.sem("h_ready"))
        block = stack.enter_context(nc.Block())

        @block.sync
        def _(sp):
            sp.dma_start(xln.rearrange("(b t) d -> t b d", b=B), g["x"][:, :, :]).then_inc(x_stored, 16)
            sp.wait_ge(h_ready, G)
            sp.dma_start(out.rearrange("b t d -> t b d"), h[:, :, :]).then_inc(out_stored, 16)
            sp.wait_ge(x_stored, 16)
            sp.wait_ge(out_stored, 16)

        @block.tensor
        def _(pe):
            for q in range(G):
                for c in range(C):
                    last = pe.matmul(ps[0:E3, 0, q, 0:NG], w.at("choose", C)[:, c, :],
                                     xT_all[:, c, q * GB:(q + 1) * GB, :], start=(c == 0), stop=(c == C - 1))
                last.then_inc(score_ps, 1)
            for q in range(G):
                for t in range(SM):
                    n = q * SM + t
                    if n < 2:
                        pe.wait_ge(score_ready, 2 * n + 2)
                    else:
                        pe.wait_ge(gu_ready, n - 1)
                    for u, name in ((0, "ws_g"), (1, "ws_u")):
                        for c in range(C):
                            last = pe.matmul(ps[:, 0, 2 * (n % 2) + u, 0:NG],
                                             w.at(name, C)[:, c, t * 128:(t + 1) * 128],
                                             xT_all[:, c, q * GB:(q + 1) * GB, :], start=(c == 0), stop=(c == C - 1))
                    last.then_inc(gu_ps, 1)
                pe.wait_ge(hidden_ready, (q + 1) * SM)
                if q:
                    pe.wait_ge(y_ready, q)
                for b in range(GB):
                    for t in range(SM):
                        last = pe.matmul(ps[0:L, 1, b, 0:D], hidden[:, q % 2, t, b * L:(b + 1) * L],
                                         w.at("ws_d", SM)[:, t, :], start=(t == 0), stop=(t == SM - 1))
                last.then_inc(y_ps, 1)
            pe.wait_ge(placef_ready, 1)
            pe.wait_ge(gu_ready, G * SM)
            for half in range(2):
                for n, src in ((0, placef), (1, value)):
                    last = pe.transpose(ps[0:L, 0, n, half * E3:(half + 1) * E3],
                                        src[:, half * L:(half + 1) * L], ident[0:E3, 0:E3])
            last.then_inc(list_ps, 1)

        @block.scalar
        def _(act):
            for q in range(G):
                act.wait_ge(score_ps, q + 1)
                act.activation(score[:, q * NG:(q + 1) * NG], ps[0:E3, 0, q, 0:NG], ACT.Sigmoid)\
                   .then_inc(score_ready, 1)
            for q in range(G):
                for t in range(SM):
                    n = q * SM + t
                    act.wait_ge(gu_ps, n + 1)
                    if q >= 2:
                        act.wait_ge(hidden_ready, (q - 1) * SM)
                    act.activation(act_gate[:, q % 2, t, :], ps[:, 0, 2 * (n % 2), 0:NG], ACT.Silu)
                    act.activation(act_up[:, q % 2, t, :], ps[:, 0, 2 * (n % 2) + 1, 0:NG], ACT.Copy)\
                       .then_inc(gu_ready, 1)
                act.wait_ge(y_ps, q + 1)
                act.activation(y[:, q * GB:(q + 1) * GB, :], ps[0:L, 1, :, 0:D], ACT.Copy).then_inc(y_ready, 1)

        @block.gpsimd
        def _(pool):
            for q in range(G):
                for t in range(SM):
                    pool.wait_ge(gu_ready, q * SM + t + 1)
                    if q >= 2:
                        pool.wait_ge(y_ps, q - 1)
                    pool.tensor_tensor(hidden[:, q % 2, t, :], act_gate[:, q % 2, t, :], act_up[:, q % 2, t, :],
                                       ALU.mult).then_inc(hidden_ready, 1)
                pool.wait_ge(y_ready, q + 1)
                pool.tensor_tensor(h[:, q * GB:(q + 1) * GB, :], h[:, q * GB:(q + 1) * GB, :],
                                   y[:, q * GB:(q + 1) * GB, :], ALU.add).then_inc(h_ready, 1)

        @block.vector
        def _(dve):
            dve.wait_ge(score_ready, G)
            for n in range(ROUNDS):
                eight = slice(n * 8, n * 8 + 8)
                if n:
                    dve.wait_ge(rounds, 2 * n)
                dve.max(value[:, eight], score[:, :]).then_inc(rounds, 1)
                dve.wait_ge(rounds, 2 * n + 1)
                dve.max_index(place[:, eight], value[:, eight], score[:, :])
                if n < ROUNDS - 1:
                    dve.match_replace(score[:, :], value[:, eight], score[:, :], -1.0).then_inc(rounds, 1)
                else:
                    dve.memset(chosen["pause"][:, :], 0.0).then_inc(rounds, 1)
            dve.drain()
            dve.tensor_copy(placef[:, :], place[:, :]).then_inc(placef_ready, 1)
            dve.wait_ge(list_ps, 1)
            dve.tensor_copy(chosen["place"][:, :, :], ps[0:L, 0, 0, 0:2 * E3].rearrange("p (a e) -> p a e", a=2))
            dve.tensor_copy(chosen["score"][:, :, :], ps[0:L, 0, 1, 0:2 * E3].rearrange("p (a e) -> p a e", a=2))


def chosen_experts(nc, g, dram, chosen, xln, out):
    ident = g["const"].at("ident")
    ps = g["ps"]
    table = out.rearrange("b t d -> (b t) d")
    with ExitStack() as stack:
        m = Memory(nc, g, stack, "l3e")
        wg = m.sb("wg", [K, 2, C, F])
        wu = m.sb("wu", [K, 2, C, F])
        wd = m.sb("wd", [128, 2, FM, D])
        rows_of = [[m.sb(f"rows{j}{a}", [L, 1], U32) for a in range(2)] for j in range(2)]
        xg = [[m.sb(f"xg{j}{a}", [L, D]) for a in range(2)] for j in range(2)]
        xgT = m.sb("xgT", [K, 2, C, 2, L])
        pause = m.sb("pause", [1, 6])
        held = m.sem("held")
        act_gate = m.sb("act_gate", [128, 2, FM, 2 * L])
        hidden = m.sb("hidden", [128, 2, FM, 2, L])
        y = [[m.sb(f"y{j}{a}", [L, D]) for a in range(2)] for j in range(2)]
        loaded = [m.sem(f"loaded{j}") for j in range(2)]
        rows_ready, gathered, xgT_ps, xgT_ready = m.sem("rows_ready"), [m.sem(f"gathered{j}") for j in range(2)], m.sem("xgT_ps"), m.sem("xgT_ready")
        hid_ps, gate_ready, hid_ready, y_ps, y_ready, added = (
            m.sem("hid_ps"), m.sem("gate_ready"), m.sem("hid_ready"), m.sem("y_ps"), m.sem("y_ready"), m.sem("added"))
        block = stack.enter_context(nc.Block())

        @block.sync
        def _(sp):
            def load(e, j):
                for dst, name in ((wg, "l3_gate"), (wu, "l3_up"), (wd, "l3_down")):
                    sp.dma_start(dst[:, j, :, :], dram[name][e].rearrange("e p (c n) -> p (e c) n", n=dst.shape[3]))\
                      .then_inc(loaded[j], 16)
            for j in range(2):
                load(slice(j, j + 1), j)
            with sp.Fori(1, E3 // 2) as i:
                for j in range(2):
                    sp.wait_ge(y_ps, 2 * i + j - 1)
                    load(ds(2 * i + j, 1), j)

        @block.gpsimd
        def _(pool):
            neg = g["const"].at("neg_half")

            def hold(n):
                pool.tensor_tensor(pause[:, n:n + 1], neg[0:1, 0:1], neg[0:1, 1:2], ALU.mult).then_inc(held, 1)

            def gather(j):
                hold(j)
                for a in range(2):
                    pool.indirect_dma_start(xg[j][a][:, :], None, xln,
                                            bass.IndirectOffsetOnAxis(ap=rows_of[j][a][:, :], axis=0))\
                        .then_inc(gathered[j], 16)

            with pool.Fori(0, E3 // 2) as i:
                for j in range(2):
                    pool.wait_ge(rows_ready, 2 * i + j + 1)
                    gather(j)
                for j in range(2):
                    pool.wait_ge(y_ready, 2 * i + j + 1)
                    for a in range(2):
                        hold(2 + 2 * j + a)
                        pool.indirect_dma_start(table, bass.IndirectOffsetOnAxis(ap=rows_of[j][a][:, :], axis=0),
                                                y[j][a][:, :], None, compute_op=ALU.add).then_inc(added, 16)
                        pool.wait_ge(added, 16 * (2 * (2 * i + j) + a + 1))
                pool.wait_ge(held, 6 * (i + 1))

        @block.tensor
        def _(pe):
            with pe.Fori(0, E3 // 2) as i:
                for j in range(2):
                    pe.wait_ge(gathered[j], 32 * (i + 1))
                    for a in range(2):
                        for c in range(C):
                            last = pe.transpose(ps[0:K, j, 3, (c * 2 + a) * L:(c * 2 + a + 1) * L],
                                                xg[j][a][:, c * K:(c + 1) * K], ident[0:L, 0:L])
                    last.then_inc(xgT_ps, 1)
                for j in range(2):
                    pe.wait_ge(xgT_ready, 2 * i + j + 1)
                    pe.wait_ge(loaded[j], 48 * (i + 1))
                    for t in range(FM):
                        n = FM * (2 * i + j) + t
                        pe.wait_ge(hid_ready, n + 1)
                        for u, wt in ((0, wg), (1, wu)):
                            for c in range(C):
                                last = pe.matmul(ps[:, j, t % 3, u * 2 * L:(u + 1) * 2 * L],
                                                 wt[:, j, c, t * 128:(t + 1) * 128],
                                                 xgT[:, j, c, :, :], start=(c == 0), stop=(c == C - 1))
                        last.then_inc(hid_ps, 1)
                for j in range(2):
                    pe.wait_ge(hid_ready, 3 + FM * (2 * i + j + 1))
                    for a in range(2):
                        for t in range(FM):
                            last = pe.matmul(ps[0:L, j, 3, a * D:(a + 1) * D], hidden[:, j, t, a, :],
                                             wd[:, j, t, :], start=(t == 0), stop=(t == FM - 1))
                    last.then_inc(y_ps, 1)

        @block.scalar
        def _(act):
            with act.Fori(0, E3 // 2) as i:
                for j in range(2):
                    act.wait_ge(xgT_ps, 2 * i + j + 1)
                    act.activation(xgT[:, j, :, :, :].rearrange("p c a n -> p (c a n)"), ps[0:K, j, 3, 0:4 * L],
                                   ACT.Copy).then_inc(xgT_ready, 1)
                for j in range(2):
                    for t in range(FM):
                        n = FM * (2 * i + j) + t
                        act.wait_ge(hid_ps, n + 1)
                        act.activation(act_gate[:, j, t, :], ps[:, j, t % 3, 0:2 * L], ACT.Silu)\
                           .then_inc(gate_ready, 1)

        @block.vector
        def _(dve):
            dve.sem_inc(hid_ready, 3)
            with dve.Fori(0, E3 // 2) as i:
                for j in range(2):
                    for a in range(2):
                        last = dve.tensor_copy(rows_of[j][a][:, :], chosen["place"][:, a, ds(2 * i + j, 1)])
                    last.then_inc(rows_ready, 1)
                for j in range(2):
                    for t in range(FM):
                        n = FM * (2 * i + j) + t
                        dve.wait_ge(gate_ready, n + 1)
                        dve.tensor_tensor(hidden[:, j, t, :, :].rearrange("p a n -> p (a n)"), act_gate[:, j, t, :],
                                          ps[:, j, t % 3, 2 * L:4 * L], ALU.mult).then_inc(hid_ready, 1)
                for j in range(2):
                    dve.wait_ge(y_ps, 2 * i + j + 1)
                    for a in range(2):
                        last = dve.tensor_scalar(y[j][a][:, :], ps[0:L, j, 3, a * D:(a + 1) * D],
                                                 chosen["score"][:, a, ds(2 * i + j, 1)], None, ALU.mult)
                    last.then_inc(y_ready, 1)
                dve.wait_ge(added, 64 * (i + 1))


def chosen_feed_forward(nc, g, dram, out):
    xln = nc.dram_tensor("xln", [T, D], F32).ap()
    with ExitStack() as stack:
        chosen = {"place": stack.enter_context(nc.sbuf_tensor("chosen_place", [L, 2, E3], U32)),
                  "score": stack.enter_context(nc.sbuf_tensor("chosen_score", [L, 2, E3], F32)),
                  "pause": stack.enter_context(nc.sbuf_tensor("chosen_pause", [1, 1], F32))}
        normalise(nc, g)
        choose(nc, g, dram, chosen, xln, out)
        chosen_experts(nc, g, dram, chosen, xln, out)


def store(nc, g, out):
    with ExitStack() as stack:
        m = Memory(nc, g, stack, "out")
        stored = m.sem("stored")
        block = stack.enter_context(nc.Block())

        @block.sync
        def _(sp):
            sp.dma_start(out.rearrange("b t d -> t b d"), g["h"][:, :, :]).then_inc(stored, 16)
            sp.wait_ge(stored, 16)


def build(nc, dram, out):
    with ExitStack() as stack:
        g = {"h": stack.enter_context(nc.sbuf_tensor("h", [L, B, D], F32)),
             "x": stack.enter_context(nc.sbuf_tensor("x", [L, B, D], F32)),
             "xT": stack.enter_context(nc.sbuf_tensor("xT", [K, C, B, L], F32)),
             "gates": stack.enter_context(nc.sbuf_tensor("gates", [L, B, 16], F32)),
             "ps": stack.enter_context(nc.psum_tensor("ps", [128, 2, 4, 512], F32)),
             "packs_loaded": stack.enter_context(nc.semaphore("packs_loaded"))}
        first = min(nc.free_semaphores)
        g["sem_banks"] = [range(first + n * SEM_BANK, first + (n + 1) * SEM_BANK) for n in range(2)]
        g["phases"] = 0
        for name in PACKS:
            if name != "tok":
                g["pack_" + name] = stack.enter_context(
                    nc.sbuf_tensor("pack_" + name, [128, offsets(name)[1]], F32))
                g[name] = Fields(g["pack_" + name], name)
        embed(nc, g, dram)
        layers = [lambda: retention(nc, g),
                  lambda: (softmax_attention(nc, g, "l0f", "normed"), route(nc, g, "l0r", False),
                           experts(nc, g, dram, "l0", ACT.Gelu)),
                  lambda: softmax_attention(nc, g, "l1a", "both", conv=True, project=False),
                  lambda: (route(nc, g, "l1r", True), experts(nc, g, dram, "l1", ACT.Silu)),
                  lambda: softmax_attention(nc, g, "l2a", "gated", mask="band"),
                  lambda: sub_feed_forward(nc, g, dram),
                  lambda: softmax_attention(nc, g, "l3a", "plain", mask="causal"),
                  lambda: chosen_feed_forward(nc, g, dram, out)]
        for n, layer in enumerate(layers):
            if (str(n + 1) in str(STAGES // 10) if STAGES % 10 == 0 else STAGES > n):
                layer()
        if STAGES < 8 or STAGES % 10 == 0 and STAGES != 80:
            store(nc, g, out)



def lay_rows(w):
    n = w.shape[1]
    return w.reshape(C, K, n).transpose(1, 0, 2).reshape(K, C * n)


def kernel(**inputs):
    import numpy as np
    import concourse.bacc as bacc
    from concourse.bass_utils import run_bass_kernel_spmd

    a = {k: np.asarray(v) for k, v in inputs.items()}
    f32 = np.float32

    def heads(w, twice=False):
        p = np.zeros((w.shape[0], HT, RG, HP), f32)
        s = w.reshape(w.shape[0], RG, HT, HD).transpose(0, 2, 1, 3)
        p[:, :, :, :HD] = s
        if twice:
            p[:, :, :, HD:] = s
        return p.reshape(w.shape[0], HT * 128)

    def head_bias(b, twice=False):
        return heads(b.reshape(1, D), twice).reshape(HT, 128).T

    def rows(b, n=L):
        return np.broadcast_to(b, (n, b.shape[0]))

    def col(b):
        return b.reshape(C, K).T

    side, nb = 32, 84 // 16
    edges = np.arange(1.0 / side, 1.0, 1.0 / side, dtype=f32)
    frac = np.arange(0.0, 1.0 - 1e-6, 1.0 / nb, dtype=f32)
    bins = np.searchsorted(edges, frac, side="right")
    pos = a["L0_tok_pos_table"][(bins[:, None] * side + bins).reshape(-1)]
    px = a["x"][:, :, :80, :80].reshape(B, 3, nb, 16, nb, 16).transpose(1, 3, 5, 0, 2, 4).reshape(CONV_K, 128, B * NP)
    conv_w = a["L0_tok_conv_w"].reshape(D, CONV_K, 128).transpose(2, 1, 0)
    steps = np.arange(L)
    ahead = steps[None, :] - steps[:, None]
    decay = np.where(ahead >= 0, f32(0.99) ** ahead.astype(f32), 0.0) / f32(np.sqrt(f32(D)))
    wqkv0 = a["L0_attn_W_qkv"].T
    b0 = a["L0_attn_b_qkv"]
    wqf, bqf = a["L0_ffn_qkv_w"], a["L0_ffn_qkv_b"]
    fields = {
        "tok": {"conv_w": conv_w.reshape(128, -1), "patches": px.transpose(1, 0, 2).reshape(128, -1),
                "pos": np.tile(pos, (GB, 1)), "conv_b": rows(a["L0_tok_conv_b"], GB * NP)},
        "const": {"ident": np.eye(128, dtype=f32), "neg_half": np.full((L, 2), -0.5, f32), "iota": rows(np.arange(64, dtype=f32))},
        "l0a": {"wq": lay_rows(wqkv0[:, :D]), "wk": lay_rows(wqkv0[:, D:2 * D]), "wv": lay_rows(wqkv0[:, 2 * D:]),
                "bq": col(b0[:D]), "bk": col(b0[D:2 * D]), "bv": rows(b0[2 * D:]), "decay": decay},
        "l0f": {"wq": lay_rows(heads(wqf[:, :D])), "wk": lay_rows(heads(wqf[:, D:2 * D])),
                "wv": lay_rows(wqf[:, 2 * D:]), "bq": head_bias(bqf[:D]), "bk": head_bias(bqf[D:2 * D]),
                "bv": rows(bqf[2 * D:]), "g": col(a["L0_ffn_ln1_g"]), "b": col(a["L0_ffn_ln1_b"]),
                "wo": lay_rows(a["L0_ffn_proj_w"]), "bo": rows(a["L0_ffn_proj_b"])},
    }
    w1a, b1a = a["L1_attn_qkv_w"].T, a["L1_attn_qkv_b"]
    half = np.arange(128) % HP < HD
    mix = np.stack([np.ones(128), 1.0 - half, np.where(half, 1.2, -0.2), np.where(half, 0.0, -0.2)], 1)
    fields["l1a"] = {"wq": lay_rows(heads(w1a[:, :D], True)), "wk": lay_rows(heads(w1a[:, D:2 * D], True)),
                     "wv": lay_rows(w1a[:, 2 * D:]), "bq": head_bias(b1a[:D], True),
                     "bk": head_bias(b1a[D:2 * D], True), "bv": rows(b1a[2 * D:]), "g": col(a["L1_attn_ln_g"]),
                     "b": col(a["L1_attn_ln_b"]), "mix": mix.astype(f32)}
    fields["l0r"] = {"g": col(a["L0_ffn_ln2_g"]), "b": col(a["L0_ffn_ln2_b"]), "gate": lay_rows(a["L0_ffn_gate_w"]),
                     "b2": a["L0_ffn_b2"]}
    fields["l1r"] = {"g": col(a["L1_ffn_ln_gamma"]), "b": col(a["L1_ffn_ln_beta"]),
                     "gate": lay_rows(a["L1_ffn_router_w"])}

    def up(w):
        return w.reshape(-1, C, K, F).transpose(0, 2, 1, 3).reshape(-1, K, C * F)

    def down(w):
        return w.reshape(-1, FM, 128, D).transpose(0, 2, 1, 3).reshape(-1, 128, FM * D)

    w2 = {n: a["L2_attn_W_" + n] for n in ("q_lin", "k_lin", "v_lin", "q_loc", "k_loc", "v_loc", "out", "g1", "g2")}
    b2 = {n: a["L2_attn_b_" + n] for n in w2}
    apart = np.abs(ahead)
    fields["l2a"] = {"wq": lay_rows(heads(w2["q_loc"])), "wk": lay_rows(heads(w2["k_loc"])),
                     "wv": lay_rows(w2["v_loc"]), "bq": head_bias(b2["q_loc"]), "bk": head_bias(b2["k_loc"]),
                     "bv": rows(b2["v_loc"]), "g": col(a["L2_attn_gamma1"]), "b": col(a["L2_attn_beta1"]),
                     "band": np.where(apart <= 32, 0.0, NEG).astype(f32), "lin_wq": lay_rows(w2["q_lin"]),
                     "lin_wk": lay_rows(w2["k_lin"]), "lin_wv": lay_rows(w2["v_lin"]), "lin_bq": col(b2["q_lin"]),
                     "lin_bk": col(b2["k_lin"]), "lin_bv": rows(b2["v_lin"]),
                     "wg1": w2["g1"].reshape(3 * C, K, D).transpose(1, 0, 2).reshape(K, -1), "bg1": col(b2["g1"]),
                     "wg2": lay_rows(w2["g2"]), "bg2": rows(b2["g2"]), "wo": lay_rows(w2["out"]),
                     "bo": rows(b2["out"])}
    def blocks(w):
        return np.moveaxis(w.reshape(RG, 2, 8, 8, *w.shape[2:]), 0, 2)

    w1s = blocks(a["L2_ffn_W1"]).reshape(2, 8, RG, 2, 4, NR, 32)
    sub_up = np.zeros((2, 8, RG, 2, NR, 2, 4, 32), f32)
    for half in range(2):
        sub_up[half, :, :, half] = w1s[half].transpose(0, 1, 4, 2, 3, 5)
    w2s = blocks(a["L2_ffn_W2"]).reshape(2, 8, RG, 2, 4, 32, NR)
    sub_down = np.zeros((2, 8, 4, 32, RG, 2, 4, NR), f32)
    for m in range(4):
        sub_down[:, :, m, :, :, :, m] = w2s[:, :, :, :, m].transpose(0, 1, 4, 2, 3, 5)
    sub_b1 = blocks(a["L2_ffn_b1"]).reshape(NV, VT, 128).transpose(0, 2, 1)
    centres = np.zeros((NS, NR, NS, NM), f32)
    for n in range(NS):
        centres[n, :, n] = a["L2_ffn_C"][n].T
    b2s = np.zeros((2, 8, RG, 8, 2, RG, NR), f32)
    b2b = blocks(a["L2_ffn_b2"])
    for half in range(2):
        for n in range(RG):
            b2s[half, :, n, :, half, n] = b2b[half, :, n]
    fields["l2f"] = {"p": lay_rows(a["L2_ffn_P"].transpose(1, 0, 2).reshape(D, 128)),
                     "centres": centres.reshape(128, -1),
                     "b2": b2s.reshape(4, 128, 128).transpose(1, 0, 2),
                     "g1": a["L2_ffn_G1"].reshape(RG, 2, NR, 64).transpose(1, 0, 2, 3).reshape(128, 64),
                     "g1b": a["L2_ffn_g1b"][:, None], "g2": a["L2_ffn_G2"], "g2b": rows(a["L2_ffn_g2b"])}
    fields["l3f"] = {"choose": lay_rows(a["L3_ffn_gate_weight"].T), "ws_g": lay_rows(a["L3_ffn_Ws_g"].T),
                     "ws_u": lay_rows(a["L3_ffn_Ws_u"].T),
                     "ws_d": a["L3_ffn_Ws_d"].T.reshape(SM, 128, D).transpose(1, 0, 2)}
    w3 = a["L3_attn_w_attn"]
    fields["l3a"] = {"wq": lay_rows(heads(w3[:, :D])), "wk": lay_rows(heads(w3[:, D:2 * D])),
                     "wv": lay_rows(w3[:, 2 * D:]), "causal": np.where(ahead <= 0, 0.0, NEG).astype(f32),
                     "wo": lay_rows(a["L3_attn_w_proj"]), "bo": rows(a["L3_attn_b_proj"])}

    arrays = {"txt": a["txt"], "l3_gate": up(a["L3_ffn_Wg"].transpose(0, 2, 1)),
              "l3_up": up(a["L3_ffn_Wu"].transpose(0, 2, 1)), "l3_down": down(a["L3_ffn_Wd"].transpose(0, 2, 1)),
              "sub_up": sub_up.reshape(NV, 128, 256), "sub_down": sub_down.reshape(NV, 128, VT * 64),
              "sub_b1": sub_b1,
              "l0_up": up(a["L0_ffn_w1"]), "l0_down": down(a["L0_ffn_w2"]),
              "l0_b1": a["L0_ffn_b1"].reshape(E01, FM, 128).transpose(0, 2, 1),
              "l1_up": up(a["L1_ffn_w1"]), "l1_down": down(a["L1_ffn_w2"])}
    for pack in PACKS:
        where, width = offsets(pack)
        arr = np.zeros((128, width), f32)
        for name, (n, start, cols) in where.items():
            arr[:n, start:start + cols] = fields[pack][name].reshape(n, cols)
        arrays["pack_" + pack] = arr

    nc = bacc.Bacc("TRN2", target_bir_lowering=False, num_devices=1)
    feed, dram = {}, {}
    for name, arr in arrays.items():
        feed["in_" + name] = np.ascontiguousarray(arr)
        dram[name] = nc.dram_tensor("in_" + name, arr.shape, mybir.dt.from_np(arr.dtype), kind="ExternalInput").ap()
    out = nc.dram_tensor("out", (B, L, D), F32, kind="ExternalOutput").ap()
    build(nc, dram, out)
    r = run_bass_kernel_spmd(nc, [feed], core_ids=[0])
    return r.results[0]["out"]
```

```python
from contextlib import ExitStack

import concourse.bass as bass
from concourse import mybir

B = 16
L = 102
NP = 25
D = 192
C = 2
K = D // C
H = 12
HD = D // H
RG = 4
HT = H // RG
HP = 32
T = B * L
CONV_K = 6
GB = 4
G = B // GB
NG = GB * L
EPS = 1e-5
E01 = 8
F = 768
FM = F // 128
NS = 8
NR = 16
NM = 64
KEEP = 4
MT = NM // 4
PAIRS = ((1, 1), (1, 2), (2, 1), (2, 2), (1, 3), (3, 1), (2, 3), (3, 2))
HALF = B // 2
E3 = 16
CAP = T * 2 // E3
ROUNDS = -(-CAP // 8)
FS = F * 2 // 4
SM = FS // 128
NEG = -1e30

F32 = mybir.dt.float32
BF16 = mybir.dt.bfloat16
U32 = mybir.dt.uint32
ALU = mybir.AluOpType
ACT = mybir.ActivationFunctionType
AX = mybir.AxisListType
ds = bass.ds

PACKS = {
    "tok": [("conv_w", 128, CONV_K * D), ("patches", 128, CONV_K * B * NP), ("pos", GB * NP, D), ("conv_b", GB * NP, D)],
    "const": [("ident", 128, 128), ("neg_half", L, 2), ("iota", L, 64)],
    "l0a": [("wq", K, C * D), ("wk", K, C * D), ("wv", K, C * D), ("bq", K, C), ("bk", K, C), ("bv", L, D),
            ("decay", L, L)],
    "l2a": [("wq", K, C * HT * 128), ("wk", K, C * HT * 128), ("wv", K, C * D), ("bq", 128, HT), ("bk", 128, HT),
            ("bv", L, D), ("g", K, C), ("b", K, C), ("band", L, L), ("lin_wq", K, C * D), ("lin_wk", K, C * D),
            ("lin_wv", K, C * D), ("lin_bq", K, C), ("lin_bk", K, C), ("lin_bv", L, D), ("wg1", K, 3 * C * D),
            ("bg1", K, C), ("wg2", K, C * D), ("bg2", L, D), ("wo", K, C * D), ("bo", L, D)],
    "l2f": [("p", K, C * 128), ("p8", K, C * NS * 128), ("centres", 128, NS * NM), ("b2", 128, 4 * 2 * 32),
            ("parts", 128, 4), ("b1", 128, NS * MT), ("g1", 128, 2 * 64), ("g1b", 64, 1), ("g2", 64, D), ("g2b", L, D)],
    "l3f": [("choose", K, C * E3), ("ws_g", K, C * FS), ("ws_u", K, C * FS), ("ws_d", 128, SM * D)],
    "l3a": [("wq", K, C * HT * 128), ("wk", K, C * HT * 128), ("wv", K, C * D), ("causal", L, L),
            ("wo", K, C * D), ("bo", L, D)],
    "l0r": [("g", K, C), ("b", K, C), ("gate", K, C * E01), ("b2", E01, D)],
    "l1r": [("g", K, C), ("b", K, C), ("gate", K, C * E01)],
    "l1a": [("wq", K, C * HT * 128), ("wk", K, C * HT * 128), ("wv", K, C * D), ("bq", 128, HT), ("bk", 128, HT),
            ("bv", L, D), ("g", K, C), ("b", K, C), ("mix", 128, 4)],
    "l0f": [("wq", K, C * HT * 128), ("wk", K, C * HT * 128), ("wv", K, C * D), ("bq", 128, HT), ("bk", 128, HT),
            ("bv", L, D), ("g", K, C), ("b", K, C), ("wo", K, C * D), ("bo", L, D)],
}


def offsets(pack):
    at, where = 0, {}
    for name, rows, cols in PACKS[pack]:
        where[name] = (rows, at, cols)
        at += cols
    return where, at


class Fields:

    def __init__(self, tile, pack):
        self.tile, self.where = tile, offsets(pack)[0]

    def at(self, name, groups=1):
        rows, start, cols = self.where[name]
        view = self.tile[0:rows, start:start + cols]
        return view if groups == 1 else view.rearrange("p (a n) -> p a n", a=groups)


class Steps:

    def __init__(self, eng, sem, before=0):
        self.eng, self.sem, self.before, self.n = eng, sem, before, 0

    def done(self, ins):
        ins.then_inc(self.sem, 1)
        self.n += 1

    def wait(self):
        self.eng.wait_ge(self.sem, self.before + self.n)


SEM_BANK = 72


class Memory:

    def __init__(self, nc, g, stack, phase):
        self.nc, self.stack, self.phase = nc, stack, phase
        self.bank = g["sem_banks"][g["phases"] % 2]
        g["phases"] += 1
        self.used = []
        stack.callback(self.retire)

    def retire(self):
        for sem in self.used:
            self.nc.release_semaphore(sem)
        if self.used:
            self.nc.sync.sem_clear(range(self.bank[0], self.bank[0] + len(self.used)))

    def sb(self, name, shape, dt=F32):
        return self.stack.enter_context(self.nc.sbuf_tensor(f"{self.phase}_{name}", shape, dt))

    def sem(self, name):
        handle = self.nc.alloc_semaphore(f"{self.phase}_{name}", self.bank[len(self.used)])
        self.used.append(handle)
        return handle


def embed(nc, g, dram):
    with ExitStack() as stack:
        m = Memory(nc, g, stack, "tok")
        width = offsets("tok")[1]
        pack = m.sb("pack", [128, width])
        f = Fields(pack, "tok")
        emb = m.sb("emb", [GB * NP, G, D])
        bias = m.sb("bias", [GB * NP, D])
        loaded, txt_loaded, moved = m.sem("loaded"), m.sem("txt_loaded"), m.sem("moved")
        bias_ready, emb_ps, emb_ready = m.sem("bias_ready"), m.sem("emb_ps"), m.sem("emb_ready")
        w = f.at("conv_w", CONV_K)
        x = f.at("patches", CONV_K)
        ps = g["ps"]

        block = stack.enter_context(nc.Block())

        @block.sync
        def _(sp):
            sp.dma_start(pack[:, :], dram["pack_tok"]).then_inc(loaded, 16)
            sp.dma_start(g["h"][NP:L, :, :], dram["txt"].rearrange("b t d -> t b d")).then_inc(txt_loaded, 16)
            for name in PACKS:
                if name != "tok":
                    sp.dma_start(g["pack_" + name][:, :], dram["pack_" + name]).then_inc(g["packs_loaded"], 16)
            for q in range(G):
                sp.wait_ge(emb_ready, q + 1)
                for j in range(GB):
                    sp.dma_start(g["h"][0:NP, q * GB + j, :], emb[j * NP:(j + 1) * NP, q, :]).then_inc(moved, 16)
            sp.wait_ge(moved, 16 * B)
            sp.wait_ge(txt_loaded, 16)
            sp.wait_ge(g["packs_loaded"], 16 * (len(PACKS) - 1))

        @block.tensor
        def _(pe):
            pe.wait_ge(loaded, 16)
            for q in range(G):
                for k in range(CONV_K):
                    last = pe.matmul(ps[0:GB * NP, 0, q, 0:D], x[:, k, q * GB * NP:(q + 1) * GB * NP], w[:, k, :],
                                     start=(k == 0), stop=(k == CONV_K - 1))
                last.then_inc(emb_ps, 1)

        @block.vector
        def _(dve):
            dve.wait_ge(loaded, 16)
            dve.tensor_tensor(bias[:, :], f.at("pos"), f.at("conv_b"), ALU.add).then_inc(bias_ready, 1)
            dve.wait_ge(bias_ready, 1)
            for q in range(G):
                dve.wait_ge(emb_ps, q + 1)
                dve.tensor_tensor(emb[:, q, :], ps[0:GB * NP, 0, q, 0:D], bias[:, :], ALU.add).then_inc(emb_ready, 1)


class Norm:

    def __init__(self, m, g, name, per_iter=1):
        self.stats = m.sb(name + "_stats", [L, 2, 6])
        self.moments = m.sb(name + "_moments", [L, 2, 2])
        self.shifted = m.sb(name + "_shifted", [L, 2])
        self.rstd = m.sb(name + "_rstd", [L, 2])
        self.pause = m.sb(name + "_pause", [1, 1])
        self.neg_half = g["const"].at("neg_half")
        self.var_ready, self.rstd_ready = m.sem(name + "_var_ready"), m.sem(name + "_rstd_ready")

    def vector(self, dve, i, steps, src, dst):
        for j in range(2):
            steps.done(dve.bn_stats(self.stats[:, j, :], src[j]))
        steps.wait()
        dve.memset(self.pause[:, :], 0.0)
        for j in range(2):
            steps.done(dve.bn_aggr(self.moments[:, j, :], self.stats[:, j, :]))
        steps.wait()
        dve.tensor_scalar(self.shifted[:, :], self.moments[:, :, 1], EPS, None, ALU.add).then_inc(self.var_ready, 1)
        dve.wait_ge(self.rstd_ready, i + 1)
        return [dve.tensor_scalar(dst[j], src[j], self.moments[:, j, 0:1], self.rstd[:, j:j + 1],
                                  ALU.subtract, ALU.mult) for j in range(2)]

    def pool(self, pool, i):
        pool.wait_ge(self.var_ready, i + 1)
        pool.tensor_tensor(self.rstd[:, :], self.shifted[:, :], self.neg_half, ALU.pow).then_inc(self.rstd_ready, 1)


def retention(nc, g):
    w = g["l0a"]
    wq, wk, wv = w.at("wq", C), w.at("wk", C), w.at("wv", C)
    ident = g["const"].at("ident")
    ps, h = g["ps"], g["h"]
    with ExitStack() as stack:
        m = Memory(nc, g, stack, "ret")
        norm = Norm(m, g, "norm")
        z = m.sb("z", [L, 2, D])
        xT = m.sb("xT", [K, 2, C, L])
        qT = m.sb("qT", [K, 2, C, L])
        kT = m.sb("kT", [K, 2, C, L])
        v = m.sb("v", [L, 2, D])
        sT = m.sb("sT", [L, 2, L])
        dve_steps = m.sem("dve_steps")
        z_ready, xT_ps, xT_ready = m.sem("z_ready"), m.sem("xT_ps"), m.sem("xT_ready")
        qkv_ps, qk_ready, v_ready = m.sem("qkv_ps"), m.sem("qk_ready"), m.sem("v_ready")
        s_ps, s_ready, o_ps = m.sem("s_ps"), m.sem("s_ready"), m.sem("o_ps")
        block = stack.enter_context(nc.Block())

        @block.tensor
        def _(pe):
            with pe.Fori(0, B // 2) as i:
                for j in range(2):
                    pe.wait_ge(z_ready, 2 * i + j + 1)
                    for c in range(C):
                        last = pe.transpose(ps[0:K, j, 3, c * L:(c + 1) * L], z[:, j, c * K:(c + 1) * K],
                                            ident[0:L, 0:L])
                    last.then_inc(xT_ps, 1)
                for j in range(2):
                    pe.wait_ge(xT_ready, 2 * i + j + 1)
                    for bank, wt in ((0, wq), (1, wk)):
                        for co in range(C):
                            for c in range(C):
                                pe.matmul(ps[0:K, j, bank, co * L:(co + 1) * L], wt[:, c, co * K:(co + 1) * K],
                                          xT[:, j, c, :], start=(c == 0), stop=(c == C - 1))
                    for c in range(C):
                        last = pe.matmul(ps[0:L, j, 2, 0:D], xT[:, j, c, :], wv[:, c, :],
                                         start=(c == 0), stop=(c == C - 1))
                    last.then_inc(qkv_ps, 1)
                for j in range(2):
                    pe.wait_ge(qk_ready, 2 * i + j + 1)
                    for c in range(C):
                        last = pe.matmul(ps[0:L, j, 3, 0:L], kT[:, j, c, :], qT[:, j, c, :],
                                         start=(c == 0), stop=(c == C - 1))
                    last.then_inc(s_ps, 1)
                for j in range(2):
                    pe.wait_ge(s_ready, 2 * i + j + 1)
                    pe.wait_ge(v_ready, 2 * i + j + 1)
                    pe.matmul(ps[0:L, j, 0, 0:D], sT[:, j, :], v[:, j, :], start=True, stop=True).then_inc(o_ps, 1)

        @block.scalar
        def _(act):
            with act.Fori(0, B // 2) as i:
                for j in range(2):
                    act.wait_ge(xT_ps, 2 * i + j + 1)
                    act.activation(xT[:, j, :, :], ps[0:K, j, 3, 0:C * L].rearrange("p (c n) -> p c n", c=C),
                                   ACT.Copy).then_inc(xT_ready, 1)
                for j in range(2):
                    act.wait_ge(qkv_ps, 2 * i + j + 1)
                    for bank, dst, bias in ((0, qT, w.at("bq")), (1, kT, w.at("bk"))):
                        for c in range(C):
                            last = act.activation(dst[:, j, c, :], ps[0:K, j, bank, c * L:(c + 1) * L],
                                                  ACT.Identity, bias=bias[:, c:c + 1])
                    last.then_inc(qk_ready, 1)

        @block.gpsimd
        def _(pool):
            with pool.Fori(0, B // 2) as i:
                norm.pool(pool, i)

        @block.vector
        def _(dve):
            own = 4
            with dve.Fori(0, B // 2) as i:
                steps = Steps(dve, dve_steps, own * i)
                for ins in norm.vector(dve, i, steps, [h[:, ds(2 * i + j, 1), :] for j in range(2)],
                                       [z[:, j:j + 1, :] for j in range(2)]):
                    ins.then_inc(z_ready, 1)
                for j in range(2):
                    dve.wait_ge(qkv_ps, 2 * i + j + 1)
                    dve.tensor_tensor(v[:, j, :], ps[0:L, j, 2, 0:D], w.at("bv"), ALU.add).then_inc(v_ready, 1)
                for j in range(2):
                    dve.wait_ge(s_ps, 2 * i + j + 1)
                    dve.tensor_tensor(sT[:, j, :], ps[0:L, j, 3, 0:L], w.at("decay"), ALU.mult).then_inc(s_ready, 1)
                for j in range(2):
                    dve.wait_ge(o_ps, 2 * i + j + 1)
                    dve.tensor_tensor(h[:, ds(2 * i + j, 1), :], h[:, ds(2 * i + j, 1), :],
                                      ps[0:L, j, 0:1, 0:D], ALU.add)
                assert steps.n == own


def softmax_attention(nc, g, phase, residual, mask=None, conv=False, project=True):
    w = g[phase]
    wq, wk, wv = w.at("wq", C), w.at("wk", C), w.at("wv", C)
    ident = g["const"].at("ident")
    ps, h, x = g["ps"], g["h"], g.get("x")
    two_norms = residual != "plain"
    gated = residual == "gated"
    VW = HD + 1
    with ExitStack() as stack:
        m = Memory(nc, g, stack, phase)
        norm = Norm(m, g, "norm")
        norm2 = Norm(m, g, "norm2") if two_norms else None
        z0 = m.sb("z0", [L, 2, D]) if two_norms else None
        z = m.sb("z", [L, 2, D])
        xT = m.sb("xT", [K, 2, C, L])
        qT = m.sb("qT", [128, 2, HT, L])
        kT = m.sb("kT", [128, 2, HT, L])
        if conv:
            side = m.sb("side", [128, 2, 2, HT, L])
            q2 = m.sb("q2", [128, 2, HT, L])
            k2 = m.sb("k2", [128, 2, HT, L])
        v = m.sb("v", [L, 2, H, VW])
        top = m.sb("top", [L, 2, H])
        p = m.sb("p", [L, 2, H, L])
        pT = m.sb("pT", [L, 2, H, L])
        rsum = m.sb("rsum", [L, 2, H])
        o = m.sb("o", [L, 2, D])
        if mask:
            mask_bf = m.sb("mask_bf", [L, HT, L], BF16)
            ident_bf = m.sb("ident_bf", [L, L], BF16)
        if project:
            oT = m.sb("oT", [K, 2, C, L])
            y = m.sb("y", [L, 2, D])
        if gated:
            lin_x = m.sb("lin_x", [K, 2, 2 * C, L])
            lin_e = m.sb("lin_e", [K, 2, 2 * C, L])
            lin_f = m.sb("lin_f", [K, 2, 2 * C, L])
            lin_v = m.sb("lin_v", [L, 2, D + 1])
            lin_s = m.sb("lin_s", [L, 2, L])
            lin_d = m.sb("lin_d", [L, 2])
            lin_o = m.sb("lin_o", [L, 2, D])
            mixT = m.sb("mixT", [K, 2, 2 * C, L])
            hidT = m.sb("hidT", [K, 2, C, L])
            gate = m.sb("gate", [L, 2, D])
            diff = m.sb("diff", [L, 2, D])
            fused = m.sb("fused", [L, 2, D])
            lin_ps, lin_x_ready, lin_m_ready = m.sem("lin_ps"), m.sem("lin_x_ready"), m.sem("lin_m_ready")
            lin_e_ready, lin_f_ready, lin_v_ready = m.sem("lin_e_ready"), m.sem("lin_f_ready"), m.sem("lin_v_ready")
            lin_s_ps, lin_s_ready, lin_o_ps = m.sem("lin_s_ps"), m.sem("lin_s_ready"), m.sem("lin_o_ps")
            lin_o_ready, mixT_ps, mixT_ready = m.sem("lin_o_ready"), m.sem("mixT_ps"), m.sem("mixT_ready")
            hid_ps, hid_ready, gate_ps = m.sem("hid_ps"), m.sem("hid_ready"), m.sem("gate_ps")
            gate_in, gate_exp, fused_ready = m.sem("gate_in"), m.sem("gate_exp"), m.sem("fused_ready")
        dve_steps, const_ready = m.sem("dve_steps"), m.sem("const_ready")
        z_ready, xT_ps, xT_ready = m.sem("z_ready"), m.sem("xT_ps"), m.sem("xT_ready")
        qkv_ps, qk_ready, v_ready = m.sem("qkv_ps"), m.sem("qk_ready"), m.sem("v_ready")
        mixed_ready, left_added = m.sem("mixed_ready"), m.sem("left_added")
        s_ps, below_ready, p_ready = m.sem("s_ps"), m.sem("below_ready"), m.sem("p_ready")
        pT_ps, pT_ready, o_ps, o_ready = m.sem("pT_ps"), m.sem("pT_ready"), m.sem("o_ps"), m.sem("o_ready")
        oT_ps, oT_ready, y_ps = m.sem("oT_ps"), m.sem("oT_ready"), m.sem("y_ps")
        block = stack.enter_context(nc.Block())

        def banked(j):
            return ps[0:L, j, :, 0:HT * L].rearrange("p r (t n) -> p r t n", t=HT)

        @block.tensor
        def _(pe):
            if mask:
                pe.wait_ge(const_ready, 3)
            with pe.Fori(0, B // 2) as i:
                for j in range(2):
                    pe.wait_ge(z_ready, 2 * i + j + 1)
                    for c in range(C):
                        last = pe.transpose(ps[0:K, j, 3, c * L:(c + 1) * L], z[:, j, c * K:(c + 1) * K],
                                            ident[0:L, 0:L])
                    last.then_inc(xT_ps, 1)
                for j in range(2):
                    pe.wait_ge(xT_ready, 2 * i + j + 1)
                    for bank, wt in ((0, wq), (1, wk)):
                        for t in range(HT):
                            for c in range(C):
                                pe.matmul(ps[:, j, bank, t * L:(t + 1) * L], wt[:, c, t * 128:(t + 1) * 128],
                                          xT[:, j, c, :], start=(c == 0), stop=(c == C - 1))
                    for c in range(C):
                        last = pe.matmul(ps[0:L, j, 2, 0:D], xT[:, j, c, :], wv[:, c, :],
                                         start=(c == 0), stop=(c == C - 1))
                    last.then_inc(qkv_ps, 1)
                qs, ks, ready = (q2, k2, mixed_ready) if conv else (qT, kT, qk_ready)
                for j in range(2):
                    pe.wait_ge(ready, 2 * i + j + 1)
                    pe.wait_ge(v_ready, 2 * i + j + 1)
                    if mask:
                        for r in range(RG):
                            pe.matmul(ps[0:L, j, r, 0:HT * L], ident_bf[:, :],
                                      mask_bf[:, :, :].rearrange("p t n -> p (t n)"),
                                      start=True, stop=False, skip_group_check=True)
                    for t in range(HT):
                        for r in range(RG):
                            last = pe.matmul(ps[0:L, j, r, t * L:(t + 1) * L], qs[HP * r:HP * (r + 1), j, t, :],
                                             ks[HP * r:HP * (r + 1), j, t, :], start=not mask, stop=True,
                                             skip_group_check=bool(mask))
                    last.then_inc(s_ps, 1)
                for j in range(2):
                    pe.wait_ge(p_ready, 2 * i + j + 1)
                    for a in range(H):
                        last = pe.transpose(ps[0:L, j, a // HT, (a % HT) * L:(a % HT + 1) * L], p[:, j, a, :],
                                            ident[0:L, 0:L])
                    last.then_inc(pT_ps, 1)
                for j in range(2):
                    pe.wait_ge(pT_ready, 2 * i + j + 1)
                    for a in range(H):
                        last = pe.matmul(ps[0:L, j, 0, a * VW:(a + 1) * VW], pT[:, j, a, :], v[:, j, a, :],
                                         start=True, stop=True)
                    last.then_inc(o_ps, 1)
                    if gated:
                        for bank, wt in ((1, "lin_wq"), (2, "lin_wk")):
                            for co in range(C):
                                for c in range(C):
                                    pe.matmul(ps[0:K, j, bank, co * L:(co + 1) * L],
                                              w.at(wt, C)[:, c, co * K:(co + 1) * K], xT[:, j, c, :],
                                              start=(c == 0), stop=(c == C - 1))
                        for c in range(C):
                            last = pe.matmul(ps[0:L, j, 3, 0:D], xT[:, j, c, :], w.at("lin_wv", C)[:, c, :],
                                             start=(c == 0), stop=(c == C - 1))
                        last.then_inc(lin_ps, 1)
                if gated:
                    for j in range(2):
                        pe.wait_ge(lin_f_ready, 2 * i + j + 1)
                        for c in range(C):
                            last = pe.matmul(ps[0:L, j, 1, 0:L], lin_f[:, j, C + c, :], lin_f[:, j, c, :],
                                             start=(c == 0), stop=(c == C - 1))
                        last.then_inc(lin_s_ps, 1)
                    for j in range(2):
                        pe.wait_ge(lin_s_ready, 2 * i + j + 1)
                        pe.wait_ge(lin_v_ready, 2 * i + j + 1)
                        pe.matmul(ps[0:L, j, 2, 0:D + 1], lin_s[:, j, :], lin_v[:, j, :], start=True, stop=True)\
                          .then_inc(lin_o_ps, 1)
                    for j in range(2):
                        pe.wait_ge(lin_o_ready, 2 * i + j + 1)
                        pe.wait_ge(o_ready, 2 * i + j + 1)
                        for n, src in ((0, lin_o), (1, o)):
                            for c in range(C):
                                last = pe.transpose(ps[0:K, j, 3, (n * C + c) * L:(n * C + c + 1) * L],
                                                    src[:, j, c * K:(c + 1) * K], ident[0:L, 0:L])
                        last.then_inc(mixT_ps, 1)
                    for j in range(2):
                        pe.wait_ge(mixT_ready, 2 * i + j + 1)
                        gate_in_T = [mixT[:, j, n, :] for n in range(2 * C)] + [xT[:, j, c, :] for c in range(C)]
                        for co in range(C):
                            for n, part in enumerate(gate_in_T):
                                last = pe.matmul(ps[0:K, j, 0, co * L:(co + 1) * L],
                                                 w.at("wg1", 3 * C)[:, n, co * K:(co + 1) * K], part,
                                                 start=(n == 0), stop=(n == 3 * C - 1))
                        last.then_inc(hid_ps, 1)
                    for j in range(2):
                        pe.wait_ge(hid_ready, 2 * i + j + 1)
                        for c in range(C):
                            last = pe.matmul(ps[0:L, j, 1, 0:D], hidT[:, j, c, :], w.at("wg2", C)[:, c, :],
                                             start=(c == 0), stop=(c == C - 1))
                        last.then_inc(gate_ps, 1)
                if project:
                    out_src, out_ready = (fused, fused_ready) if gated else (o, o_ready)
                    for j in range(2):
                        pe.wait_ge(out_ready, 2 * i + j + 1)
                        for c in range(C):
                            last = pe.transpose(ps[0:K, j, 1, c * L:(c + 1) * L], out_src[:, j, c * K:(c + 1) * K],
                                                ident[0:L, 0:L])
                        last.then_inc(oT_ps, 1)
                    for j in range(2):
                        pe.wait_ge(oT_ready, 2 * i + j + 1)
                        for c in range(C):
                            last = pe.matmul(ps[0:L, j, 2, 0:D], oT[:, j, c, :], w.at("wo", C)[:, c, :],
                                             start=(c == 0), stop=(c == C - 1))
                        last.then_inc(y_ps, 1)

        @block.scalar
        def _(act):
            with act.Fori(0, B // 2) as i:
                for j in range(2):
                    act.wait_ge(xT_ps, 2 * i + j + 1)
                    if two_norms:
                        for c in range(C):
                            last = act.activation(xT[:, j, c, :], ps[0:K, j, 3, c * L:(c + 1) * L], ACT.Identity,
                                                  scale=w.at("g")[:, c:c + 1], bias=w.at("b")[:, c:c + 1])
                    else:
                        last = act.activation(xT[:, j, :, :].rearrange("p c n -> p (c n)"),
                                              ps[0:K, j, 3, 0:C * L], ACT.Copy)
                    last.then_inc(xT_ready, 1)
                for j in range(2):
                    act.wait_ge(qkv_ps, 2 * i + j + 1)
                    for bank, dst, bias in ((0, qT, "bq"), (1, kT, "bk")):
                        if bias in w.where:
                            for t in range(HT):
                                last = act.activation(dst[:, j, t, :], ps[:, j, bank, t * L:(t + 1) * L],
                                                      ACT.Identity, bias=w.at(bias)[:, t:t + 1])
                        else:
                            last = act.activation(dst[:, j, :, :].rearrange("p t n -> p (t n)"),
                                                  ps[:, j, bank, 0:HT * L], ACT.Copy)
                    last.then_inc(qk_ready, 1)
                for j in range(2):
                    act.wait_ge(below_ready, 2 * i + j + 1)
                    act.activation(p[:, j, :, :], p[:, j, :, :], ACT.Exp, scale=HD ** -0.5).then_inc(p_ready, 1)
                for j in range(2):
                    act.wait_ge(pT_ps, 2 * i + j + 1)
                    act.activation(pT[:, j, :, :].rearrange("p (r t) n -> p r t n", r=RG), banked(j), ACT.Copy)\
                       .then_inc(pT_ready, 1)
                if gated:
                    for j in range(2):
                        act.wait_ge(lin_ps, 2 * i + j + 1)
                        for n, bias in ((0, "lin_bq"), (1, "lin_bk")):
                            for c in range(C):
                                last = act.activation(lin_x[:, j, n * C + c, :], ps[0:K, j, 1 + n, c * L:(c + 1) * L],
                                                      ACT.Identity, bias=w.at(bias)[:, c:c + 1])
                        last.then_inc(lin_x_ready, 1)
                    for j in range(2):
                        act.wait_ge(lin_m_ready, 2 * i + j + 1)
                        act.activation(lin_e[:, j, :, :], lin_e[:, j, :, :], ACT.Exp).then_inc(lin_e_ready, 1)
                    for j in range(2):
                        act.wait_ge(lin_s_ps, 2 * i + j + 1)
                        act.activation(lin_s[:, j, :], ps[0:L, j, 1, 0:L], ACT.Copy).then_inc(lin_s_ready, 1)
                    for j in range(2):
                        act.wait_ge(mixT_ps, 2 * i + j + 1)
                        act.activation(mixT[:, j, :, :].rearrange("p c n -> p (c n)"), ps[0:K, j, 3, 0:2 * C * L],
                                       ACT.Copy).then_inc(mixT_ready, 1)
                    for j in range(2):
                        act.wait_ge(hid_ps, 2 * i + j + 1)
                        for c in range(C):
                            last = act.activation(hidT[:, j, c, :], ps[0:K, j, 0, c * L:(c + 1) * L], ACT.Relu,
                                                  bias=w.at("bg1")[:, c:c + 1])
                        last.then_inc(hid_ready, 1)
                    for j in range(2):
                        act.wait_ge(gate_in, 2 * i + j + 1)
                        act.activation(gate[:, j, :], gate[:, j, :], ACT.Exp, scale=-1.0).then_inc(gate_exp, 1)
                if project:
                    for j in range(2):
                        act.wait_ge(oT_ps, 2 * i + j + 1)
                        act.activation(oT[:, j, :, :].rearrange("p c n -> p (c n)"), ps[0:K, j, 1, 0:C * L],
                                       ACT.Copy).then_inc(oT_ready, 1)

        @block.gpsimd
        def _(pool):
            if gated:
                pool.memset(lin_v[:, :, :], 1.0)
            pool.memset(v[:, :, :, :], 1.0).then_inc(const_ready, 1)
            with pool.Fori(0, B // 2) as i:
                norm.pool(pool, i)
                if two_norms:
                    norm2.pool(pool, i)

        @block.vector
        def _(dve):
            if mask:
                for t in range(HT):
                    last = dve.tensor_copy(mask_bf[:, t, :], w.at(mask))
                last.then_inc(const_ready, 1)
                dve.tensor_copy(ident_bf[:, :], ident[0:L, 0:L]).then_inc(const_ready, 1)
            dve.wait_ge(const_ready, 3 if mask else 1)
            own = 4 + 6 * two_norms + 4 * conv + 4 + 2 * project + 14 * gated
            with dve.Fori(0, B // 2) as i:
                steps = Steps(dve, dve_steps, own * i)
                tile = [ds(2 * i + j, 1) for j in range(2)]
                if two_norms:
                    for ins in norm.vector(dve, i, steps, [h[:, tile[j], :] for j in range(2)],
                                           [z0[:, j:j + 1, :] for j in range(2)]):
                        steps.done(ins)
                    steps.wait()
                    second = norm2.vector(dve, i, steps, [z0[:, j:j + 1, :] for j in range(2)],
                                          [z[:, j:j + 1, :] for j in range(2)])
                else:
                    second = norm.vector(dve, i, steps, [h[:, tile[j], :] for j in range(2)],
                                         [z[:, j:j + 1, :] for j in range(2)])
                for ins in second:
                    ins.then_inc(z_ready, 1)
                for j in range(2):
                    dve.wait_ge(qkv_ps, 2 * i + j + 1)
                    heads = ps[0:L, j, 2, 0:D].rearrange("p (a n) -> p a n", a=H)
                    if "bv" in w.where:
                        last = dve.tensor_tensor(v[:, j, :, 0:HD], heads, w.at("bv", H), ALU.add)
                    else:
                        last = dve.tensor_copy(v[:, j, :, 0:HD], heads)
                    last.then_inc(v_ready, 1)
                if conv:
                    for j in range(2):
                        dve.wait_ge(qk_ready, 2 * i + j + 1)
                        for n, src, dst, own_w, side_w in ((0, qT, q2, 0, 1), (1, kT, k2, 2, 3)):
                            mix = w.at("mix")
                            dve.tensor_scalar(side[:, j, n, :, :], src[:, j, :, :], mix[:, side_w:side_w + 1], None,
                                              ALU.mult)
                            steps.done(dve.tensor_scalar(dst[:, j, :, :], src[:, j, :, :], mix[:, own_w:own_w + 1],
                                                         None, ALU.mult))
                    for j in range(2):
                        steps.wait()
                        for n, dst in ((0, q2), (1, k2)):
                            left = dve.tensor_tensor(dst[:, j, :, 1:L], dst[:, j, :, 1:L], side[:, j, n, :, 0:L - 1],
                                                     ALU.add)
                        left.then_inc(left_added, 1)
                        dve.wait_ge(left_added, 2 * i + j + 1)
                        for n, dst in ((0, q2), (1, k2)):
                            last = dve.tensor_tensor(dst[:, j, :, 0:L - 1], dst[:, j, :, 0:L - 1],
                                                     side[:, j, n, :, 1:L], ALU.add)
                        last.then_inc(mixed_ready, 1)
                for j in range(2):
                    dve.wait_ge(s_ps, 2 * i + j + 1)
                    steps.done(dve.tensor_reduce(top[:, j, :].rearrange("p (r t) -> p r t", r=RG), banked(j),
                                                 AX.X, ALU.max))
                    steps.wait()
                    peak = top[:, j, :].rearrange("p (r t) -> p r t", r=RG).unsqueeze(3).broadcast_to([L, RG, HT, L])
                    dve.tensor_tensor(p[:, j, :, :].rearrange("p (r t) n -> p r t n", r=RG), banked(j), peak,
                                      ALU.subtract).then_inc(below_ready, 1)
                for j in range(2):
                    dve.wait_ge(o_ps, 2 * i + j + 1)
                    heads = ps[0:L, j, 0, 0:H * VW].rearrange("p (a n) -> p a n", a=H)
                    steps.done(dve.reciprocal(rsum[:, j, :].unsqueeze(2), heads[:, :, HD:VW]))
                    steps.wait()
                    dve.tensor_tensor(o[:, j, :].rearrange("p (a n) -> p a n", a=H), heads[:, :, 0:HD],
                                      rsum[:, j, :].unsqueeze(2).broadcast_to([L, H, HD]), ALU.mult)\
                       .then_inc(o_ready, 1)
                if gated:
                    for j in range(2):
                        dve.wait_ge(lin_x_ready, 2 * i + j + 1)
                        dve.tensor_scalar(lin_e[:, j, :, :], lin_x[:, j, :, :], 0.0, None, ALU.min)\
                           .then_inc(lin_m_ready, 1)
                        dve.wait_ge(lin_ps, 2 * i + j + 1)
                        dve.tensor_tensor(lin_v[:, j, 0:D], ps[0:L, j, 3, 0:D], w.at("lin_bv"), ALU.add)\
                           .then_inc(lin_v_ready, 1)
                    for j in range(2):
                        dve.wait_ge(lin_e_ready, 2 * i + j + 1)
                        dve.scalar_tensor_tensor(lin_f[:, j, :, :], lin_x[:, j, :, :], 0.0, lin_e[:, j, :, :],
                                                 ALU.max, ALU.add).then_inc(lin_f_ready, 1)
                    for j in range(2):
                        dve.wait_ge(lin_o_ps, 2 * i + j + 1)
                        steps.done(dve.tensor_scalar(lin_d[:, j:j + 1], ps[0:L, j, 2, D:D + 1], 1e-6, None, ALU.add))
                        steps.wait()
                        steps.done(dve.reciprocal(lin_d[:, j:j + 1], lin_d[:, j:j + 1]))
                        steps.wait()
                        dve.tensor_scalar(lin_o[:, j, :], ps[0:L, j, 2, 0:D], lin_d[:, j:j + 1], None, ALU.mult)\
                           .then_inc(lin_o_ready, 1)
                    for j in range(2):
                        dve.wait_ge(lin_o_ready, 2 * i + j + 1)
                        steps.done(dve.tensor_tensor(diff[:, j, :], lin_o[:, j, :], o[:, j, :], ALU.subtract))
                    for j in range(2):
                        dve.wait_ge(gate_ps, 2 * i + j + 1)
                        dve.tensor_tensor(gate[:, j, :], ps[0:L, j, 1, 0:D], w.at("bg2"), ALU.add)\
                           .then_inc(gate_in, 1)
                    for j in range(2):
                        dve.wait_ge(gate_exp, 2 * i + j + 1)
                        steps.done(dve.tensor_scalar(gate[:, j, :], gate[:, j, :], 1.0, None, ALU.add))
                        steps.wait()
                        steps.done(dve.reciprocal(gate[:, j, :], gate[:, j, :]))
                        steps.wait()
                        steps.done(dve.tensor_tensor(diff[:, j, :], diff[:, j, :], gate[:, j, :], ALU.mult))
                        steps.wait()
                        dve.tensor_tensor(fused[:, j, :], diff[:, j, :], o[:, j, :], ALU.add)\
                           .then_inc(fused_ready, 1)
                for j in range(2):
                    if project:
                        dve.wait_ge(y_ps, 2 * i + j + 1)
                        steps.done(dve.tensor_tensor(y[:, j, :], ps[0:L, j, 2, 0:D], w.at("bo"), ALU.add))
                        steps.wait()
                        add = y[:, j:j + 1, :]
                    else:
                        dve.wait_ge(o_ready, 2 * i + j + 1)
                        add = o[:, j:j + 1, :]
                    if gated:
                        steps.done(dve.tensor_tensor(y[:, j, :], y[:, j, :], z0[:, j, :], ALU.add))
                        steps.wait()
                    if residual == "normed":
                        dve.tensor_tensor(x[:, tile[j], :], z0[:, j:j + 1, :], add, ALU.add)
                    else:
                        dve.tensor_tensor(h[:, tile[j], :], h[:, tile[j], :], add, ALU.add)
                assert steps.n == own, (steps.n, own)


def route(nc, g, phase, two_norms):
    w = g[phase]
    ident, iota = g["const"].at("ident"), g["const"].at("iota")[:, 0:E01]
    bias = "b2" in w.where
    ps, h, x, xT_all, gates = g["ps"], g["h"], g["x"], g["xT"], g["gates"]
    with ExitStack() as stack:
        m = Memory(nc, g, stack, phase)
        norm = Norm(m, g, "norm")
        norm2 = Norm(m, g, "norm2") if two_norms else None
        z0 = m.sb("z0", [L, 2, D]) if two_norms else None
        z = m.sb("z", [L, 2, D])
        xT = m.sb("xT", [K, 2, C, L])
        logits = m.sb("logits", [L, 2, E01])
        best = m.sb("best", [L, 2, 8])
        place = m.sb("place", [L, 2, 8], U32)
        placef = m.sb("placef", [L, 2, 8])
        gap = m.sb("gap", [L, 2])
        ratio = m.sb("ratio", [L, 2])
        total = m.sb("total", [L, 2])
        share = m.sb("share", [L, 2, 2])
        part = m.sb("part", [L, 2, 2, E01])
        pause = m.sb("pause", [1, 1])
        if bias:
            gate_row = m.sb("gate_row", [L, 2, E01])
            gT = m.sb("gT", [E01, 2, L])
        dve_steps = m.sem("dve_steps")
        z_ready, xT_ps, xT_ready, xT_kept = m.sem("z_ready"), m.sem("xT_ps"), m.sem("xT_ready"), m.sem("xT_kept")
        logits_ps, gap_ready, ratio_ready = m.sem("logits_ps"), m.sem("gap_ready"), m.sem("ratio_ready")
        gates_ready, gT_ps, gT_ready, b2_ps = m.sem("gates_ready"), m.sem("gT_ps"), m.sem("gT_ready"), m.sem("b2_ps")
        block = stack.enter_context(nc.Block())

        @block.tensor
        def _(pe):
            with pe.Fori(0, B // 2) as i:
                for j in range(2):
                    pe.wait_ge(z_ready, 2 * i + j + 1)
                    for c in range(C):
                        last = pe.transpose(ps[0:K, j, 3, c * L:(c + 1) * L], z[:, j, c * K:(c + 1) * K],
                                            ident[0:L, 0:L])
                    last.then_inc(xT_ps, 1)
                for j in range(2):
                    pe.wait_ge(xT_ready, 2 * i + j + 1)
                    for c in range(C):
                        last = pe.matmul(ps[0:L, j, 0, 0:E01], xT[:, j, c, :], w.at("gate", C)[:, c, :],
                                         start=(c == 0), stop=(c == C - 1))
                    last.then_inc(logits_ps, 1)
                if bias:
                    for j in range(2):
                        pe.wait_ge(gates_ready, i + 1)
                        pe.transpose(ps[0:E01, j, 1, 0:L], gate_row[:, j, :], ident[0:L, 0:L]).then_inc(gT_ps, 1)
                    for j in range(2):
                        pe.wait_ge(gT_ready, 2 * i + j + 1)
                        pe.matmul(ps[0:L, j, 2, 0:D], gT[:, j, :], w.at("b2"), start=True, stop=True)\
                          .then_inc(b2_ps, 1)

        @block.scalar
        def _(act):
            with act.Fori(0, B // 2) as i:
                for j in range(2):
                    act.wait_ge(xT_ps, 2 * i + j + 1)
                    for c in range(C):
                        last = act.activation(xT[:, j, c, :], ps[0:K, j, 3, c * L:(c + 1) * L], ACT.Identity,
                                              scale=w.at("g")[:, c:c + 1], bias=w.at("b")[:, c:c + 1])
                    last.then_inc(xT_ready, 1)
                act.wait_ge(gap_ready, i + 1)
                act.activation(ratio[:, :], gap[:, :], ACT.Exp).then_inc(ratio_ready, 1)
                if bias:
                    for j in range(2):
                        act.wait_ge(gT_ps, 2 * i + j + 1)
                        act.activation(gT[:, j, :], ps[0:E01, j, 1, 0:L], ACT.Copy).then_inc(gT_ready, 1)
                act.wait_ge(xT_kept, 2 * i + 2)

        @block.gpsimd
        def _(pool):
            with pool.Fori(0, B // 2) as i:
                norm.pool(pool, i)
                if two_norms:
                    norm2.pool(pool, i)
                for j in range(2):
                    pool.wait_ge(xT_ready, 2 * i + j + 1)
                    pool.tensor_copy(xT_all[:, :, ds(2 * i + j, 1), :], xT[:, j, :, :].unsqueeze(2))\
                        .then_inc(xT_kept, 1)

        @block.vector
        def _(dve):
            own = 4 + 6 * two_norms + 2 + 2 + 3 + 1 + 1 + 2 + 2 + (2 if bias else 0)
            with dve.Fori(0, B // 2) as i:
                steps = Steps(dve, dve_steps, own * i)
                tile = [ds(2 * i + j, 1) for j in range(2)]
                if two_norms:
                    for ins in norm.vector(dve, i, steps, [h[:, tile[j], :] for j in range(2)],
                                           [z0[:, j:j + 1, :] for j in range(2)]):
                        steps.done(ins)
                    steps.wait()
                    src = [z0[:, j:j + 1, :] for j in range(2)]
                    second = norm2
                else:
                    src = [x[:, tile[j], :] for j in range(2)]
                    second = norm
                for ins in second.vector(dve, i, steps, src, [z[:, j:j + 1, :] for j in range(2)]):
                    ins.then_inc(z_ready, 1)
                for j in range(2):
                    steps.done(dve.tensor_tensor(h[:, tile[j], :], h[:, tile[j], :], src[j], ALU.add))
                for j in range(2):
                    dve.wait_ge(logits_ps, 2 * i + j + 1)
                    steps.done(dve.tensor_copy(logits[:, j, :], ps[0:L, j, 0, 0:E01]))
                steps.wait()
                dve.memset(pause[:, :], 0.0)
                for j in range(2):
                    last = dve.max(best[:, j, :], logits[:, j, :])
                steps.done(last)
                steps.wait()
                dve.tensor_tensor(gap[:, :], best[:, :, 1], best[:, :, 0], ALU.subtract).then_inc(gap_ready, 1)
                for j in range(2):
                    last = dve.max_index(place[:, j, :], best[:, j, :], logits[:, j, :])
                steps.done(last)
                steps.wait()
                steps.done(dve.tensor_copy(placef[:, :, :], place[:, :, :]))
                dve.wait_ge(ratio_ready, i + 1)
                steps.done(dve.tensor_scalar(total[:, :], ratio[:, :], 1.0, None, ALU.add))
                steps.wait()
                steps.done(dve.reciprocal(share[:, :, 0], total[:, :]))
                steps.wait()
                steps.done(dve.tensor_tensor(share[:, :, 1], share[:, :, 0], ratio[:, :], ALU.mult))
                steps.wait()
                for j in range(2):
                    for n in range(2):
                        last = dve.tensor_scalar(part[:, j, n, :], iota, placef[:, j, n:n + 1],
                                                 share[:, j, n:n + 1], ALU.is_equal, ALU.mult)
                    steps.done(last)
                steps.wait()
                if bias:
                    dve.tensor_tensor(gate_row[:, :, :], part[:, :, 0, :], part[:, :, 1, :], ALU.add)\
                       .then_inc(gates_ready, 1)
                steps.done(dve.tensor_tensor(gates[:, ds(2 * i, 2), 0:E01], part[:, :, 0, :], part[:, :, 1, :],
                                             ALU.add))
                if bias:
                    for j in range(2):
                        dve.wait_ge(b2_ps, 2 * i + j + 1)
                        steps.done(dve.tensor_tensor(h[:, tile[j], :], h[:, tile[j], :], ps[0:L, j, 2:3, 0:D],
                                                     ALU.add))
                assert steps.n == own, (steps.n, own)


def experts(nc, g, dram, phase, func):
    bias = phase == "l0"
    ps, h, xT_all, gates = g["ps"], g["h"], g["xT"], g["gates"]
    hid_banks = 4
    with ExitStack() as stack:
        m = Memory(nc, g, stack, phase)
        up = m.sb("up", [K, 2, C, F])
        down = m.sb("down", [128, 2, FM, D])
        b1 = m.sb("b1", [128, 2, FM]) if bias else None
        hidden = m.sb("hidden", [128, 2, FM, NG])
        up_loaded = [m.sem(f"up_loaded{j}") for j in range(2)]
        hid_ps, hid_ready = m.sem("hid_ps"), m.sem("hid_ready")
        y_ps, y_added = m.sem("y_ps"), m.sem("y_added")
        per_load = 16 * (3 if bias else 2)
        block = stack.enter_context(nc.Block())

        def visit(i, j, qq, jj):
            return (2 * i + j) * G + 2 * qq + jj

        @block.sync
        def _(sp):
            def load(e, j):
                sp.dma_start(up[:, j, :, :], dram[phase + "_up"][e].rearrange("e p (c n) -> p (e c) n", c=C))\
                  .then_inc(up_loaded[j], 16)
                sp.dma_start(down[:, j, :, :], dram[phase + "_down"][e].rearrange("e p (m n) -> p (e m) n", m=FM))\
                  .then_inc(up_loaded[j], 16)
                if bias:
                    sp.dma_start(b1[:, j, :], dram[phase + "_b1"][e].rearrange("e p m -> p (e m)"))\
                      .then_inc(up_loaded[j], 16)
            for j in range(2):
                load(slice(j, j + 1), j)
            with sp.Fori(1, E01 // 2) as i:
                for j in range(2):
                    sp.wait_ge(y_ps, (2 * i + j - 1) * G * GB)
                    load(ds(2 * i + j, 1), j)

        @block.tensor
        def _(pe):
            with pe.Fori(0, E01 // 2) as i:
                for j in range(2):
                    with pe.Fori(0, G // 2) as qq:
                        pe.wait_ge(up_loaded[j], per_load * (i + 1))
                        for jj in range(2):
                            n = visit(i, j, qq, jj)
                            for t in range(FM):
                                pe.wait_ge(hid_ready, n * FM + t + 1)
                                bank = (jj * FM + t) % hid_banks
                                for c in range(C):
                                    last = pe.matmul(ps[:, 0, bank, 0:NG], up[:, j, c, t * 128:(t + 1) * 128],
                                                     xT_all[:, c, ds((2 * qq + jj) * GB, GB), :],
                                                     start=(c == 0), stop=(c == C - 1))
                                last.then_inc(hid_ps, 1)
                        for jj in range(2):
                            n = visit(i, j, qq, jj)
                            pe.wait_ge(hid_ready, hid_banks + (n + 1) * FM)
                            for b in range(GB):
                                pe.wait_ge(y_added, n * GB + b + 1)
                                for t in range(FM):
                                    last = pe.matmul(ps[0:L, 1, b, 0:D], hidden[:, jj, t, b * L:(b + 1) * L],
                                                     down[:, j, t, :], start=(t == 0), stop=(t == FM - 1))
                                last.then_inc(y_ps, 1)

        @block.scalar
        def _(act):
            act.sem_inc(hid_ready, hid_banks)
            if bias:
                act.wait_ge(up_loaded[0], per_load)
            with act.Fori(0, E01 // 2) as i:
                for j in range(2):
                    with act.Fori(0, G // 2) as qq:
                        if bias:
                            act.wait_ge(up_loaded[j], per_load * (i + 1))
                        for jj in range(2):
                            n = visit(i, j, qq, jj)
                            for t in range(FM):
                                act.wait_ge(hid_ps, n * FM + t + 1)
                                bank = (jj * FM + t) % hid_banks
                                act.activation(hidden[:, jj, t, :], ps[:, 0, bank, 0:NG], func,
                                               bias=b1[:, j, t:t + 1] if bias else 0.0).then_inc(hid_ready, 1)

        @block.vector
        def _(dve):
            dve.sem_inc(y_added, GB)
            with dve.Fori(0, E01 // 2) as i:
                for j in range(2):
                    with dve.Fori(0, G // 2) as qq:
                        for jj in range(2):
                            n = visit(i, j, qq, jj)
                            for b in range(GB):
                                dve.wait_ge(y_ps, n * GB + b + 1)
                                tile = ds((2 * qq + jj) * GB + b, 1)
                                dve.scalar_tensor_tensor(h[:, tile, :], ps[0:L, 1, b:b + 1, 0:D],
                                                         gates[:, tile, ds(2 * i + j, 1)].rearrange("p a b -> p (a b)"),
                                                         h[:, tile, :], ALU.mult, ALU.add).then_inc(y_added, 1)


def sub_weights(nc, g, dram, sub):
    less = g["l2f"].at("parts")
    up_parts, down, spread = sub["up"], sub["down"], sub["spread"]
    cols = NM * 32
    with ExitStack() as stack:
        m = Memory(nc, g, stack, "l2w")
        raw = m.sb("raw", [128, 2, cols])
        first = m.sb("first", [128, cols], BF16)
        rest = m.sb("rest", [128, cols])
        spread_f = m.sb("spread_f", [96, 8 * 128])
        raw_loaded, down_loaded = [m.sem(f"raw_loaded{j}") for j in range(2)], m.sem("down_loaded")
        spread_loaded = m.sem("spread_loaded")
        first_ready, rest_ready, second_ready, parts_ready = (
            m.sem("first_ready"), m.sem("rest_ready"), m.sem("second_ready"), m.sem("parts_ready"))
        block = stack.enter_context(nc.Block())

        @block.sync
        def _(sp):
            sp.dma_start(spread_f[:, :], dram["sub_spread"]).then_inc(spread_loaded, 16)
            for n in range(NS):
                if n >= 2:
                    sp.wait_ge(parts_ready, n - 1)
                sp.dma_start(raw[:, n % 2, :], dram["sub_up"][n]).then_inc(raw_loaded[n % 2], 16)
            sp.dma_start(down.rearrange("p s t r -> p (s t r)"), dram["sub_down"]).then_inc(down_loaded, 16)
            sp.wait_ge(down_loaded, 16)

        @block.scalar
        def _(act):
            act.wait_ge(spread_loaded, 16)
            act.activation(spread.rearrange("p t n -> p (t n)"), spread_f[:, :], ACT.Copy)
            for n in range(NS):
                act.wait_ge(raw_loaded[n % 2], 16 * (n // 2 + 1))
                if n:
                    act.wait_ge(parts_ready, n)
                act.activation(first[:, :], raw[:, n % 2, :], ACT.Copy).then_inc(first_ready, 1)
                act.wait_ge(rest_ready, n + 1)
                act.activation(first[:, :], rest[:, :], ACT.Copy).then_inc(second_ready, 1)

        @block.vector
        def _(dve):
            for n in range(NS):
                dve.wait_ge(first_ready, n + 1)
                dve.scalar_tensor_tensor(rest[:, :], first[:, :], less[:, 2:3], raw[:, n % 2, :],
                                         ALU.mult, ALU.add).then_inc(rest_ready, 1)
                dve.wait_ge(second_ready, n + 1)
                dve.scalar_tensor_tensor(up_parts[:, n, :], first[:, :], less[:, 3:4], rest[:, :],
                                         ALU.mult, ALU.add).then_inc(parts_ready, 1)


def sub_gates(nc, g, sub, base):
    w = g["l2f"]
    ident, iota, less = g["const"].at("ident"), g["const"].at("iota"), w.at("parts")
    ps, h = g["ps"], g["h"]
    zs, gs, comb = sub["zs"], sub["gs"], sub["comb"]
    with ExitStack() as stack:
        m = Memory(nc, g, stack, f"l2g{base}")
        norm = Norm(m, g, "norm")
        z = m.sb("z", [L, 2, D])
        xT = m.sb("xT", [K, 2, C, L])
        sT = m.sb("sT", [128, 2, L])
        z_part = m.sb("z_part", [128, 2, 2, 4 * L], BF16)
        z_rest = m.sb("z_rest", [128, 2, 2, 4 * L])
        score = m.sb("score", [L, 2, NS, NM])
        best = m.sb("best", [L, 2, NS, 8])
        place = m.sb("place", [L, 2, NS, 8], U32)
        last_place = m.sb("last_place", [L, 2, NS])
        few = m.sb("few", [L, 2, NS, KEEP])
        share = m.sb("share", [L, 2, NS])
        expo = m.sb("expo", [L, 2, NS, NM])
        above = m.sb("above", [L, 2, NS, NM])
        tied = m.sb("tied", [L, 2, NS, NM])
        early = m.sb("early", [L, 2, NS, NM], BF16)
        gate = m.sb("gate", [L, 2, NS * 2, 32])
        gate_parts = m.sb("gate_parts", [L, 2, NS * 2, 3, 32], BF16)
        gT = m.sb("gT", [128, 2, 4, L])
        ident_bf = m.sb("ident_bf", [L, L], BF16)
        pause = m.sb("pause", [1, 1])
        dve_steps, ident_ready = m.sem("dve_steps"), m.sem("ident_ready")
        z_ready, xT_ps, xT_ready = m.sem("z_ready"), m.sem("xT_ps"), m.sem("xT_ready")
        sT_ps, sT_ready, score_ps, score_ready = m.sem("sT_ps"), m.sem("sT_ready"), m.sem("score_ps"), m.sem("score_ready")
        z8_ps, z1_ready, z_rest_ready, z2_ready, zs_ready = (
            m.sem("z8_ps"), m.sem("z1_ready"), m.sem("z_rest_ready"), m.sem("z2_ready"), m.sem("zs_ready"))
        few_ready, few_exp, below, below_exp = m.sem("few_ready"), m.sem("few_exp"), m.sem("below"), m.sem("below_exp")
        gate_ready = m.sem("gate_ready")
        g1_ready, less1_ready, g2_ready, less2_ready, g3_ready = (
            m.sem("g1_ready"), m.sem("less1_ready"), m.sem("g2_ready"), m.sem("less2_ready"), m.sem("g3_ready"))
        gs_ps, gs_ready = m.sem("gs_ps"), m.sem("gs_ready")
        gT_ps, gT_ready, b2_ps = m.sem("gT_ps"), m.sem("gT_ready"), m.sem("b2_ps")
        block = stack.enter_context(nc.Block())

        def parts_bank(j, n):
            return ps[0:96, j, 1 + n, 0:4 * L].bitcast(BF16).rearrange("p (a n) -> p a n", a=8)

        @block.tensor
        def _(pe):
            pe.wait_ge(ident_ready, 1)
            with pe.Fori(0, HALF // 2) as i:
                for j in range(2):
                    pe.wait_ge(z_ready, 2 * i + j + 1)
                    for c in range(C):
                        last = pe.transpose(ps[0:K, j, 3, c * L:(c + 1) * L], z[:, j, c * K:(c + 1) * K],
                                            ident[0:L, 0:L])
                    last.then_inc(xT_ps, 1)
                for j in range(2):
                    pe.wait_ge(xT_ready, 2 * i + j + 1)
                    for c in range(C):
                        last = pe.matmul(ps[:, j, 0, 0:L], w.at("p", C)[:, c, :], xT[:, j, c, :],
                                         start=(c == 0), stop=(c == C - 1))
                    last.then_inc(sT_ps, 1)
                for j in range(2):
                    pe.wait_ge(sT_ready, 2 * i + j + 1)
                    pe.matmul(ps[0:L, j, 1, :], sT[:, j, :], w.at("centres"), start=True, stop=True)\
                      .then_inc(score_ps, 1)
                for j in range(2):
                    for n in range(NS):
                        for c in range(C):
                            last = pe.matmul(ps[:, j, 2 + n // 4, (n % 4) * L:(n % 4 + 1) * L],
                                             w.at("p8", C)[:, c, n * 128:(n + 1) * 128], xT[:, j, c, :],
                                             start=(c == 0), stop=(c == C - 1))
                    last.then_inc(z8_ps, 1)
                for j in range(2):
                    pe.wait_ge(gate_ready, 2 * i + j + 1)
                    for n in range(4):
                        last = pe.transpose(ps[:, j, 0, n * L:(n + 1) * L],
                                            gate[:, j, 4 * n:4 * n + 4, :].rearrange("p a m -> p (a m)"),
                                            ident[0:L, 0:L])
                    last.then_inc(gT_ps, 1)
                for j in range(2):
                    pe.wait_ge(g3_ready, 2 * i + j + 1)
                    pe.wait_ge(zs_ready, 2 * i + j + 1)
                    for n in range(2 * NS):
                        last = pe.transpose(parts_bank(j, n // 8)[:, n % 8, :],
                                            gate_parts[:, j, n, :, :].rearrange("p a m -> p (a m)"), ident_bf[:, :])
                    last.then_inc(gs_ps, 1)
                for j in range(2):
                    pe.wait_ge(gT_ready, 2 * i + j + 1)
                    for half in range(2):
                        for n in range(RG):
                            last = pe.matmul(ps[HP * n:HP * (n + 1), j, 3, half * L:(half + 1) * L],
                                             w.at("b2", 8)[:, 2 * n + half, :], gT[:, j, n, :],
                                             start=True, stop=True)
                    last.then_inc(b2_ps, 1)

        @block.scalar
        def _(act):
            with act.Fori(0, HALF // 2) as i:
                for j in range(2):
                    act.wait_ge(xT_ps, 2 * i + j + 1)
                    act.activation(xT[:, j, :, :].rearrange("p c n -> p (c n)"), ps[0:K, j, 3, 0:C * L],
                                   ACT.Copy).then_inc(xT_ready, 1)
                for j in range(2):
                    act.wait_ge(sT_ps, 2 * i + j + 1)
                    act.activation(sT[:, j, :], ps[:, j, 0, 0:L], ACT.Copy).then_inc(sT_ready, 1)
                for j in range(2):
                    act.wait_ge(score_ps, 2 * i + j + 1)
                    act.activation(score[:, j, :, :].rearrange("p s m -> p (s m)"), ps[0:L, j, 1, :], ACT.Copy)\
                       .then_inc(score_ready, 1)
                for j in range(2):
                    act.wait_ge(z8_ps, 2 * i + j + 1)
                    act.activation(z_part[:, j, :, :], ps[:, j, 2:4, 0:4 * L], ACT.Copy).then_inc(z1_ready, 1)
                for j in range(2):
                    act.wait_ge(below, 2 * i + j + 1)
                    act.activation(expo[:, j, :, :], expo[:, j, :, :], ACT.Exp).then_inc(below_exp, 1)
                    act.wait_ge(few_ready, 2 * i + j + 1)
                    act.activation(few[:, j, :, :], few[:, j, :, :], ACT.Exp).then_inc(few_exp, 1)
                    act.wait_ge(z_rest_ready, 2 * i + j + 1)
                    act.activation(z_part[:, j, :, :], z_rest[:, j, :, :], ACT.Copy).then_inc(z2_ready, 1)
                for j in range(2):
                    act.wait_ge(gate_ready, 2 * i + j + 1)
                    act.activation(gate_parts[:, j, :, 0, :], gate[:, j, :, :], ACT.Copy).then_inc(g1_ready, 1)
                for j in range(2):
                    act.wait_ge(less1_ready, 2 * i + j + 1)
                    act.activation(gate_parts[:, j, :, 1, :], expo[:, j, :, :].rearrange("p s (a m) -> p (s a) m", a=2),
                                   ACT.Copy).then_inc(g2_ready, 1)
                for j in range(2):
                    act.wait_ge(less2_ready, 2 * i + j + 1)
                    act.activation(gate_parts[:, j, :, 2, :], tied[:, j, :, :].rearrange("p s (a m) -> p (s a) m", a=2),
                                   ACT.Copy).then_inc(g3_ready, 1)
                for j in range(2):
                    act.wait_ge(gT_ps, 2 * i + j + 1)
                    act.activation(gT[:, j, :, :].rearrange("p a n -> p (a n)"), ps[:, j, 0, 0:4 * L], ACT.Copy)\
                       .then_inc(gT_ready, 1)
                for j in range(2):
                    act.wait_ge(gs_ps, 2 * i + j + 1)
                    for n in range(2):
                        last = act.activation(gs[:, 8 * n:8 * n + 8, ds(2 * i + j, 1), :],
                                              parts_bank(j, n).unsqueeze(2), ACT.Copy)
                    last.then_inc(gs_ready, 1)

        @block.gpsimd
        def _(pool):
            with pool.Fori(0, HALF // 2) as i:
                norm.pool(pool, i)
                for j in range(2):
                    pool.wait_ge(g1_ready, 2 * i + j + 1)
                    pool.tensor_tensor(expo[:, j, :, :].rearrange("p s (a m) -> p (s a) m", a=2), gate[:, j, :, :],
                                       gate_parts[:, j, :, 0, :], ALU.subtract).then_inc(less1_ready, 1)
                for j in range(2):
                    pool.wait_ge(g2_ready, 2 * i + j + 1)
                    pool.tensor_tensor(tied[:, j, :, :].rearrange("p s (a m) -> p (s a) m", a=2),
                                       expo[:, j, :, :].rearrange("p s (a m) -> p (s a) m", a=2),
                                       gate_parts[:, j, :, 1, :], ALU.subtract).then_inc(less2_ready, 1)

        @block.vector
        def _(dve):
            dve.tensor_copy(ident_bf[:, :], ident[0:L, 0:L]).then_inc(ident_ready, 1)
            own = 4 + 2 * 11
            with dve.Fori(0, HALF // 2) as i:
                steps = Steps(dve, dve_steps, own * i)
                for ins in norm.vector(dve, i, steps, [h[:, ds(2 * i + j + base, 1), :] for j in range(2)],
                                       [z[:, j:j + 1, :] for j in range(2)]):
                    ins.then_inc(z_ready, 1)
                for j in range(2):
                    dve.wait_ge(score_ready, 2 * i + j + 1)
                    dve.memset(pause[:, :], 0.0)
                    for n in range(NS):
                        last = dve.max(best[:, j, n, :], score[:, j, n, :])
                    steps.done(last)
                    steps.wait()
                    dve.tensor_tensor(expo[:, j, :, :], score[:, j, :, :],
                                      best[:, j, :, 0:1].broadcast_to([L, NS, NM]), ALU.subtract).then_inc(below, 1)
                    dve.tensor_tensor(few[:, j, :, :], best[:, j, :, 0:KEEP],
                                      best[:, j, :, 0:1].broadcast_to([L, NS, KEEP]), ALU.subtract)\
                       .then_inc(few_ready, 1)
                    for n in range(NS):
                        last = dve.max_index(place[:, j, n, :], best[:, j, n, :], score[:, j, n, :])
                    steps.done(last)
                    dve.wait_ge(z1_ready, 2 * i + j + 1)
                    dve.scalar_tensor_tensor(z_rest[:, j, :, :], z_part[:, j, :, :], less[:, 0:1],
                                             ps[:, j, 2:4, 0:4 * L], ALU.mult, ALU.add).then_inc(z_rest_ready, 1)
                    fourth = best[:, j, :, KEEP - 1:KEEP].broadcast_to([L, NS, NM])
                    steps.done(dve.tensor_tensor(above[:, j, :, :], score[:, j, :, :], fourth, ALU.is_gt))
                    steps.done(dve.tensor_tensor(tied[:, j, :, :], score[:, j, :, :], fourth, ALU.is_equal))
                    steps.wait()
                    steps.done(dve.tensor_copy(last_place[:, j, :], place[:, j, :, KEEP - 1]))
                    steps.wait()
                    steps.done(dve.tensor_tensor(early[:, j, :, :], iota.unsqueeze(1).broadcast_to([L, NS, NM]),
                                                 last_place[:, j, :].unsqueeze(2).broadcast_to([L, NS, NM]),
                                                 ALU.is_le))
                    dve.wait_ge(few_exp, 2 * i + j + 1)
                    steps.done(dve.tensor_reduce(share[:, j, :], few[:, j, :, :], AX.X, ALU.add))
                    steps.wait()
                    steps.done(dve.tensor_tensor(tied[:, j, :, :], tied[:, j, :, :], early[:, j, :, :], ALU.mult))
                    steps.wait()
                    steps.done(dve.reciprocal(share[:, j, :], share[:, j, :]))
                    steps.done(dve.tensor_tensor(above[:, j, :, :], above[:, j, :, :], tied[:, j, :, :], ALU.add))
                    dve.wait_ge(below_exp, 2 * i + j + 1)
                    steps.wait()
                    steps.done(dve.tensor_tensor(above[:, j, :, :], above[:, j, :, :], expo[:, j, :, :], ALU.mult))
                    steps.wait()
                    dve.tensor_tensor(gate[:, j, :, :].rearrange("p (s a) m -> p s (a m)", a=2), above[:, j, :, :],
                                      share[:, j, :].unsqueeze(2).broadcast_to([L, NS, NM]), ALU.mult)\
                       .then_inc(gate_ready, 1)
                    dve.wait_ge(z2_ready, 2 * i + j + 1)
                    for n in range(2):
                        last = dve.scalar_tensor_tensor(
                            zs[:, 4 * n:4 * n + 4, ds(2 * i + j, 1), :].rearrange("p s a n -> p (s a) n"),
                            z_part[:, j, n, :].rearrange("p (s n) -> p s n", s=4), less[:, 1:2],
                            z_rest[:, j, n, :].rearrange("p (s n) -> p s n", s=4), ALU.mult, ALU.add)
                    last.then_inc(zs_ready, 1)
                for j in range(2):
                    dve.wait_ge(b2_ps, 2 * i + j + 1)
                    dve.tensor_copy(comb[:, :, ds(2 * i + j + base, 1), :],
                                    ps[:, j, 3, 0:2 * L].rearrange("p (c a n) -> p c a n", c=2, a=1))
                dve.wait_ge(gs_ready, 2 * i + 2)
                assert steps.n == own, (steps.n, own)


def sub_experts(nc, g, sub, base):
    w = g["l2f"]
    ps, comb = g["ps"], sub["comb"]
    zs, gs, up_parts, down, spread = sub["zs"], sub["gs"], sub["up"], sub["down"], sub["spread"]
    chunks = HALF // GB
    tiles = NS * MT
    deep = 3
    order = [(2 * r + half, t, r) for half in range(2) for t in range(MT) for r in range(RG)]
    with ExitStack() as stack:
        m = Memory(nc, g, stack, f"l2s{base}")
        hidden = m.sb("hidden", [128, deep, NG])
        gated = m.sb("gated", [128, 2 * RG, NG])
        tile_ps, hid_ready, gated_ready = m.sem("tile_ps"), m.sem("hid_ready"), m.sem("gated_ready")
        comb_ps, comb_ready = m.sem("comb_ps"), m.sem("comb_ready")
        block = stack.enter_context(nc.Block())

        def bank(kind, n):
            at = 3 * kind + n % deep
            return ps[:, at // 4, at % 4, 0:NG]

        sums = [ps[:, 1, 2 + half, 0:NG] for half in range(2)]

        @block.tensor
        def _(pe):
            def second(n, q):
                pe.wait_ge(gated_ready, deep + tiles * q + n + RG)
                for at in range(n, n + RG):
                    s, t, r = order[at]
                    last = pe.matmul(sums[at // (tiles // 2)][HP * r:HP * (r + 1)], down[:, s, t, :],
                                     gated[:, at % (2 * RG), :], start=(t == 0), stop=(t == MT - 1))
                if n + RG == tiles:
                    last.then_inc(comb_ps, 1)

            with pe.Fori(0, chunks) as q:
                for n, (s, t, r) in enumerate(order):
                    before = n - deep if n >= deep else max(a for a in range(tiles) if a % deep == n) - tiles
                    pe.wait_ge(gated_ready, tiles * q + before + 1 + deep)
                    pe.matmul(bank(1, n), spread[:, t % 8, :], gs[:, 2 * s + t // 8, ds(q * GB, GB), :],
                              start=True, stop=True)
                    pe.matmul(bank(0, n), up_parts[:, s, t * 128:(t + 1) * 128], zs[:, s, ds(q * GB, GB), :],
                              start=True, stop=True).then_inc(tile_ps, 1)
                    if n == RG - 1:
                        pe.wait_ge(comb_ready, q + 1)
                    if n % RG == RG - 1 and n > RG:
                        second(n - 2 * RG + 1, q)
                second(tiles - RG, q)

        @block.scalar
        def _(act):
            with act.Fori(0, chunks) as q:
                for n, (s, t, r) in enumerate(order):
                    act.wait_ge(tile_ps, tiles * q + n + 1)
                    act.activation(hidden[:, n % deep, :], bank(0, n), ACT.Gelu_apprx_tanh,
                                   bias=w.at("b1")[:, s * MT + t:s * MT + t + 1]).then_inc(hid_ready, 1)

        @block.vector
        def _(dve):
            dve.sem_inc(gated_ready, deep)
            dve.sem_inc(comb_ready, 1)
            with dve.Fori(0, chunks) as q:
                for n in range(tiles):
                    dve.wait_ge(hid_ready, tiles * q + n + 1)
                    dve.tensor_tensor(gated[:, n % (2 * RG), :], hidden[:, n % deep, :], bank(1, n), ALU.mult)\
                       .then_inc(gated_ready, 1)
                dve.wait_ge(comb_ps, q + 1)
                for half in range(2):
                    part = comb[:, half, ds(q * GB + base, GB), :]
                    last = dve.tensor_tensor(part, part, sums[half].rearrange("p (a n) -> p a n", a=GB), ALU.add)
                last.then_inc(comb_ready, 1)


def sub_output(nc, g, sub):
    w = g["l2f"]
    ps, h, comb = g["ps"], g["h"], sub["comb"]
    with ExitStack() as stack:
        m = Memory(nc, g, stack, "l2o")
        hT = m.sb("hT", [64, 2, L])
        y = m.sb("y", [L, 2, D])
        h_ps, h_ready, y_ps, y_ready, added = m.sem("h_ps"), m.sem("h_ready"), m.sem("y_ps"), m.sem("y_ready"), m.sem("added")
        block = stack.enter_context(nc.Block())

        @block.tensor
        def _(pe):
            with pe.Fori(0, B // 2) as i:
                for j in range(2):
                    pe.wait_ge(h_ready, 2 * i + j + 1)
                    for half in range(2):
                        last = pe.matmul(ps[0:64, j, 1, 0:L], w.at("g1", 2)[:, half, :], comb[:, half, ds(2 * i + j, 1), :],
                                         start=(half == 0), stop=(half == 1))
                    last.then_inc(h_ps, 1)
                for j in range(2):
                    pe.wait_ge(h_ready, 2 + 2 * i + j + 1)
                    pe.wait_ge(y_ready, 2 * i + j + 1)
                    pe.matmul(ps[0:L, j, 2, 0:D], hT[:, j, :], w.at("g2"), start=True, stop=True).then_inc(y_ps, 1)

        @block.scalar
        def _(act):
            act.sem_inc(h_ready, 2)
            with act.Fori(0, B // 2) as i:
                for j in range(2):
                    act.wait_ge(h_ps, 2 * i + j + 1)
                    act.activation(hT[:, j, :], ps[0:64, j, 1, 0:L], ACT.Gelu_apprx_tanh, bias=w.at("g1b"))\
                       .then_inc(h_ready, 1)

        @block.vector
        def _(dve):
            dve.sem_inc(y_ready, 2)
            with dve.Fori(0, B // 2) as i:
                for j in range(2):
                    dve.wait_ge(y_ps, 2 * i + j + 1)
                    dve.tensor_tensor(y[:, j, :], ps[0:L, j, 2, 0:D], w.at("g2b"), ALU.add).then_inc(y_ready, 1)
                for j in range(2):
                    tile = ds(2 * i + j, 1)
                    dve.wait_ge(y_ready, 2 + 2 * i + j + 1)
                    dve.tensor_tensor(h[:, tile, :], h[:, tile, :], y[:, j:j + 1, :], ALU.add).then_inc(added, 1)
                dve.wait_ge(added, 2 * i + 2)


def sub_feed_forward(nc, g, dram):
    with ExitStack() as stack:
        def sb(name, shape, dt=F32):
            return stack.enter_context(nc.sbuf_tensor("sub_" + name, shape, dt))[:]

        sub = {"comb": sb("comb", [128, 2, B, L]), "up": sb("up", [128, NS, NM * 32], BF16),
               "down": sb("down", [128, NS, MT, HP]), "spread": sb("spread", [96, 8, 128], BF16)}
        sub_weights(nc, g, dram, sub)
        with ExitStack() as inner:
            sub["zs"] = inner.enter_context(nc.sbuf_tensor("sub_zs", [128, NS, HALF, L], BF16))[:]
            sub["gs"] = inner.enter_context(nc.sbuf_tensor("sub_gs", [96, 2 * NS, HALF, L], BF16))[:]
            for base in (0, HALF):
                sub_gates(nc, g, sub, base)
                sub_experts(nc, g, sub, base)
        sub_output(nc, g, sub)


def normalise(nc, g):
    ident = g["const"].at("ident")
    ps, h, x, xT_all = g["ps"], g["h"], g["x"], g["xT"]
    with ExitStack() as stack:
        m = Memory(nc, g, stack, "l3n")
        norm = Norm(m, g, "norm")
        z = m.sb("z", [L, 2, D])
        dve_steps = m.sem("dve_steps")
        z_ready, z_kept, xT_ps, xT_ready = m.sem("z_ready"), m.sem("z_kept"), m.sem("xT_ps"), m.sem("xT_ready")
        block = stack.enter_context(nc.Block())

        @block.tensor
        def _(pe):
            with pe.Fori(0, B // 2) as i:
                for j in range(2):
                    pe.wait_ge(z_ready, 2 * i + j + 1)
                    pe.wait_ge(xT_ready, 2 * i + j + 1)
                    for c in range(C):
                        last = pe.transpose(ps[0:K, j, 3, c * L:(c + 1) * L], z[:, j, c * K:(c + 1) * K],
                                            ident[0:L, 0:L])
                    last.then_inc(xT_ps, 1)

        @block.scalar
        def _(act):
            act.sem_inc(xT_ready, 2)
            with act.Fori(0, B // 2) as i:
                for j in range(2):
                    act.wait_ge(xT_ps, 2 * i + j + 1)
                    act.activation(xT_all[:, :, ds(2 * i + j, 1), :],
                                   ps[0:K, j, 3, 0:C * L].rearrange("p (c a n) -> p c a n", c=C, a=1),
                                   ACT.Copy).then_inc(xT_ready, 1)

        @block.gpsimd
        def _(pool):
            with pool.Fori(0, B // 2) as i:
                norm.pool(pool, i)
                for j in range(2):
                    pool.wait_ge(z_ready, 2 * i + j + 1)
                    pool.tensor_copy(x[:, ds(2 * i + j, 1), :], z[:, j:j + 1, :]).then_inc(z_kept, 1)

        @block.vector
        def _(dve):
            with dve.Fori(0, B // 2) as i:
                steps = Steps(dve, dve_steps, 4 * i)
                for ins in norm.vector(dve, i, steps, [h[:, ds(2 * i + j, 1), :] for j in range(2)],
                                       [z[:, j:j + 1, :] for j in range(2)]):
                    ins.then_inc(z_ready, 1)
                dve.wait_ge(z_kept, 2 * i + 2)
                dve.wait_ge(xT_ps, 2 * i + 2)


def choose(nc, g, dram, chosen, xln, out):
    w = g["l3f"]
    ident = g["const"].at("ident")
    ps, h, xT_all = g["ps"], g["h"], g["xT"]
    with ExitStack() as stack:
        m = Memory(nc, g, stack, "l3c")
        score = m.sb("score", [E3, T])
        value = m.sb("value", [E3, ROUNDS * 8])
        place = m.sb("place", [E3, ROUNDS * 8], U32)
        placef = m.sb("placef", [E3, ROUNDS * 8])
        act_gate = m.sb("act_gate", [128, 2, SM, NG])
        act_up = m.sb("act_up", [128, 2, SM, NG])
        hidden = m.sb("hidden", [128, 2, SM, NG])
        y = m.sb("y", [L, B, D])
        x_stored, out_stored = m.sem("x_stored"), m.sem("out_stored")
        score_ps, score_ready, rounds, placef_ready = m.sem("score_ps"), m.sem("score_ready"), m.sem("rounds"), m.sem("placef_ready")
        list_ps = m.sem("list_ps")
        gu_ps, gu_ready, hidden_ready, y_ps, y_ready, h_ready = (
            m.sem("gu_ps"), m.sem("gu_ready"), m.sem("hidden_ready"), m.sem("y_ps"), m.sem("y_ready"), m.sem("h_ready"))
        block = stack.enter_context(nc.Block())

        @block.sync
        def _(sp):
            sp.dma_start(xln.rearrange("(b t) d -> t b d", b=B), g["x"][:, :, :]).then_inc(x_stored, 16)
            sp.wait_ge(h_ready, G)
            sp.dma_start(out.rearrange("b t d -> t b d"), h[:, :, :]).then_inc(out_stored, 16)
            sp.wait_ge(x_stored, 16)
            sp.wait_ge(out_stored, 16)

        @block.tensor
        def _(pe):
            for q in range(G):
                for c in range(C):
                    last = pe.matmul(ps[0:E3, 0, q, 0:NG], w.at("choose", C)[:, c, :],
                                     xT_all[:, c, q * GB:(q + 1) * GB, :], start=(c == 0), stop=(c == C - 1))
                last.then_inc(score_ps, 1)
            for q in range(G):
                for t in range(SM):
                    n = q * SM + t
                    if n < 2:
                        pe.wait_ge(score_ready, 2 * n + 2)
                    else:
                        pe.wait_ge(gu_ready, n - 1)
                    for u, name in ((0, "ws_g"), (1, "ws_u")):
                        for c in range(C):
                            last = pe.matmul(ps[:, 0, 2 * (n % 2) + u, 0:NG],
                                             w.at(name, C)[:, c, t * 128:(t + 1) * 128],
                                             xT_all[:, c, q * GB:(q + 1) * GB, :], start=(c == 0), stop=(c == C - 1))
                    last.then_inc(gu_ps, 1)
                pe.wait_ge(hidden_ready, (q + 1) * SM)
                if q:
                    pe.wait_ge(y_ready, q)
                for b in range(GB):
                    for t in range(SM):
                        last = pe.matmul(ps[0:L, 1, b, 0:D], hidden[:, q % 2, t, b * L:(b + 1) * L],
                                         w.at("ws_d", SM)[:, t, :], start=(t == 0), stop=(t == SM - 1))
                last.then_inc(y_ps, 1)
            pe.wait_ge(placef_ready, 1)
            pe.wait_ge(gu_ready, G * SM)
            for half in range(2):
                for n, src in ((0, placef), (1, value)):
                    last = pe.transpose(ps[0:L, 0, n, half * E3:(half + 1) * E3],
                                        src[:, half * L:(half + 1) * L], ident[0:E3, 0:E3])
            last.then_inc(list_ps, 1)

        @block.scalar
        def _(act):
            for q in range(G):
                act.wait_ge(score_ps, q + 1)
                act.activation(score[:, q * NG:(q + 1) * NG], ps[0:E3, 0, q, 0:NG], ACT.Sigmoid)\
                   .then_inc(score_ready, 1)
            for q in range(G):
                for t in range(SM):
                    n = q * SM + t
                    act.wait_ge(gu_ps, n + 1)
                    if q >= 2:
                        act.wait_ge(hidden_ready, (q - 1) * SM)
                    act.activation(act_gate[:, q % 2, t, :], ps[:, 0, 2 * (n % 2), 0:NG], ACT.Silu)
                    act.activation(act_up[:, q % 2, t, :], ps[:, 0, 2 * (n % 2) + 1, 0:NG], ACT.Copy)\
                       .then_inc(gu_ready, 1)
                act.wait_ge(y_ps, q + 1)
                act.activation(y[:, q * GB:(q + 1) * GB, :], ps[0:L, 1, :, 0:D], ACT.Copy).then_inc(y_ready, 1)

        @block.gpsimd
        def _(pool):
            for q in range(G):
                for t in range(SM):
                    pool.wait_ge(gu_ready, q * SM + t + 1)
                    if q >= 2:
                        pool.wait_ge(y_ps, q - 1)
                    pool.tensor_tensor(hidden[:, q % 2, t, :], act_gate[:, q % 2, t, :], act_up[:, q % 2, t, :],
                                       ALU.mult).then_inc(hidden_ready, 1)
                pool.wait_ge(y_ready, q + 1)
                pool.tensor_tensor(h[:, q * GB:(q + 1) * GB, :], h[:, q * GB:(q + 1) * GB, :],
                                   y[:, q * GB:(q + 1) * GB, :], ALU.add).then_inc(h_ready, 1)

        @block.vector
        def _(dve):
            dve.wait_ge(score_ready, G)
            for n in range(ROUNDS):
                eight = slice(n * 8, n * 8 + 8)
                if n:
                    dve.wait_ge(rounds, 2 * n)
                dve.max(value[:, eight], score[:, :]).then_inc(rounds, 1)
                dve.wait_ge(rounds, 2 * n + 1)
                dve.max_index(place[:, eight], value[:, eight], score[:, :])
                if n < ROUNDS - 1:
                    dve.match_replace(score[:, :], value[:, eight], score[:, :], -1.0).then_inc(rounds, 1)
                else:
                    dve.memset(chosen["pause"][:, :], 0.0).then_inc(rounds, 1)
            dve.drain()
            dve.tensor_copy(placef[:, :], place[:, :]).then_inc(placef_ready, 1)
            dve.wait_ge(list_ps, 1)
            dve.tensor_copy(chosen["place"][:, :, :], ps[0:L, 0, 0, 0:2 * E3].rearrange("p (a e) -> p a e", a=2))
            dve.tensor_copy(chosen["score"][:, :, :], ps[0:L, 0, 1, 0:2 * E3].rearrange("p (a e) -> p a e", a=2))


def chosen_experts(nc, g, dram, chosen, xln, out):
    ident = g["const"].at("ident")
    ps = g["ps"]
    table = out.rearrange("b t d -> (b t) d")
    with ExitStack() as stack:
        m = Memory(nc, g, stack, "l3e")
        wg = m.sb("wg", [K, 2, C, F])
        wu = m.sb("wu", [K, 2, C, F])
        wd = m.sb("wd", [128, 2, FM, D])
        rows_of = [[m.sb(f"rows{j}{a}", [L, 1], U32) for a in range(2)] for j in range(2)]
        xg = [[m.sb(f"xg{j}{a}", [L, D]) for a in range(2)] for j in range(2)]
        xgT = m.sb("xgT", [K, 2, C, 2, L])
        pause = m.sb("pause", [1, 6])
        held = m.sem("held")
        act_gate = m.sb("act_gate", [128, 2, FM, 2 * L])
        hidden = m.sb("hidden", [128, 2, FM, 2, L])
        y = [[m.sb(f"y{j}{a}", [L, D]) for a in range(2)] for j in range(2)]
        loaded = [m.sem(f"loaded{j}") for j in range(2)]
        rows_ready, gathered, xgT_ps, xgT_ready = m.sem("rows_ready"), [m.sem(f"gathered{j}") for j in range(2)], m.sem("xgT_ps"), m.sem("xgT_ready")
        hid_ps, gate_ready, hid_ready, y_ps, y_ready, added = (
            m.sem("hid_ps"), m.sem("gate_ready"), m.sem("hid_ready"), m.sem("y_ps"), m.sem("y_ready"), m.sem("added"))
        block = stack.enter_context(nc.Block())

        @block.sync
        def _(sp):
            def load(e, j):
                for dst, name in ((wg, "l3_gate"), (wu, "l3_up"), (wd, "l3_down")):
                    sp.dma_start(dst[:, j, :, :], dram[name][e].rearrange("e p (c n) -> p (e c) n", n=dst.shape[3]))\
                      .then_inc(loaded[j], 16)
            for j in range(2):
                load(slice(j, j + 1), j)
            with sp.Fori(1, E3 // 2) as i:
                for j in range(2):
                    sp.wait_ge(y_ps, 2 * i + j - 1)
                    load(ds(2 * i + j, 1), j)

        @block.gpsimd
        def _(pool):
            neg = g["const"].at("neg_half")

            def hold(n):
                pool.tensor_tensor(pause[:, n:n + 1], neg[0:1, 0:1], neg[0:1, 1:2], ALU.mult).then_inc(held, 1)

            def gather(j):
                hold(j)
                for a in range(2):
                    pool.indirect_dma_start(xg[j][a][:, :], None, xln,
                                            bass.IndirectOffsetOnAxis(ap=rows_of[j][a][:, :], axis=0))\
                        .then_inc(gathered[j], 16)

            with pool.Fori(0, E3 // 2) as i:
                for j in range(2):
                    pool.wait_ge(rows_ready, 2 * i + j + 1)
                    gather(j)
                for j in range(2):
                    pool.wait_ge(y_ready, 2 * i + j + 1)
                    for a in range(2):
                        hold(2 + 2 * j + a)
                        pool.indirect_dma_start(table, bass.IndirectOffsetOnAxis(ap=rows_of[j][a][:, :], axis=0),
                                                y[j][a][:, :], None, compute_op=ALU.add).then_inc(added, 16)
                        pool.wait_ge(added, 16 * (2 * (2 * i + j) + a + 1))
                pool.wait_ge(held, 6 * (i + 1))

        @block.tensor
        def _(pe):
            with pe.Fori(0, E3 // 2) as i:
                for j in range(2):
                    pe.wait_ge(gathered[j], 32 * (i + 1))
                    for a in range(2):
                        for c in range(C):
                            last = pe.transpose(ps[0:K, j, 3, (c * 2 + a) * L:(c * 2 + a + 1) * L],
                                                xg[j][a][:, c * K:(c + 1) * K], ident[0:L, 0:L])
                    last.then_inc(xgT_ps, 1)
                for j in range(2):
                    pe.wait_ge(xgT_ready, 2 * i + j + 1)
                    pe.wait_ge(loaded[j], 48 * (i + 1))
                    for t in range(FM):
                        n = FM * (2 * i + j) + t
                        pe.wait_ge(hid_ready, n + 1)
                        for u, wt in ((0, wg), (1, wu)):
                            for c in range(C):
                                last = pe.matmul(ps[:, j, t % 3, u * 2 * L:(u + 1) * 2 * L],
                                                 wt[:, j, c, t * 128:(t + 1) * 128],
                                                 xgT[:, j, c, :, :], start=(c == 0), stop=(c == C - 1))
                        last.then_inc(hid_ps, 1)
                for j in range(2):
                    pe.wait_ge(hid_ready, 3 + FM * (2 * i + j + 1))
                    for a in range(2):
                        for t in range(FM):
                            last = pe.matmul(ps[0:L, j, 3, a * D:(a + 1) * D], hidden[:, j, t, a, :],
                                             wd[:, j, t, :], start=(t == 0), stop=(t == FM - 1))
                    last.then_inc(y_ps, 1)

        @block.scalar
        def _(act):
            with act.Fori(0, E3 // 2) as i:
                for j in range(2):
                    act.wait_ge(xgT_ps, 2 * i + j + 1)
                    act.activation(xgT[:, j, :, :, :].rearrange("p c a n -> p (c a n)"), ps[0:K, j, 3, 0:4 * L],
                                   ACT.Copy).then_inc(xgT_ready, 1)
                for j in range(2):
                    for t in range(FM):
                        n = FM * (2 * i + j) + t
                        act.wait_ge(hid_ps, n + 1)
                        act.activation(act_gate[:, j, t, :], ps[:, j, t % 3, 0:2 * L], ACT.Silu)\
                           .then_inc(gate_ready, 1)

        @block.vector
        def _(dve):
            dve.sem_inc(hid_ready, 3)
            with dve.Fori(0, E3 // 2) as i:
                for j in range(2):
                    for a in range(2):
                        last = dve.tensor_copy(rows_of[j][a][:, :], chosen["place"][:, a, ds(2 * i + j, 1)])
                    last.then_inc(rows_ready, 1)
                for j in range(2):
                    for t in range(FM):
                        n = FM * (2 * i + j) + t
                        dve.wait_ge(gate_ready, n + 1)
                        dve.tensor_tensor(hidden[:, j, t, :, :].rearrange("p a n -> p (a n)"), act_gate[:, j, t, :],
                                          ps[:, j, t % 3, 2 * L:4 * L], ALU.mult).then_inc(hid_ready, 1)
                for j in range(2):
                    dve.wait_ge(y_ps, 2 * i + j + 1)
                    for a in range(2):
                        last = dve.tensor_scalar(y[j][a][:, :], ps[0:L, j, 3, a * D:(a + 1) * D],
                                                 chosen["score"][:, a, ds(2 * i + j, 1)], None, ALU.mult)
                    last.then_inc(y_ready, 1)
                dve.wait_ge(added, 64 * (i + 1))


def chosen_feed_forward(nc, g, dram, out):
    xln = nc.dram_tensor("xln", [T, D], F32).ap()
    with ExitStack() as stack:
        g["x"] = stack.enter_context(nc.sbuf_tensor("x3", [L, B, D], F32))
        g["xT"] = stack.enter_context(nc.sbuf_tensor("x3T", [K, C, B, L], F32))
        chosen = {"place": stack.enter_context(nc.sbuf_tensor("chosen_place", [L, 2, E3], U32)),
                  "score": stack.enter_context(nc.sbuf_tensor("chosen_score", [L, 2, E3], F32)),
                  "pause": stack.enter_context(nc.sbuf_tensor("chosen_pause", [1, 1], F32))}
        normalise(nc, g)
        choose(nc, g, dram, chosen, xln, out)
        chosen_experts(nc, g, dram, chosen, xln, out)


def build(nc, dram, out):
    with ExitStack() as stack, ExitStack() as to_layer_2, ExitStack() as to_layer_1:
        g = {"h": stack.enter_context(nc.sbuf_tensor("h", [L, B, D], F32)),
             "ps": stack.enter_context(nc.psum_tensor("ps", [128, 2, 4, 512], F32)),
             "packs_loaded": stack.enter_context(nc.semaphore("packs_loaded"))}
        first = min(nc.free_semaphores)
        g["sem_banks"] = [range(first + n * SEM_BANK, first + (n + 1) * SEM_BANK) for n in range(2)]
        g["phases"] = 0
        for scope, names in ((stack, ("const", "l3a", "l3f")), (to_layer_2, ("l2f", "l2a")),
                             (to_layer_1, ("l0a", "l0f", "l0r", "l1a", "l1r"))):
            for name in names:
                if name == "l2a":
                    continue
                g["pack_" + name] = scope.enter_context(
                    nc.sbuf_tensor("pack_" + name, [128, offsets(name)[1]], F32))
                g[name] = Fields(g["pack_" + name], name)
        l2a = to_layer_1.enter_context(nc.sbuf_tensor("pack_l2a", [128, offsets("l2a")[1]], F32))
        g["pack_l2a"], g["l2a"] = l2a, Fields(l2a, "l2a")
        g["x"] = to_layer_1.enter_context(nc.sbuf_tensor("x", [L, B, D], F32))
        g["xT"] = to_layer_1.enter_context(nc.sbuf_tensor("xT", [K, C, B, L], F32))
        g["gates"] = to_layer_1.enter_context(nc.sbuf_tensor("gates", [L, B, E01], F32))

        embed(nc, g, dram)
        layers = [lambda: retention(nc, g),
                  lambda: (softmax_attention(nc, g, "l0f", "normed"), route(nc, g, "l0r", False),
                           experts(nc, g, dram, "l0", ACT.Gelu)),
                  lambda: softmax_attention(nc, g, "l1a", "both", conv=True, project=False),
                  lambda: (route(nc, g, "l1r", True), experts(nc, g, dram, "l1", ACT.Silu)),
                  lambda: softmax_attention(nc, g, "l2a", "gated", mask="band"),
                  lambda: (to_layer_1.close(), sub_feed_forward(nc, g, dram)),
                  lambda: (to_layer_1.close(), to_layer_2.close(),
                           softmax_attention(nc, g, "l3a", "plain", mask="causal")),
                  lambda: (to_layer_1.close(), to_layer_2.close(), chosen_feed_forward(nc, g, dram, out))]
        for layer in layers:
            layer()



def lay_rows(w):
    n = w.shape[1]
    return w.reshape(C, K, n).transpose(1, 0, 2).reshape(K, C * n)


def kernel(**inputs):
    import numpy as np
    import concourse.bacc as bacc
    from concourse.bass_utils import run_bass_kernel_spmd

    a = {k: np.asarray(v) for k, v in inputs.items()}
    f32 = np.float32

    def heads(w, twice=False):
        p = np.zeros((w.shape[0], HT, RG, HP), f32)
        s = w.reshape(w.shape[0], RG, HT, HD).transpose(0, 2, 1, 3)
        p[:, :, :, :HD] = s
        if twice:
            p[:, :, :, HD:] = s
        return p.reshape(w.shape[0], HT * 128)

    def head_bias(b, twice=False):
        return heads(b.reshape(1, D), twice).reshape(HT, 128).T

    def rows(b, n=L):
        return np.broadcast_to(b, (n, b.shape[0]))

    def col(b):
        return b.reshape(C, K).T

    side, nb = 32, 84 // 16
    edges = np.arange(1.0 / side, 1.0, 1.0 / side, dtype=f32)
    frac = np.arange(0.0, 1.0 - 1e-6, 1.0 / nb, dtype=f32)
    bins = np.searchsorted(edges, frac, side="right")
    pos = a["L0_tok_pos_table"][(bins[:, None] * side + bins).reshape(-1)]
    px = a["x"][:, :, :80, :80].reshape(B, 3, nb, 16, nb, 16).transpose(1, 3, 5, 0, 2, 4).reshape(CONV_K, 128, B * NP)
    conv_w = a["L0_tok_conv_w"].reshape(D, CONV_K, 128).transpose(2, 1, 0)
    steps = np.arange(L)
    ahead = steps[None, :] - steps[:, None]
    decay = np.where(ahead >= 0, f32(0.99) ** ahead.astype(f32), 0.0) / f32(np.sqrt(f32(D)))
    wqkv0 = a["L0_attn_W_qkv"].T
    b0 = a["L0_attn_b_qkv"]
    wqf, bqf = a["L0_ffn_qkv_w"], a["L0_ffn_qkv_b"]
    fields = {
        "tok": {"conv_w": conv_w.reshape(128, -1), "patches": px.transpose(1, 0, 2).reshape(128, -1),
                "pos": np.tile(pos, (GB, 1)), "conv_b": rows(a["L0_tok_conv_b"], GB * NP)},
        "const": {"ident": np.eye(128, dtype=f32), "neg_half": np.full((L, 2), -0.5, f32), "iota": rows(np.arange(64, dtype=f32))},
        "l0a": {"wq": lay_rows(wqkv0[:, :D]), "wk": lay_rows(wqkv0[:, D:2 * D]), "wv": lay_rows(wqkv0[:, 2 * D:]),
                "bq": col(b0[:D]), "bk": col(b0[D:2 * D]), "bv": rows(b0[2 * D:]), "decay": decay},
        "l0f": {"wq": lay_rows(heads(wqf[:, :D])), "wk": lay_rows(heads(wqf[:, D:2 * D])),
                "wv": lay_rows(wqf[:, 2 * D:]), "bq": head_bias(bqf[:D]), "bk": head_bias(bqf[D:2 * D]),
                "bv": rows(bqf[2 * D:]), "g": col(a["L0_ffn_ln1_g"]), "b": col(a["L0_ffn_ln1_b"]),
                "wo": lay_rows(a["L0_ffn_proj_w"]), "bo": rows(a["L0_ffn_proj_b"])},
    }
    w1a, b1a = a["L1_attn_qkv_w"].T, a["L1_attn_qkv_b"]
    half = np.arange(128) % HP < HD
    mix = np.stack([np.ones(128), 1.0 - half, np.where(half, 1.2, -0.2), np.where(half, 0.0, -0.2)], 1)
    fields["l1a"] = {"wq": lay_rows(heads(w1a[:, :D], True)), "wk": lay_rows(heads(w1a[:, D:2 * D], True)),
                     "wv": lay_rows(w1a[:, 2 * D:]), "bq": head_bias(b1a[:D], True),
                     "bk": head_bias(b1a[D:2 * D], True), "bv": rows(b1a[2 * D:]), "g": col(a["L1_attn_ln_g"]),
                     "b": col(a["L1_attn_ln_b"]), "mix": mix.astype(f32)}
    fields["l0r"] = {"g": col(a["L0_ffn_ln2_g"]), "b": col(a["L0_ffn_ln2_b"]), "gate": lay_rows(a["L0_ffn_gate_w"]),
                     "b2": a["L0_ffn_b2"]}
    fields["l1r"] = {"g": col(a["L1_ffn_ln_gamma"]), "b": col(a["L1_ffn_ln_beta"]),
                     "gate": lay_rows(a["L1_ffn_router_w"])}

    def up(w):
        return w.reshape(-1, C, K, F).transpose(0, 2, 1, 3).reshape(-1, K, C * F)

    def down(w):
        return w.reshape(-1, FM, 128, D).transpose(0, 2, 1, 3).reshape(-1, 128, FM * D)

    w2 = {n: a["L2_attn_W_" + n] for n in ("q_lin", "k_lin", "v_lin", "q_loc", "k_loc", "v_loc", "out", "g1", "g2")}
    b2 = {n: a["L2_attn_b_" + n] for n in w2}
    apart = np.abs(ahead)
    fields["l2a"] = {"wq": lay_rows(heads(w2["q_loc"])), "wk": lay_rows(heads(w2["k_loc"])),
                     "wv": lay_rows(w2["v_loc"]), "bq": head_bias(b2["q_loc"]), "bk": head_bias(b2["k_loc"]),
                     "bv": rows(b2["v_loc"]), "g": col(a["L2_attn_gamma1"]), "b": col(a["L2_attn_beta1"]),
                     "band": np.where(apart <= 32, 0.0, NEG).astype(f32), "lin_wq": lay_rows(w2["q_lin"]),
                     "lin_wk": lay_rows(w2["k_lin"]), "lin_wv": lay_rows(w2["v_lin"]), "lin_bq": col(b2["q_lin"]),
                     "lin_bk": col(b2["k_lin"]), "lin_bv": rows(b2["v_lin"]),
                     "wg1": w2["g1"].reshape(3 * C, K, D).transpose(1, 0, 2).reshape(K, -1), "bg1": col(b2["g1"]),
                     "wg2": lay_rows(w2["g2"]), "bg2": rows(b2["g2"]), "wo": lay_rows(w2["out"]),
                     "bo": rows(b2["out"])}
    sub_up = np.tile(a["L2_ffn_W1"].transpose(0, 2, 1, 3).reshape(NS, NR, NM * 32), (1, len(PAIRS), 1))
    sub_down = np.zeros((4, 32, NS, MT, HP), f32)
    sub_down[..., :NR] = a["L2_ffn_W2"].reshape(NS, MT, 4, 32, NR).transpose(2, 3, 0, 1, 4)
    spread = np.zeros((3, 32, 8, 4, 32), f32)
    for n in range(32):
        spread[:, n, n // 4, n % 4] = 1.0
    centres = np.zeros((NS, NR, NS, NM), f32)
    for n in range(NS):
        centres[n, :, n] = a["L2_ffn_C"][n].T
    b2s = np.zeros((2, NM, RG, 2, HP), f32)
    for half in range(2):
        b2s[half, :, :, half, :NR] = a["L2_ffn_b2"][half::2].transpose(1, 0, 2)
    g1s = np.zeros((RG, HP, 2, 64), f32)
    g1s[:, :NR] = a["L2_ffn_G1"].reshape(RG, 2, NR, 64).transpose(0, 2, 1, 3)
    less = np.array([[-(p > 1), -(p > 2), -(q > 1), -(q > 2)] for p, q in PAIRS], f32).repeat(NR, 0)
    sub_p = a["L2_ffn_P"].transpose(1, 0, 2)
    fields["l2f"] = {"p": lay_rows(sub_p.reshape(D, 128)),
                     "p8": lay_rows(np.tile(sub_p[:, :, None, :], (1, 1, len(PAIRS), 1)).reshape(D, NS * 128)),
                     "centres": centres.reshape(128, -1), "b2": b2s.reshape(128, -1), "parts": less,
                     "b1": a["L2_ffn_b1"].reshape(NS * MT, 128).T, "g1": g1s.reshape(128, -1),
                     "g1b": a["L2_ffn_g1b"][:, None], "g2": a["L2_ffn_G2"], "g2b": rows(a["L2_ffn_g2b"])}
    fields["l3f"] = {"choose": lay_rows(a["L3_ffn_gate_weight"].T), "ws_g": lay_rows(a["L3_ffn_Ws_g"].T),
                     "ws_u": lay_rows(a["L3_ffn_Ws_u"].T),
                     "ws_d": a["L3_ffn_Ws_d"].T.reshape(SM, 128, D).transpose(1, 0, 2)}
    w3 = a["L3_attn_w_attn"]
    fields["l3a"] = {"wq": lay_rows(heads(w3[:, :D])), "wk": lay_rows(heads(w3[:, D:2 * D])),
                     "wv": lay_rows(w3[:, 2 * D:]), "causal": np.where(ahead <= 0, 0.0, NEG).astype(f32),
                     "wo": lay_rows(a["L3_attn_w_proj"]), "bo": rows(a["L3_attn_b_proj"])}

    arrays = {"txt": a["txt"], "l3_gate": up(a["L3_ffn_Wg"].transpose(0, 2, 1)),
              "l3_up": up(a["L3_ffn_Wu"].transpose(0, 2, 1)), "l3_down": down(a["L3_ffn_Wd"].transpose(0, 2, 1)),
              "sub_up": sub_up, "sub_down": sub_down.reshape(128, -1), "sub_spread": spread.reshape(96, -1),
              "l0_up": up(a["L0_ffn_w1"]), "l0_down": down(a["L0_ffn_w2"]),
              "l0_b1": a["L0_ffn_b1"].reshape(E01, FM, 128).transpose(0, 2, 1),
              "l1_up": up(a["L1_ffn_w1"]), "l1_down": down(a["L1_ffn_w2"])}
    for pack in PACKS:
        where, width = offsets(pack)
        arr = np.zeros((128, width), f32)
        for name, (n, start, cols) in where.items():
            arr[:n, start:start + cols] = fields[pack][name].reshape(n, cols)
        arrays["pack_" + pack] = arr

    nc = bacc.Bacc("TRN2", target_bir_lowering=False, num_devices=1)
    feed, dram = {}, {}
    for name, arr in arrays.items():
        feed["in_" + name] = np.ascontiguousarray(arr)
        dram[name] = nc.dram_tensor("in_" + name, arr.shape, mybir.dt.from_np(arr.dtype), kind="ExternalInput").ap()
    out = nc.dram_tensor("out", (B, L, D), F32, kind="ExternalOutput").ap()
    build(nc, dram, out)
    r = run_bass_kernel_spmd(nc, [feed], core_ids=[0])
    return r.results[0]["out"]
```

```python
from contextlib import ExitStack

import concourse.bass as bass
from concourse import mybir

B = 16
L = 102
NP = 25
D = 192
C = 2
K = D // C
H = 12
HD = D // H
RG = 4
HT = H // RG
HP = 32
T = B * L
CONV_K = 6
GB = 4
G = B // GB
NG = GB * L
EPS = 1e-5
E01 = 8
F = 768
FM = F // 128
NS = 8
NR = 16
NM = 64
KEEP = 4
MT = NM // 4
PAIRS = ((1, 1), (1, 2), (2, 1), (2, 2), (1, 3), (3, 1), (2, 3), (3, 2))
HALF = B // 2
E3 = 16
CAP = T * 2 // E3
ROUNDS = -(-CAP // 8)
FS = F * 2 // 4
SM = FS // 128
NEG = -1e30

F32 = mybir.dt.float32
BF16 = mybir.dt.bfloat16
U32 = mybir.dt.uint32
ALU = mybir.AluOpType
ACT = mybir.ActivationFunctionType
AX = mybir.AxisListType
ds = bass.ds

PACKS = {
    "tok": [("conv_w", 128, CONV_K * D), ("patches", 128, CONV_K * B * NP), ("pos", GB * NP, D), ("conv_b", GB * NP, D)],
    "const": [("ident", 128, 128), ("neg_half", L, 2), ("iota", L, 64)],
    "l0a": [("wq", K, C * D), ("wk", K, C * D), ("wv", K, C * D), ("bq", K, C), ("bk", K, C), ("bv", L, D),
            ("decay", L, L)],
    "l2a": [("wq", K, C * HT * 128), ("wk", K, C * HT * 128), ("wv", K, C * D), ("bq", 128, HT), ("bk", 128, HT),
            ("bv", L, D), ("g", K, C), ("b", K, C), ("band", L, L), ("lin_wq", K, C * D), ("lin_wk", K, C * D),
            ("lin_wv", K, C * D), ("lin_bq", K, C), ("lin_bk", K, C), ("lin_bv", L, D), ("wg1", K, 3 * C * D),
            ("bg1", K, C), ("wg2", K, C * D), ("bg2", L, D), ("wo", K, C * D), ("bo", L, D)],
    "l2f": [("p", K, C * 128), ("p8", K, C * NS * 128), ("centres", 128, NS * NM), ("b2", 128, 4 * 2 * 32),
            ("parts", 128, 4), ("b1", 128, NS * MT), ("g1", 128, 2 * 64), ("g1b", 64, 1), ("g2", 64, D), ("g2b", L, D)],
    "l3f": [("choose", K, C * E3), ("ws_g", K, C * FS), ("ws_u", K, C * FS), ("ws_d", 128, SM * D)],
    "l3a": [("wq", K, C * HT * 128), ("wk", K, C * HT * 128), ("wv", K, C * D), ("causal", L, L),
            ("wo", K, C * D), ("bo", L, D)],
    "l0r": [("g", K, C), ("b", K, C), ("gate", K, C * E01), ("b2", E01, D)],
    "l1r": [("g", K, C), ("b", K, C), ("gate", K, C * E01)],
    "l1a": [("wq", K, C * HT * 128), ("wk", K, C * HT * 128), ("wv", K, C * D), ("bq", 128, HT), ("bk", 128, HT),
            ("bv", L, D), ("g", K, C), ("b", K, C), ("mix", 128, 4)],
    "l0f": [("wq", K, C * HT * 128), ("wk", K, C * HT * 128), ("wv", K, C * D), ("bq", 128, HT), ("bk", 128, HT),
            ("bv", L, D), ("g", K, C), ("b", K, C), ("wo", K, C * D), ("bo", L, D)],
}


def offsets(pack):
    at, where = 0, {}
    for name, rows, cols in PACKS[pack]:
        where[name] = (rows, at, cols)
        at += cols
    return where, at


class Fields:

    def __init__(self, tile, pack):
        self.tile, self.where = tile, offsets(pack)[0]

    def at(self, name, groups=1):
        rows, start, cols = self.where[name]
        view = self.tile[0:rows, start:start + cols]
        return view if groups == 1 else view.rearrange("p (a n) -> p a n", a=groups)


class Steps:

    def __init__(self, eng, sem, before=0):
        self.eng, self.sem, self.before, self.n = eng, sem, before, 0

    def done(self, ins):
        ins.then_inc(self.sem, 1)
        self.n += 1

    def wait(self):
        self.eng.wait_ge(self.sem, self.before + self.n)


SEM_BANK = 72


class Memory:

    def __init__(self, nc, g, stack, phase):
        self.nc, self.stack, self.phase = nc, stack, phase
        self.bank = g["sem_banks"][g["phases"] % 2]
        g["phases"] += 1
        self.used = []
        stack.callback(self.retire)

    def retire(self):
        for sem in self.used:
            self.nc.release_semaphore(sem)
        if self.used:
            self.nc.sync.sem_clear(range(self.bank[0], self.bank[0] + len(self.used)))

    def sb(self, name, shape, dt=F32):
        return self.stack.enter_context(self.nc.sbuf_tensor(f"{self.phase}_{name}", shape, dt))

    def sem(self, name):
        handle = self.nc.alloc_semaphore(f"{self.phase}_{name}", self.bank[len(self.used)])
        self.used.append(handle)
        return handle


def embed(nc, g, dram):
    with ExitStack() as stack:
        m = Memory(nc, g, stack, "tok")
        width = offsets("tok")[1]
        pack = m.sb("pack", [128, width])
        f = Fields(pack, "tok")
        emb = m.sb("emb", [GB * NP, G, D])
        bias = m.sb("bias", [GB * NP, D])
        loaded, txt_loaded, moved = m.sem("loaded"), m.sem("txt_loaded"), m.sem("moved")
        bias_ready, emb_ps, emb_ready = m.sem("bias_ready"), m.sem("emb_ps"), m.sem("emb_ready")
        w = f.at("conv_w", CONV_K)
        x = f.at("patches", CONV_K)
        ps = g["ps"]

        block = stack.enter_context(nc.Block())

        @block.sync
        def _(sp):
            sp.dma_start(pack[:, :], dram["pack_tok"]).then_inc(loaded, 16)
            sp.dma_start(g["h"][NP:L, 0:B, :], dram["txt"].rearrange("b t d -> t b d")).then_inc(txt_loaded, 16)
            for name in PACKS:
                if name != "tok":
                    sp.dma_start(g["pack_" + name][:, :], dram["pack_" + name]).then_inc(g["packs_loaded"], 16)
            for q in range(G):
                sp.wait_ge(emb_ready, q + 1)
                for j in range(GB):
                    sp.dma_start(g["h"][0:NP, q * GB + j, :], emb[j * NP:(j + 1) * NP, q, :]).then_inc(moved, 16)
            sp.wait_ge(moved, 16 * B)
            sp.wait_ge(txt_loaded, 16)
            sp.wait_ge(g["packs_loaded"], 16 * (len(PACKS) - 1))

        @block.gpsimd
        def _(pool):
            pool.memset(g["h"][:, B:B + 4, :], 0.0)

        @block.tensor
        def _(pe):
            pe.wait_ge(loaded, 16)
            for q in range(G):
                for k in range(CONV_K):
                    last = pe.matmul(ps[0:GB * NP, 0, q, 0:D], x[:, k, q * GB * NP:(q + 1) * GB * NP], w[:, k, :],
                                     start=(k == 0), stop=(k == CONV_K - 1))
                last.then_inc(emb_ps, 1)

        @block.vector
        def _(dve):
            dve.wait_ge(loaded, 16)
            dve.tensor_tensor(bias[:, :], f.at("pos"), f.at("conv_b"), ALU.add).then_inc(bias_ready, 1)
            dve.wait_ge(bias_ready, 1)
            for q in range(G):
                dve.wait_ge(emb_ps, q + 1)
                dve.tensor_tensor(emb[:, q, :], ps[0:GB * NP, 0, q, 0:D], bias[:, :], ALU.add).then_inc(emb_ready, 1)


class Norm:

    def __init__(self, m, g, name, per_iter=1):
        self.stats = m.sb(name + "_stats", [L, 2, 6])
        self.moments = m.sb(name + "_moments", [L, 2, 2])
        self.shifted = m.sb(name + "_shifted", [L, 2])
        self.rstd = m.sb(name + "_rstd", [L, 2])
        self.pause = m.sb(name + "_pause", [1, 1])
        self.neg_half = g["const"].at("neg_half")
        self.var_ready, self.rstd_ready = m.sem(name + "_var_ready"), m.sem(name + "_rstd_ready")

    def vector(self, dve, i, steps, src, dst):
        for j in range(2):
            steps.done(dve.bn_stats(self.stats[:, j, :], src[j]))
        steps.wait()
        dve.memset(self.pause[:, :], 0.0)
        for j in range(2):
            steps.done(dve.bn_aggr(self.moments[:, j, :], self.stats[:, j, :]))
        steps.wait()
        dve.tensor_scalar(self.shifted[:, :], self.moments[:, :, 1], EPS, None, ALU.add).then_inc(self.var_ready, 1)
        dve.wait_ge(self.rstd_ready, i + 1)
        return [dve.tensor_scalar(dst[j], src[j], self.moments[:, j, 0:1], self.rstd[:, j:j + 1],
                                  ALU.subtract, ALU.mult) for j in range(2)]

    def pool(self, pool, i):
        pool.wait_ge(self.var_ready, i + 1)
        pool.tensor_tensor(self.rstd[:, :], self.shifted[:, :], self.neg_half, ALU.pow).then_inc(self.rstd_ready, 1)


def retention(nc, g):
    w = g["l0a"]
    wq, wk, wv = w.at("wq", C), w.at("wk", C), w.at("wv", C)
    ident = g["const"].at("ident")
    ps, h = g["ps"], g["h"]
    with ExitStack() as stack:
        m = Memory(nc, g, stack, "ret")
        norm = Norm(m, g, "norm")
        z = m.sb("z", [L, 2, D])
        xT = m.sb("xT", [K, 2, C, L])
        qT = m.sb("qT", [K, 2, C, L])
        kT = m.sb("kT", [K, 2, C, L])
        v = m.sb("v", [L, 2, D])
        sT = m.sb("sT", [L, 2, L])
        dve_steps = m.sem("dve_steps")
        z_ready, xT_ps, xT_ready = m.sem("z_ready"), m.sem("xT_ps"), m.sem("xT_ready")
        qkv_ps, qk_ready, v_ready = m.sem("qkv_ps"), m.sem("qk_ready"), m.sem("v_ready")
        s_ps, s_ready, o_ps = m.sem("s_ps"), m.sem("s_ready"), m.sem("o_ps")
        block = stack.enter_context(nc.Block())

        @block.tensor
        def _(pe):
            with pe.Fori(0, B // 2) as i:
                for j in range(2):
                    pe.wait_ge(z_ready, 2 * i + j + 1)
                    for c in range(C):
                        last = pe.transpose(ps[0:K, j, 3, c * L:(c + 1) * L], z[:, j, c * K:(c + 1) * K],
                                            ident[0:L, 0:L])
                    last.then_inc(xT_ps, 1)
                for j in range(2):
                    pe.wait_ge(xT_ready, 2 * i + j + 1)
                    for bank, wt in ((0, wq), (1, wk)):
                        for co in range(C):
                            for c in range(C):
                                pe.matmul(ps[0:K, j, bank, co * L:(co + 1) * L], wt[:, c, co * K:(co + 1) * K],
                                          xT[:, j, c, :], start=(c == 0), stop=(c == C - 1))
                    for c in range(C):
                        last = pe.matmul(ps[0:L, j, 2, 0:D], xT[:, j, c, :], wv[:, c, :],
                                         start=(c == 0), stop=(c == C - 1))
                    last.then_inc(qkv_ps, 1)
                for j in range(2):
                    pe.wait_ge(qk_ready, 2 * i + j + 1)
                    for c in range(C):
                        last = pe.matmul(ps[0:L, j, 3, 0:L], kT[:, j, c, :], qT[:, j, c, :],
                                         start=(c == 0), stop=(c == C - 1))
                    last.then_inc(s_ps, 1)
                for j in range(2):
                    pe.wait_ge(s_ready, 2 * i + j + 1)
                    pe.wait_ge(v_ready, 2 * i + j + 1)
                    pe.matmul(ps[0:L, j, 0, 0:D], sT[:, j, :], v[:, j, :], start=True, stop=True).then_inc(o_ps, 1)

        @block.scalar
        def _(act):
            with act.Fori(0, B // 2) as i:
                for j in range(2):
                    act.wait_ge(xT_ps, 2 * i + j + 1)
                    act.activation(xT[:, j, :, :], ps[0:K, j, 3, 0:C * L].rearrange("p (c n) -> p c n", c=C),
                                   ACT.Copy).then_inc(xT_ready, 1)
                for j in range(2):
                    act.wait_ge(qkv_ps, 2 * i + j + 1)
                    for bank, dst, bias in ((0, qT, w.at("bq")), (1, kT, w.at("bk"))):
                        for c in range(C):
                            last = act.activation(dst[:, j, c, :], ps[0:K, j, bank, c * L:(c + 1) * L],
                                                  ACT.Identity, bias=bias[:, c:c + 1])
                    last.then_inc(qk_ready, 1)

        @block.gpsimd
        def _(pool):
            with pool.Fori(0, B // 2) as i:
                norm.pool(pool, i)

        @block.vector
        def _(dve):
            own = 4
            with dve.Fori(0, B // 2) as i:
                steps = Steps(dve, dve_steps, own * i)
                for ins in norm.vector(dve, i, steps, [h[:, ds(2 * i + j, 1), :] for j in range(2)],
                                       [z[:, j:j + 1, :] for j in range(2)]):
                    ins.then_inc(z_ready, 1)
                for j in range(2):
                    dve.wait_ge(qkv_ps, 2 * i + j + 1)
                    dve.tensor_tensor(v[:, j, :], ps[0:L, j, 2, 0:D], w.at("bv"), ALU.add).then_inc(v_ready, 1)
                for j in range(2):
                    dve.wait_ge(s_ps, 2 * i + j + 1)
                    dve.tensor_tensor(sT[:, j, :], ps[0:L, j, 3, 0:L], w.at("decay"), ALU.mult).then_inc(s_ready, 1)
                for j in range(2):
                    dve.wait_ge(o_ps, 2 * i + j + 1)
                    dve.tensor_tensor(h[:, ds(2 * i + j, 1), :], h[:, ds(2 * i + j, 1), :],
                                      ps[0:L, j, 0:1, 0:D], ALU.add)
                assert steps.n == own


def softmax_attention(nc, g, phase, residual, mask=None, conv=False, project=True):
    w = g[phase]
    wq, wk, wv = w.at("wq", C), w.at("wk", C), w.at("wv", C)
    ident = g["const"].at("ident")
    ps, h, x = g["ps"], g["h"], g.get("x")
    two_norms = residual != "plain"
    gated = residual == "gated"
    ahead = 1 if gated else 2
    with ExitStack() as stack:
        m = Memory(nc, g, stack, phase)
        norm = Norm(m, g, "norm")
        norm2 = Norm(m, g, "norm2") if two_norms else None
        z = m.sb("z", [L, 2, D])
        xT = m.sb("xT", [K, 2, C, L])
        qT = m.sb("qT", [128, 2, HT, L])
        k_apart = m.sb("k_apart", [128, 2, HT, RG, L])
        if conv:
            kT = m.sb("kT", [128, 2, HT, L])
            side = m.sb("side", [128, 2, 2, HT, L])
            q2 = m.sb("q2", [128, 2, HT, L])
            k2 = m.sb("k2", [128, 2, HT, L])
        v = m.sb("v", [L, 2, H, HP])
        head_oT = m.sb("head_oT", [128, 2, HT, L])
        top = m.sb("top", [L, 2, H])
        p = m.sb("p", [L, 2, HT, RG, L])
        pT = m.sb("pT", [L, 2, HT, RG, L])
        rsum = m.sb("rsum", [L, 2, H])
        o = m.sb("o", [L, 2, D])
        if mask:
            mask_bf = m.sb("mask_bf", [L, RG, L], BF16)
            ident_bf = m.sb("ident_bf", [L, L], BF16)
        if project:
            oT = m.sb("oT", [K, 2, C, L])
            y = m.sb("y", [L, 2, D])
        if gated:
            lin_x = m.sb("lin_x", [K, 2, 2 * C, L])
            lin_e = m.sb("lin_e", [K, 2, 2 * C, L])
            lin_f = m.sb("lin_f", [K, 2, 2 * C, L])
            lin_v = m.sb("lin_v", [L, 2, D + 1])
            lin_s = m.sb("lin_s", [L, 2, L])
            lin_d = m.sb("lin_d", [L, 2])
            lin_o = m.sb("lin_o", [L, 2, D])
            mixT = m.sb("mixT", [K, 2, 2 * C, L])
            hidT = m.sb("hidT", [K, 2, C, L])
            gate = m.sb("gate", [L, 2, D])
            diff = m.sb("diff", [L, 2, D])
            fused = m.sb("fused", [L, 2, D])
            lin_ps, lin_x_ready, lin_m_ready = m.sem("lin_ps"), m.sem("lin_x_ready"), m.sem("lin_m_ready")
            lin_e_ready, lin_f_ready, lin_v_ready = m.sem("lin_e_ready"), m.sem("lin_f_ready"), m.sem("lin_v_ready")
            lin_s_ps, lin_s_ready, lin_o_ps = m.sem("lin_s_ps"), m.sem("lin_s_ready"), m.sem("lin_o_ps")
            lin_o_ready, mixT_ps, mixT_ready = m.sem("lin_o_ready"), m.sem("mixT_ps"), m.sem("mixT_ready")
            hid_ps, hid_ready, gate_ps = m.sem("hid_ps"), m.sem("hid_ready"), m.sem("gate_ps")
            gate_in, gate_exp, fused_ready = m.sem("gate_in"), m.sem("gate_exp"), m.sem("fused_ready")
        dve_steps, const_ready = m.sem("dve_steps"), m.sem("const_ready")
        enter_steps, k_ready = m.sem("enter_steps"), m.sem("k_ready")
        top_ready, head_oT_ps, head_oT_ready = m.sem("top_ready"), m.sem("head_oT_ps"), m.sem("head_oT_ready")
        z_ready, xT_ps, xT_ready = m.sem("z_ready"), m.sem("xT_ps"), m.sem("xT_ready")
        qkv_ps, qk_ready, v_ready = m.sem("qkv_ps"), m.sem("qk_ready"), m.sem("v_ready")
        mixed_ready, left_added = m.sem("mixed_ready"), m.sem("left_added")
        s_ps, below_ready, p_ready = m.sem("s_ps"), m.sem("below_ready"), m.sem("p_ready")
        pT_ps, pT_ready, o_ps, o_ready = m.sem("pT_ps"), m.sem("pT_ready"), m.sem("o_ps"), m.sem("o_ready")
        oT_ps, oT_ready, y_ps = m.sem("oT_ps"), m.sem("oT_ready"), m.sem("y_ps")
        block = stack.enter_context(nc.Block())

        def banked(j):
            return ps[0:L, j, 0:HT, 0:RG * L].rearrange("p t (r n) -> p t r n", r=RG)

        def zT_at(j):
            return ps[0:K, j, 2, D:D + C * L]

        def head_oT_at(j):
            return ps[:, j, 0 if gated else 3, 0:HT * L].rearrange("p (t n) -> p t n", t=HT)

        def o_at(j):
            return ps[0:L, j, 0 if gated else 3, 0:HT * 128]

        def oT_at(j):
            return ps[0:K, j, 1 if gated else 3, 0:C * L]

        def y_at(j):
            return ps[0:L, j, 3, C * L:C * L + D]

        @block.tensor
        def _(pe):
            def transposes(n, j):
                pe.wait_ge(z_ready, 2 * n + j + 1)
                for c in range(C):
                    last = pe.transpose(zT_at(j)[:, c * L:(c + 1) * L], z[:, j, c * K:(c + 1) * K],
                                        ident[0:L, 0:L])
                last.then_inc(xT_ps, 1)

            def qkv(n, j):
                pe.wait_ge(xT_ready, 2 * n + j + 1)
                for bank, wt in ((0, wq), (1, wk)):
                    for t in range(HT):
                        for c in range(C):
                            pe.matmul(ps[:, j, bank, t * L:(t + 1) * L], wt[:, c, t * 128:(t + 1) * 128],
                                      xT[:, j, c, :], start=(c == 0), stop=(c == C - 1))
                for c in range(C):
                    last = pe.matmul(ps[0:L, j, 2, 0:D], xT[:, j, c, :], wv[:, c, :],
                                     start=(c == 0), stop=(c == C - 1))
                last.then_inc(qkv_ps, 1)

            def out_transposes(i, j):
                out_src, out_ready = (fused, fused_ready) if gated else (o, o_ready)
                pe.wait_ge(out_ready, 2 * i + j + 1)
                for c in range(C):
                    last = pe.transpose(oT_at(j)[:, c * L:(c + 1) * L], out_src[:, j, c * K:(c + 1) * K],
                                        ident[0:L, 0:L])
                last.then_inc(oT_ps, 1)

            def out_products(i, j):
                pe.wait_ge(oT_ready, 2 * i + j + 1)
                for c in range(C):
                    last = pe.matmul(y_at(j), oT[:, j, c, :], w.at("wo", C)[:, c, :],
                                     start=(c == 0), stop=(c == C - 1))
                last.then_inc(y_ps, 1)

            def scores(n, j):
                if not conv:
                    pe.wait_ge(qk_ready, 2 * n + j + 1)
                pe.wait_ge(k_ready, 2 * n + j + 1)
                pe.wait_ge(v_ready, 2 * n + j + 1)
                if mask:
                    for t in range(HT):
                        pe.matmul(ps[0:L, j, t, 0:RG * L], ident_bf[:, :],
                                  mask_bf[:, :, :].rearrange("p r n -> p (r n)"),
                                  start=True, stop=False, skip_group_check=True)
                qs = q2 if conv else qT
                for t in range(HT):
                    last = pe.matmul(ps[0:L, j, t, 0:RG * L], qs[:, j, t, :],
                                     k_apart[:, j, t, :, :].rearrange("p r n -> p (r n)"), start=not mask,
                                     stop=True, skip_group_check=bool(mask))
                last.then_inc(s_ps, 1)

            def turn(i, j):
                pe.wait_ge(p_ready, 2 * i + j + 1)
                for t in range(HT):
                    for r in range(RG):
                        last = pe.transpose(ps[0:L, j, t, r * L:(r + 1) * L], p[:, j, t, r, :], ident[0:L, 0:L])
                last.then_inc(pT_ps, 1)

            def outputs(i, j):
                pe.wait_ge(pT_ready, 2 * i + j + 1)
                for t in range(HT):
                    for r in range(RG):
                        last = pe.matmul(head_oT_at(j)[HP * r:HP * (r + 1), t, :], v[:, j, HT * r + t, :],
                                         pT[:, j, t, r, :], start=True, stop=True, tile_position=(0, HP * r))
                last.then_inc(head_oT_ps, 1)

            def outputs_back(i, j):
                pe.wait_ge(head_oT_ready, 2 * i + j + 1)
                for t in range(HT):
                    last = pe.transpose(o_at(j)[:, t * 128:(t + 1) * 128], head_oT[:, j, t, :], ident[:, :])
                last.then_inc(o_ps, 1)

            for j in range(2):
                transposes(0, j)
            for j in range(2):
                qkv(0, j)
            pe.wait_ge(const_ready, 3 if mask else 1)
            if not gated:
                scores(0, 0)
                turn(0, 0)
            with pe.Fori(0, B // 2) as i:
                if not gated:
                    for j in range(2):
                        scores(i + j, 1 - j)
                        outputs(i, j)
                        transposes(i + 1, j)
                        outputs_back(i, j)
                        qkv(i + 1, j)
                        if project:
                            out_transposes(i, j)
                        turn(i + j, 1 - j)
                        if project:
                            out_products(i, j)
                else:
                    for j in range(2):
                        scores(i, j)
                    for j in range(2):
                        turn(i, j)
                    for j in range(2):
                        outputs(i, j)
                        for bank, wt in ((1, "lin_wq"), (2, "lin_wk")):
                            for co in range(C):
                                for c in range(C):
                                    pe.matmul(ps[0:K, j, bank, co * L:(co + 1) * L],
                                              w.at(wt, C)[:, c, co * K:(co + 1) * K], xT[:, j, c, :],
                                              start=(c == 0), stop=(c == C - 1))
                        for c in range(C):
                            last = pe.matmul(ps[0:L, j, 3, 0:D], xT[:, j, c, :], w.at("lin_wv", C)[:, c, :],
                                             start=(c == 0), stop=(c == C - 1))
                        last.then_inc(lin_ps, 1)
                    for j in range(2):
                        outputs_back(i, j)
                if gated:
                    for j in range(2):
                        pe.wait_ge(lin_f_ready, 2 * i + j + 1)
                        for c in range(C):
                            last = pe.matmul(ps[0:L, j, 1, 0:L], lin_f[:, j, C + c, :], lin_f[:, j, c, :],
                                             start=(c == 0), stop=(c == C - 1))
                        last.then_inc(lin_s_ps, 1)
                    for j in range(2):
                        pe.wait_ge(lin_s_ready, 2 * i + j + 1)
                        pe.wait_ge(lin_v_ready, 2 * i + j + 1)
                        pe.matmul(ps[0:L, j, 2, 0:D + 1], lin_s[:, j, :], lin_v[:, j, :], start=True, stop=True)\
                          .then_inc(lin_o_ps, 1)
                    for j in range(2):
                        pe.wait_ge(lin_o_ready, 2 * i + j + 1)
                        pe.wait_ge(o_ready, 2 * i + j + 1)
                        for n, src in ((0, lin_o), (1, o)):
                            for c in range(C):
                                last = pe.transpose(ps[0:K, j, 3, (n * C + c) * L:(n * C + c + 1) * L],
                                                    src[:, j, c * K:(c + 1) * K], ident[0:L, 0:L])
                        last.then_inc(mixT_ps, 1)
                    for j in range(2):
                        pe.wait_ge(mixT_ready, 2 * i + j + 1)
                        gate_in_T = [mixT[:, j, n, :] for n in range(2 * C)] + [xT[:, j, c, :] for c in range(C)]
                        for co in range(C):
                            for n, part in enumerate(gate_in_T):
                                last = pe.matmul(ps[0:K, j, 0, co * L:(co + 1) * L],
                                                 w.at("wg1", 3 * C)[:, n, co * K:(co + 1) * K], part,
                                                 start=(n == 0), stop=(n == 3 * C - 1))
                        last.then_inc(hid_ps, 1)
                    for j in range(2):
                        pe.wait_ge(hid_ready, 2 * i + j + 1)
                        for c in range(C):
                            last = pe.matmul(ps[0:L, j, 1, 0:D], hidT[:, j, c, :], w.at("wg2", C)[:, c, :],
                                             start=(c == 0), stop=(c == C - 1))
                        last.then_inc(gate_ps, 1)
                    for j in range(2):
                        out_transposes(i, j)
                    for j in range(2):
                        out_products(i, j)
                    for j in range(2):
                        transposes(i + 1, j)
                    for j in range(2):
                        qkv(i + 1, j)

        @block.scalar
        def _(act):
            def xT_copies(n, j):
                act.wait_ge(xT_ps, 2 * n + j + 1)
                if two_norms:
                    for c in range(C):
                        last = act.activation(xT[:, j, c, :], zT_at(j)[:, c * L:(c + 1) * L], ACT.Identity,
                                              scale=w.at("g")[:, c:c + 1], bias=w.at("b")[:, c:c + 1])
                else:
                    last = act.activation(xT[:, j, :, :].rearrange("p c n -> p (c n)"), zT_at(j), ACT.Copy)
                last.then_inc(xT_ready, 1)

            def qk_copies(n, j):
                act.wait_ge(qkv_ps, 2 * n + j + 1)
                for bank, dst, bias in ((0, qT, "bq"), (1, kT, "bk")) if conv else ((0, qT, "bq"),):
                    if bias in w.where:
                        for t in range(HT):
                            last = act.activation(dst[:, j, t, :], ps[:, j, bank, t * L:(t + 1) * L],
                                                  ACT.Identity, bias=w.at(bias)[:, t:t + 1])
                    else:
                        last = act.activation(dst[:, j, :, :].rearrange("p t n -> p (t n)"),
                                              ps[:, j, bank, 0:HT * L], ACT.Copy)
                last.then_inc(qk_ready, 1)

            def k_copies(n, j):
                act.wait_ge(mixed_ready, 2 * n + j + 1)
                for r in range(RG):
                    rows = slice(HP * r, HP * (r + 1))
                    last = act.activation(k_apart[rows, j, :, r, :], k2[rows, j, :, :], ACT.Copy)
                last.then_inc(k_ready, 1)

            def oT_copies(i, j):
                act.wait_ge(oT_ps, 2 * i + j + 1)
                act.activation(oT[:, j, :, :].rearrange("p c n -> p (c n)"), oT_at(j), ACT.Copy)\
                   .then_inc(oT_ready, 1)

            def exponentials(n, j):
                act.wait_ge(below_ready, 2 * n + j + 1)
                act.activation(p[:, j, :, :, :], p[:, j, :, :, :], ACT.Exp, scale=HD ** -0.5).then_inc(p_ready, 1)

            def pT_copies(i, j):
                act.wait_ge(pT_ps, 2 * i + j + 1)
                act.activation(pT[:, j, :, :, :], banked(j), ACT.Copy).then_inc(pT_ready, 1)

            def head_oT_copies(i, j):
                act.wait_ge(head_oT_ps, 2 * i + j + 1)
                act.activation(head_oT[:, j, :, :], head_oT_at(j), ACT.Copy).then_inc(head_oT_ready, 1)

            for j in range(2):
                xT_copies(0, j)
            if conv:
                act.wait_ge(const_ready, 1)
            for j in range(2):
                qk_copies(0, j)
            if conv:
                for j in range(2):
                    k_copies(0, j)
            if not gated:
                exponentials(0, 0)
                pT_copies(0, 0)
            with act.Fori(0, B // 2) as i:
                if not gated:
                    for j in range(2):
                        head_oT_copies(i, j)
                        xT_copies(i + 1, j)
                        exponentials(i + j, 1 - j)
                        qk_copies(i + 1, j)
                        if project:
                            oT_copies(i, j)
                        if conv:
                            k_copies(i + 1, j)
                        pT_copies(i + j, 1 - j)
                else:
                    for j in range(2):
                        exponentials(i, j)
                    for j in range(2):
                        pT_copies(i, j)
                    for j in range(2):
                        head_oT_copies(i, j)
                if gated:
                    for j in range(2):
                        act.wait_ge(lin_ps, 2 * i + j + 1)
                        for n, bias in ((0, "lin_bq"), (1, "lin_bk")):
                            for c in range(C):
                                last = act.activation(lin_x[:, j, n * C + c, :], ps[0:K, j, 1 + n, c * L:(c + 1) * L],
                                                      ACT.Identity, bias=w.at(bias)[:, c:c + 1])
                        last.then_inc(lin_x_ready, 1)
                    for j in range(2):
                        act.wait_ge(lin_m_ready, 2 * i + j + 1)
                        act.activation(lin_e[:, j, :, :], lin_e[:, j, :, :], ACT.Exp).then_inc(lin_e_ready, 1)
                    for j in range(2):
                        act.wait_ge(lin_s_ps, 2 * i + j + 1)
                        act.activation(lin_s[:, j, :], ps[0:L, j, 1, 0:L], ACT.Copy).then_inc(lin_s_ready, 1)
                    for j in range(2):
                        act.wait_ge(mixT_ps, 2 * i + j + 1)
                        act.activation(mixT[:, j, :, :].rearrange("p c n -> p (c n)"), ps[0:K, j, 3, 0:2 * C * L],
                                       ACT.Copy).then_inc(mixT_ready, 1)
                    for j in range(2):
                        act.wait_ge(hid_ps, 2 * i + j + 1)
                        for c in range(C):
                            last = act.activation(hidT[:, j, c, :], ps[0:K, j, 0, c * L:(c + 1) * L], ACT.Relu,
                                                  bias=w.at("bg1")[:, c:c + 1])
                        last.then_inc(hid_ready, 1)
                    for j in range(2):
                        act.wait_ge(gate_in, 2 * i + j + 1)
                        act.activation(gate[:, j, :], gate[:, j, :], ACT.Exp, scale=-1.0).then_inc(gate_exp, 1)
                    for j in range(2):
                        oT_copies(i, j)
                    for j in range(2):
                        xT_copies(i + 1, j)
                    for j in range(2):
                        qk_copies(i + 1, j)

        @block.gpsimd
        def _(pool):
            if gated:
                pool.memset(lin_v[:, :, :], 1.0)
            pool.memset(k_apart[:, :, :, :, :], 0.0)
            pool.memset(v[:, :, :, 0:HD + 1], 1.0)
            pool.memset(v[:, :, :, HD + 1:HP], 0.0).then_inc(const_ready, 1)
            for n in range(ahead):
                norm.pool(pool, n)
                if two_norms:
                    norm2.pool(pool, n)
            with pool.Fori(0, B // 2) as i:
                norm.pool(pool, i + ahead)
                if two_norms:
                    norm2.pool(pool, i + ahead)

        @block.vector
        def _(dve):
            if mask:
                for r in range(RG):
                    last = dve.tensor_copy(mask_bf[:, r, :], w.at(mask))
                last.then_inc(const_ready, 1)
                dve.tensor_copy(ident_bf[:, :], ident[0:L, 0:L]).then_inc(const_ready, 1)
            enter_own = 4 + 6 * two_norms + 4 * conv

            def first_norm(n, steps):
                tile = [ds(2 * n + j, 1) for j in range(2)]
                for ins in norm.vector(dve, n, steps, [h[:, tile[j], :] for j in range(2)],
                                       [x[:, tile[j], :] for j in range(2)]):
                    steps.done(ins)

            def last_norm(n, steps):
                tile = [ds(2 * n + j, 1) for j in range(2)]
                if two_norms:
                    steps.wait()
                    dve.memset(norm2.pause[:, :], 0.0)
                for ins in (norm2 if two_norms else norm).vector(
                        dve, n, steps, [(x if two_norms else h)[:, tile[j], :] for j in range(2)],
                        [z[:, j:j + 1, :] for j in range(2)]):
                    ins.then_inc(z_ready, 1)

            def values_and_keys(n, j, steps):
                dve.wait_ge(qkv_ps, 2 * n + j + 1)
                if not conv:
                    keys = ps[:, j, 1, 0:HT * L].rearrange("p (t n) -> p t n", t=HT)
                    for r in range(RG):
                        rows = slice(HP * r, HP * (r + 1))
                        if "bk" in w.where:
                            bias = w.at("bk")[rows, :].unsqueeze(2).broadcast_to([HP, HT, L])
                            last = dve.tensor_tensor(k_apart[rows, j, :, r, :], keys[rows, :, :], bias, ALU.add)
                        else:
                            last = dve.tensor_copy(k_apart[rows, j, :, r, :], keys[rows, :, :])
                    last.then_inc(k_ready, 1)
                heads = ps[0:L, j, 2, 0:D].rearrange("p (a n) -> p a n", a=H)
                if "bv" in w.where:
                    last = dve.tensor_tensor(v[:, j, :, 0:HD], heads, w.at("bv", H), ALU.add)
                else:
                    last = dve.tensor_copy(v[:, j, :, 0:HD], heads)
                last.then_inc(v_ready, 1)
                if conv:
                    dve.wait_ge(qk_ready, 2 * n + j + 1)
                    for a, src, dst, own_w, side_w in ((0, qT, q2, 0, 1), (1, kT, k2, 2, 3)):
                        mix = w.at("mix")
                        dve.tensor_scalar(side[:, j, a, :, :], src[:, j, :, :], mix[:, side_w:side_w + 1], None,
                                          ALU.mult)
                        steps.done(dve.tensor_scalar(dst[:, j, :, :], src[:, j, :, :], mix[:, own_w:own_w + 1],
                                                     None, ALU.mult))
                    steps.wait()
                    for a, dst in ((0, q2), (1, k2)):
                        left = dve.tensor_tensor(dst[:, j, :, 1:L], dst[:, j, :, 1:L], side[:, j, a, :, 0:L - 1],
                                                 ALU.add)
                    left.then_inc(left_added, 1)
                    dve.wait_ge(left_added, 2 * n + j + 1)
                    for a, dst in ((0, q2), (1, k2)):
                        last = dve.tensor_tensor(dst[:, j, :, 0:L - 1], dst[:, j, :, 0:L - 1],
                                                 side[:, j, a, :, 1:L], ALU.add)
                    last.then_inc(mixed_ready, 1)

            entering = Steps(dve, enter_steps)
            if two_norms:
                first_norm(0, entering)
            last_norm(0, entering)
            dve.wait_ge(const_ready, 3 if mask else 1)
            for j in range(2):
                values_and_keys(0, j, entering)

            def below_maximum(n, j):
                dve.wait_ge(s_ps, 2 * n + j + 1)
                peaks = top[:, j, :].rearrange("p (t r) -> p t r", t=HT)
                dve.tensor_reduce(peaks, banked(j), AX.X, ALU.max).then_inc(top_ready, 1)
                dve.wait_ge(top_ready, 2 * n + j + 1)
                dve.tensor_tensor(p[:, j, :, :, :], banked(j), peaks.unsqueeze(3).broadcast_to([L, HT, RG, L]),
                                  ALU.subtract).then_inc(below_ready, 1)

            def divide(i, j, steps):
                dve.wait_ge(o_ps, 2 * i + j + 1)
                heads = o_at(j).rearrange("p (t r n) -> p t r n", t=HT, r=RG)
                sums = rsum[:, j, :].rearrange("p (t r) -> p t r", t=HT)
                steps.done(dve.reciprocal(sums.unsqueeze(3), heads[:, :, :, HD:HD + 1]))
                steps.wait()
                dve.tensor_tensor(o[:, j, :].rearrange("p (r t n) -> p t r n", r=RG, t=HT), heads[:, :, :, 0:HD],
                                  sums.unsqueeze(3).broadcast_to([L, HT, RG, HD]), ALU.mult).then_inc(o_ready, 1)

            def add_up(i, j, steps):
                tile = ds(2 * i + j, 1)
                if project:
                    dve.wait_ge(y_ps, 2 * i + j + 1)
                    steps.done(dve.tensor_tensor(y[:, j, :], y_at(j), w.at("bo"), ALU.add))
                    steps.wait()
                    add = y[:, j:j + 1, :]
                else:
                    dve.wait_ge(o_ready, 2 * i + j + 1)
                    add = o[:, j:j + 1, :]
                if gated:
                    steps.done(dve.tensor_tensor(y[:, j:j + 1, :], y[:, j:j + 1, :], x[:, tile, :], ALU.add))
                    steps.wait()
                if residual == "normed":
                    dve.tensor_tensor(x[:, tile, :], x[:, tile, :], add, ALU.add)
                else:
                    dve.tensor_tensor(h[:, tile, :], h[:, tile, :], add, ALU.add)

            own = 2 + 2 * project + 14 * gated
            if not gated:
                if two_norms:
                    first_norm(1, entering)
                last_norm(1, entering)
                below_maximum(0, 0)
            entered = entering.n
            with dve.Fori(0, B // 2) as i:
                steps = Steps(dve, dve_steps, own * i)
                entering = Steps(dve, enter_steps, enter_own * i + entered)
                if not gated:
                    for j in range(2):
                        below_maximum(i + j, 1 - j)
                        divide(i, j, steps)
                        if two_norms and j == 0:
                            first_norm(i + 2, entering)
                        values_and_keys(i + 1, j, entering)
                        if j == 1:
                            last_norm(i + 2, entering)
                        add_up(i, j, steps)
                else:
                    for j in range(2):
                        below_maximum(i, j)
                    first_norm(i + 1, entering)
                    last_norm(i + 1, entering)
                    for j in range(2):
                        divide(i, j, steps)
                if gated:
                    for j in range(2):
                        dve.wait_ge(lin_x_ready, 2 * i + j + 1)
                        dve.tensor_scalar(lin_e[:, j, :, :], lin_x[:, j, :, :], 0.0, None, ALU.min)\
                           .then_inc(lin_m_ready, 1)
                        dve.wait_ge(lin_ps, 2 * i + j + 1)
                        dve.tensor_tensor(lin_v[:, j, 0:D], ps[0:L, j, 3, 0:D], w.at("lin_bv"), ALU.add)\
                           .then_inc(lin_v_ready, 1)
                    for j in range(2):
                        dve.wait_ge(lin_e_ready, 2 * i + j + 1)
                        dve.scalar_tensor_tensor(lin_f[:, j, :, :], lin_x[:, j, :, :], 0.0, lin_e[:, j, :, :],
                                                 ALU.max, ALU.add).then_inc(lin_f_ready, 1)
                    for j in range(2):
                        dve.wait_ge(lin_o_ps, 2 * i + j + 1)
                        steps.done(dve.tensor_scalar(lin_d[:, j:j + 1], ps[0:L, j, 2, D:D + 1], 1e-6, None, ALU.add))
                        steps.wait()
                        steps.done(dve.reciprocal(lin_d[:, j:j + 1], lin_d[:, j:j + 1]))
                        steps.wait()
                        dve.tensor_scalar(lin_o[:, j, :], ps[0:L, j, 2, 0:D], lin_d[:, j:j + 1], None, ALU.mult)\
                           .then_inc(lin_o_ready, 1)
                    for j in range(2):
                        dve.wait_ge(lin_o_ready, 2 * i + j + 1)
                        steps.done(dve.tensor_tensor(diff[:, j, :], lin_o[:, j, :], o[:, j, :], ALU.subtract))
                    for j in range(2):
                        dve.wait_ge(gate_ps, 2 * i + j + 1)
                        dve.tensor_tensor(gate[:, j, :], ps[0:L, j, 1, 0:D], w.at("bg2"), ALU.add)\
                           .then_inc(gate_in, 1)
                    for j in range(2):
                        dve.wait_ge(gate_exp, 2 * i + j + 1)
                        steps.done(dve.tensor_scalar(gate[:, j, :], gate[:, j, :], 1.0, None, ALU.add))
                        steps.wait()
                        steps.done(dve.reciprocal(gate[:, j, :], gate[:, j, :]))
                        steps.wait()
                        steps.done(dve.tensor_tensor(diff[:, j, :], diff[:, j, :], gate[:, j, :], ALU.mult))
                        steps.wait()
                        dve.tensor_tensor(fused[:, j, :], diff[:, j, :], o[:, j, :], ALU.add)\
                           .then_inc(fused_ready, 1)
                    for j in range(2):
                        add_up(i, j, steps)
                    for j in range(2):
                        values_and_keys(i + 1, j, entering)
                assert steps.n == own and entering.n == enter_own, (steps.n, entering.n)


def route(nc, g, phase, two_norms):
    w = g[phase]
    ident, iota = g["const"].at("ident"), g["const"].at("iota")[:, 0:E01]
    bias = "b2" in w.where
    ps, h, x, xT_all, gates = g["ps"], g["h"], g["x"], g["xT"], g["gates"]
    with ExitStack() as stack:
        m = Memory(nc, g, stack, phase)
        norm = Norm(m, g, "norm")
        norm2 = Norm(m, g, "norm2") if two_norms else None
        z0 = m.sb("z0", [L, 2, D]) if two_norms else None
        z = m.sb("z", [L, 2, D])
        xT = m.sb("xT", [K, 2, C, L])
        logits = m.sb("logits", [L, 2, E01])
        best = m.sb("best", [L, 2, 8])
        place = m.sb("place", [L, 2, 8], U32)
        placef = m.sb("placef", [L, 2, 8])
        gap = m.sb("gap", [L, 2])
        ratio = m.sb("ratio", [L, 2])
        total = m.sb("total", [L, 2])
        share = m.sb("share", [L, 2, 2])
        part = m.sb("part", [L, 2, 2, E01])
        pause = m.sb("pause", [1, 1])
        if bias:
            gate_row = m.sb("gate_row", [L, 2, E01])
            gT = m.sb("gT", [E01, 2, L])
        dve_steps = m.sem("dve_steps")
        z_ready, xT_ps, xT_ready, xT_kept = m.sem("z_ready"), m.sem("xT_ps"), m.sem("xT_ready"), m.sem("xT_kept")
        logits_ps, gap_ready, ratio_ready = m.sem("logits_ps"), m.sem("gap_ready"), m.sem("ratio_ready")
        gates_ready, gT_ps, gT_ready, b2_ps = m.sem("gates_ready"), m.sem("gT_ps"), m.sem("gT_ready"), m.sem("b2_ps")
        block = stack.enter_context(nc.Block())

        @block.tensor
        def _(pe):
            with pe.Fori(0, B // 2) as i:
                for j in range(2):
                    pe.wait_ge(z_ready, 2 * i + j + 1)
                    for c in range(C):
                        last = pe.transpose(ps[0:K, j, 3, c * L:(c + 1) * L], z[:, j, c * K:(c + 1) * K],
                                            ident[0:L, 0:L])
                    last.then_inc(xT_ps, 1)
                for j in range(2):
                    pe.wait_ge(xT_ready, 2 * i + j + 1)
                    for c in range(C):
                        last = pe.matmul(ps[0:L, j, 0, 0:E01], xT[:, j, c, :], w.at("gate", C)[:, c, :],
                                         start=(c == 0), stop=(c == C - 1))
                    last.then_inc(logits_ps, 1)
                if bias:
                    for j in range(2):
                        pe.wait_ge(gates_ready, i + 1)
                        pe.transpose(ps[0:E01, j, 1, 0:L], gate_row[:, j, :], ident[0:L, 0:L]).then_inc(gT_ps, 1)
                    for j in range(2):
                        pe.wait_ge(gT_ready, 2 * i + j + 1)
                        pe.matmul(ps[0:L, j, 2, 0:D], gT[:, j, :], w.at("b2"), start=True, stop=True)\
                          .then_inc(b2_ps, 1)

        @block.scalar
        def _(act):
            with act.Fori(0, B // 2) as i:
                for j in range(2):
                    act.wait_ge(xT_ps, 2 * i + j + 1)
                    for c in range(C):
                        last = act.activation(xT[:, j, c, :], ps[0:K, j, 3, c * L:(c + 1) * L], ACT.Identity,
                                              scale=w.at("g")[:, c:c + 1], bias=w.at("b")[:, c:c + 1])
                    last.then_inc(xT_ready, 1)
                act.wait_ge(gap_ready, i + 1)
                act.activation(ratio[:, :], gap[:, :], ACT.Exp).then_inc(ratio_ready, 1)
                if bias:
                    for j in range(2):
                        act.wait_ge(gT_ps, 2 * i + j + 1)
                        act.activation(gT[:, j, :], ps[0:E01, j, 1, 0:L], ACT.Copy).then_inc(gT_ready, 1)
                act.wait_ge(xT_kept, 2 * i + 2)

        @block.gpsimd
        def _(pool):
            with pool.Fori(0, B // 2) as i:
                norm.pool(pool, i)
                if two_norms:
                    norm2.pool(pool, i)
                for j in range(2):
                    pool.wait_ge(xT_ready, 2 * i + j + 1)
                    pool.tensor_copy(xT_all[:, :, ds(2 * i + j, 1), :], xT[:, j, :, :].unsqueeze(2))\
                        .then_inc(xT_kept, 1)

        @block.vector
        def _(dve):
            own = 4 + 6 * two_norms + 2 + 2 + 3 + 1 + 1 + 2 + 2 + (2 if bias else 0)
            with dve.Fori(0, B // 2) as i:
                steps = Steps(dve, dve_steps, own * i)
                tile = [ds(2 * i + j, 1) for j in range(2)]
                if two_norms:
                    for ins in norm.vector(dve, i, steps, [h[:, tile[j], :] for j in range(2)],
                                           [z0[:, j:j + 1, :] for j in range(2)]):
                        steps.done(ins)
                    steps.wait()
                    src = [z0[:, j:j + 1, :] for j in range(2)]
                    second = norm2
                else:
                    src = [x[:, tile[j], :] for j in range(2)]
                    second = norm
                for ins in second.vector(dve, i, steps, src, [z[:, j:j + 1, :] for j in range(2)]):
                    ins.then_inc(z_ready, 1)
                for j in range(2):
                    steps.done(dve.tensor_tensor(h[:, tile[j], :], h[:, tile[j], :], src[j], ALU.add))
                for j in range(2):
                    dve.wait_ge(logits_ps, 2 * i + j + 1)
                    steps.done(dve.tensor_copy(logits[:, j, :], ps[0:L, j, 0, 0:E01]))
                steps.wait()
                dve.memset(pause[:, :], 0.0)
                for j in range(2):
                    last = dve.max(best[:, j, :], logits[:, j, :])
                steps.done(last)
                steps.wait()
                dve.tensor_tensor(gap[:, :], best[:, :, 1], best[:, :, 0], ALU.subtract).then_inc(gap_ready, 1)
                for j in range(2):
                    last = dve.max_index(place[:, j, :], best[:, j, :], logits[:, j, :])
                steps.done(last)
                steps.wait()
                steps.done(dve.tensor_copy(placef[:, :, :], place[:, :, :]))
                dve.wait_ge(ratio_ready, i + 1)
                steps.done(dve.tensor_scalar(total[:, :], ratio[:, :], 1.0, None, ALU.add))
                steps.wait()
                steps.done(dve.reciprocal(share[:, :, 0], total[:, :]))
                steps.wait()
                steps.done(dve.tensor_tensor(share[:, :, 1], share[:, :, 0], ratio[:, :], ALU.mult))
                steps.wait()
                for j in range(2):
                    for n in range(2):
                        last = dve.tensor_scalar(part[:, j, n, :], iota, placef[:, j, n:n + 1],
                                                 share[:, j, n:n + 1], ALU.is_equal, ALU.mult)
                    steps.done(last)
                steps.wait()
                if bias:
                    dve.tensor_tensor(gate_row[:, :, :], part[:, :, 0, :], part[:, :, 1, :], ALU.add)\
                       .then_inc(gates_ready, 1)
                steps.done(dve.tensor_tensor(gates[:, ds(2 * i, 2), 0:E01], part[:, :, 0, :], part[:, :, 1, :],
                                             ALU.add))
                if bias:
                    for j in range(2):
                        dve.wait_ge(b2_ps, 2 * i + j + 1)
                        steps.done(dve.tensor_tensor(h[:, tile[j], :], h[:, tile[j], :], ps[0:L, j, 2:3, 0:D],
                                                     ALU.add))
                assert steps.n == own, (steps.n, own)


def experts(nc, g, dram, phase, func):
    bias = phase == "l0"
    ps, h, xT_all, gates = g["ps"], g["h"], g["xT"], g["gates"]
    hid_banks = 4
    with ExitStack() as stack:
        m = Memory(nc, g, stack, phase)
        up = m.sb("up", [K, 2, C, F])
        down = m.sb("down", [128, 2, FM, D])
        b1 = m.sb("b1", [128, 2, FM]) if bias else None
        hidden = m.sb("hidden", [128, 2, FM, NG])
        up_loaded = [m.sem(f"up_loaded{j}") for j in range(2)]
        hid_ps, hid_ready = m.sem("hid_ps"), m.sem("hid_ready")
        y_ps, y_added = m.sem("y_ps"), m.sem("y_added")
        per_load = 16 * (3 if bias else 2)
        block = stack.enter_context(nc.Block())

        def visit(i, j, qq, jj):
            return (2 * i + j) * G + 2 * qq + jj

        @block.sync
        def _(sp):
            def load(e, j):
                sp.dma_start(up[:, j, :, :], dram[phase + "_up"][e].rearrange("e p (c n) -> p (e c) n", c=C))\
                  .then_inc(up_loaded[j], 16)
                sp.dma_start(down[:, j, :, :], dram[phase + "_down"][e].rearrange("e p (m n) -> p (e m) n", m=FM))\
                  .then_inc(up_loaded[j], 16)
                if bias:
                    sp.dma_start(b1[:, j, :], dram[phase + "_b1"][e].rearrange("e p m -> p (e m)"))\
                      .then_inc(up_loaded[j], 16)
            for j in range(2):
                load(slice(j, j + 1), j)
            with sp.Fori(1, E01 // 2) as i:
                for j in range(2):
                    sp.wait_ge(y_ps, (2 * i + j - 1) * G * GB)
                    load(ds(2 * i + j, 1), j)

        @block.tensor
        def _(pe):
            with pe.Fori(0, E01 // 2) as i:
                for j in range(2):
                    with pe.Fori(0, G // 2) as qq:
                        pe.wait_ge(up_loaded[j], per_load * (i + 1))
                        for jj in range(2):
                            n = visit(i, j, qq, jj)
                            for t in range(FM):
                                pe.wait_ge(hid_ready, n * FM + t + 1)
                                bank = (jj * FM + t) % hid_banks
                                for c in range(C):
                                    last = pe.matmul(ps[:, 0, bank, 0:NG], up[:, j, c, t * 128:(t + 1) * 128],
                                                     xT_all[:, c, ds((2 * qq + jj) * GB, GB), :],
                                                     start=(c == 0), stop=(c == C - 1))
                                last.then_inc(hid_ps, 1)
                        for jj in range(2):
                            n = visit(i, j, qq, jj)
                            pe.wait_ge(hid_ready, hid_banks + (n + 1) * FM)
                            for b in range(GB):
                                pe.wait_ge(y_added, n * GB + b + 1)
                                for t in range(FM):
                                    last = pe.matmul(ps[0:L, 1, b, 0:D], hidden[:, jj, t, b * L:(b + 1) * L],
                                                     down[:, j, t, :], start=(t == 0), stop=(t == FM - 1))
                                last.then_inc(y_ps, 1)

        @block.scalar
        def _(act):
            act.sem_inc(hid_ready, hid_banks)
            if bias:
                act.wait_ge(up_loaded[0], per_load)
            with act.Fori(0, E01 // 2) as i:
                for j in range(2):
                    with act.Fori(0, G // 2) as qq:
                        if bias:
                            act.wait_ge(up_loaded[j], per_load * (i + 1))
                        for jj in range(2):
                            n = visit(i, j, qq, jj)
                            for t in range(FM):
                                act.wait_ge(hid_ps, n * FM + t + 1)
                                bank = (jj * FM + t) % hid_banks
                                act.activation(hidden[:, jj, t, :], ps[:, 0, bank, 0:NG], func,
                                               bias=b1[:, j, t:t + 1] if bias else 0.0).then_inc(hid_ready, 1)

        @block.vector
        def _(dve):
            dve.sem_inc(y_added, GB)
            with dve.Fori(0, E01 // 2) as i:
                for j in range(2):
                    with dve.Fori(0, G // 2) as qq:
                        for jj in range(2):
                            n = visit(i, j, qq, jj)
                            for b in range(GB):
                                dve.wait_ge(y_ps, n * GB + b + 1)
                                tile = ds((2 * qq + jj) * GB + b, 1)
                                dve.scalar_tensor_tensor(h[:, tile, :], ps[0:L, 1, b:b + 1, 0:D],
                                                         gates[:, tile, ds(2 * i + j, 1)].rearrange("p a b -> p (a b)"),
                                                         h[:, tile, :], ALU.mult, ALU.add).then_inc(y_added, 1)


def sub_weights(nc, g, dram, sub):
    less = g["l2f"].at("parts")
    up_parts, down, spread = sub["up"], sub["down"], sub["spread"]
    cols = NM * 32
    with ExitStack() as stack:
        m = Memory(nc, g, stack, "l2w")
        raw = m.sb("raw", [128, 2, cols])
        first = m.sb("first", [128, 2, cols], BF16)
        rest = m.sb("rest", [128, 2, cols])
        spread_f = m.sb("spread_f", [96, 8 * 128])
        raw_loaded, down_loaded = [m.sem(f"raw_loaded{j}") for j in range(2)], m.sem("down_loaded")
        spread_loaded = m.sem("spread_loaded")
        first_ready, rest_ready, second_ready, parts_ready = (
            m.sem("first_ready"), m.sem("rest_ready"), m.sem("second_ready"), m.sem("parts_ready"))
        block = stack.enter_context(nc.Block())

        @block.sync
        def _(sp):
            sp.dma_start(spread_f[:, :], dram["sub_spread"]).then_inc(spread_loaded, 16)
            for n in range(NS):
                if n >= 2:
                    sp.wait_ge(rest_ready, n - 1)
                sp.dma_start(raw[:, n % 2, :], dram["sub_up"][n]).then_inc(raw_loaded[n % 2], 16)
            sp.dma_start(down.rearrange("p s t r -> p (s t r)"), dram["sub_down"]).then_inc(down_loaded, 16)
            sp.wait_ge(down_loaded, 16)

        @block.scalar
        def _(act):
            act.wait_ge(spread_loaded, 16)
            act.activation(spread.rearrange("p t n -> p (t n)"), spread_f[:, :], ACT.Copy)

            def second_part(n):
                act.wait_ge(rest_ready, n + 1)
                act.activation(first[:, n % 2, :], rest[:, n % 2, :], ACT.Copy).then_inc(second_ready, 1)

            for n in range(NS):
                act.wait_ge(raw_loaded[n % 2], 16 * (n // 2 + 1))
                if n >= 2:
                    act.wait_ge(parts_ready, n - 1)
                act.activation(first[:, n % 2, :], raw[:, n % 2, :], ACT.Copy).then_inc(first_ready, 1)
                if n:
                    second_part(n - 1)
            second_part(NS - 1)

        @block.vector
        def _(dve):
            def parts(n):
                dve.wait_ge(second_ready, n + 1)
                dve.scalar_tensor_tensor(up_parts[:, n, :], first[:, n % 2, :], less[:, 3:4], rest[:, n % 2, :],
                                         ALU.mult, ALU.add).then_inc(parts_ready, 1)

            for n in range(NS):
                dve.wait_ge(first_ready, n + 1)
                if n >= 2:
                    dve.wait_ge(parts_ready, n - 1)
                dve.scalar_tensor_tensor(rest[:, n % 2, :], first[:, n % 2, :], less[:, 2:3], raw[:, n % 2, :],
                                         ALU.mult, ALU.add).then_inc(rest_ready, 1)
                if n:
                    parts(n - 1)
            parts(NS - 1)


def sub_gates(nc, g, sub, base):
    w = g["l2f"]
    ident, iota, less = g["const"].at("ident"), g["const"].at("iota"), w.at("parts")
    ps, h = g["ps"], g["h"]
    zs, gs, comb = sub["zs"], sub["gs"], sub["comb"]
    with ExitStack() as stack:
        m = Memory(nc, g, stack, f"l2g{base}")
        norm = Norm(m, g, "norm")
        z = m.sb("z", [L, 2, D])
        xT = m.sb("xT", [K, 2, C, L])
        sT = m.sb("sT", [128, 2, L])
        z_part = m.sb("z_part", [128, 2, 2, 4 * L], BF16)
        z_rest = m.sb("z_rest", [128, 2, 2, 4 * L])
        score = m.sb("score", [L, 2, NS, NM])
        best = m.sb("best", [L, 2, NS, 8])
        place = m.sb("place", [L, 2, NS, 8], U32)
        last_place = m.sb("last_place", [L, 2, NS])
        few = m.sb("few", [L, 2, NS, KEEP])
        share = m.sb("share", [L, 2, NS])
        expo = m.sb("expo", [L, 2, NS, NM])
        above = m.sb("above", [L, 2, NS, NM])
        tied = m.sb("tied", [L, 2, NS, NM])
        early = m.sb("early", [L, 2, NS, NM], BF16)
        gate = m.sb("gate", [L, 2, NS * 2, 32])
        gate_parts = m.sb("gate_parts", [L, 2, NS * 2, 3, 32], BF16)
        gT = m.sb("gT", [128, 2, 4, L])
        ident_bf = m.sb("ident_bf", [L, L], BF16)
        pause = m.sb("pause", [1, 1])
        dve_steps, ident_ready = m.sem("dve_steps"), m.sem("ident_ready")
        z_ready, xT_ps, xT_ready = m.sem("z_ready"), m.sem("xT_ps"), m.sem("xT_ready")
        sT_ps, sT_ready, score_ps, score_ready = m.sem("sT_ps"), m.sem("sT_ready"), m.sem("score_ps"), m.sem("score_ready")
        z8_ps, z1_ready, z_rest_ready, z2_ready, zs_ready = (
            m.sem("z8_ps"), m.sem("z1_ready"), m.sem("z_rest_ready"), m.sem("z2_ready"), m.sem("zs_ready"))
        few_ready, few_exp, below, below_exp = m.sem("few_ready"), m.sem("few_exp"), m.sem("below"), m.sem("below_exp")
        gate_ready = m.sem("gate_ready")
        g1_ready, less1_ready, g2_ready, less2_ready, g3_ready = (
            m.sem("g1_ready"), m.sem("less1_ready"), m.sem("g2_ready"), m.sem("less2_ready"), m.sem("g3_ready"))
        gs_ps, gs_ready = m.sem("gs_ps"), m.sem("gs_ready")
        gT_ps, gT_ready, b2_ps = m.sem("gT_ps"), m.sem("gT_ready"), m.sem("b2_ps")
        block = stack.enter_context(nc.Block())

        def parts_bank(j, n):
            return ps[0:96, j, 1 + n, 0:4 * L].bitcast(BF16).rearrange("p (a n) -> p a n", a=8)

        @block.tensor
        def _(pe):
            pe.wait_ge(ident_ready, 1)
            with pe.Fori(0, HALF // 2) as i:
                for j in range(2):
                    pe.wait_ge(z_ready, 2 * i + j + 1)
                    for c in range(C):
                        last = pe.transpose(ps[0:K, j, 3, c * L:(c + 1) * L], z[:, j, c * K:(c + 1) * K],
                                            ident[0:L, 0:L])
                    last.then_inc(xT_ps, 1)
                for j in range(2):
                    pe.wait_ge(xT_ready, 2 * i + j + 1)
                    for c in range(C):
                        last = pe.matmul(ps[:, j, 0, 0:L], w.at("p", C)[:, c, :], xT[:, j, c, :],
                                         start=(c == 0), stop=(c == C - 1))
                    last.then_inc(sT_ps, 1)
                for j in range(2):
                    pe.wait_ge(sT_ready, 2 * i + j + 1)
                    pe.matmul(ps[0:L, j, 1, :], sT[:, j, :], w.at("centres"), start=True, stop=True)\
                      .then_inc(score_ps, 1)
                for j in range(2):
                    for n in range(NS):
                        for c in range(C):
                            last = pe.matmul(ps[:, j, 2 + n // 4, (n % 4) * L:(n % 4 + 1) * L],
                                             w.at("p8", C)[:, c, n * 128:(n + 1) * 128], xT[:, j, c, :],
                                             start=(c == 0), stop=(c == C - 1))
                    last.then_inc(z8_ps, 1)
                for j in range(2):
                    pe.wait_ge(gate_ready, 2 * i + j + 1)
                    for n in range(4):
                        last = pe.transpose(ps[:, j, 0, n * L:(n + 1) * L],
                                            gate[:, j, 4 * n:4 * n + 4, :].rearrange("p a m -> p (a m)"),
                                            ident[0:L, 0:L])
                    last.then_inc(gT_ps, 1)
                for j in range(2):
                    pe.wait_ge(g3_ready, 2 * i + j + 1)
                    pe.wait_ge(zs_ready, 2 * i + j + 1)
                    for n in range(2 * NS):
                        last = pe.transpose(parts_bank(j, n // 8)[:, n % 8, :],
                                            gate_parts[:, j, n, :, :].rearrange("p a m -> p (a m)"), ident_bf[:, :])
                    last.then_inc(gs_ps, 1)
                for j in range(2):
                    pe.wait_ge(gT_ready, 2 * i + j + 1)
                    for half in range(2):
                        for n in range(RG):
                            last = pe.matmul(ps[HP * n:HP * (n + 1), j, 3, half * L:(half + 1) * L],
                                             w.at("b2", 8)[:, 2 * n + half, :], gT[:, j, n, :],
                                             start=True, stop=True)
                    last.then_inc(b2_ps, 1)

        @block.scalar
        def _(act):
            with act.Fori(0, HALF // 2) as i:
                for j in range(2):
                    act.wait_ge(xT_ps, 2 * i + j + 1)
                    act.activation(xT[:, j, :, :].rearrange("p c n -> p (c n)"), ps[0:K, j, 3, 0:C * L],
                                   ACT.Copy).then_inc(xT_ready, 1)
                for j in range(2):
                    act.wait_ge(sT_ps, 2 * i + j + 1)
                    act.activation(sT[:, j, :], ps[:, j, 0, 0:L], ACT.Copy).then_inc(sT_ready, 1)
                for j in range(2):
                    act.wait_ge(score_ps, 2 * i + j + 1)
                    act.activation(score[:, j, :, :].rearrange("p s m -> p (s m)"), ps[0:L, j, 1, :], ACT.Copy)\
                       .then_inc(score_ready, 1)
                for j in range(2):
                    act.wait_ge(z8_ps, 2 * i + j + 1)
                    act.activation(z_part[:, j, :, :], ps[:, j, 2:4, 0:4 * L], ACT.Copy).then_inc(z1_ready, 1)
                for j in range(2):
                    act.wait_ge(below, 2 * i + j + 1)
                    act.activation(expo[:, j, :, :], expo[:, j, :, :], ACT.Exp).then_inc(below_exp, 1)
                    act.wait_ge(few_ready, 2 * i + j + 1)
                    act.activation(few[:, j, :, :], few[:, j, :, :], ACT.Exp).then_inc(few_exp, 1)
                    act.wait_ge(z_rest_ready, 2 * i + j + 1)
                    act.activation(z_part[:, j, :, :], z_rest[:, j, :, :], ACT.Copy).then_inc(z2_ready, 1)
                for j in range(2):
                    act.wait_ge(gate_ready, 2 * i + j + 1)
                    act.activation(gate_parts[:, j, :, 0, :], gate[:, j, :, :], ACT.Copy).then_inc(g1_ready, 1)
                for j in range(2):
                    act.wait_ge(less1_ready, 2 * i + j + 1)
                    act.activation(gate_parts[:, j, :, 1, :], expo[:, j, :, :].rearrange("p s (a m) -> p (s a) m", a=2),
                                   ACT.Copy).then_inc(g2_ready, 1)
                for j in range(2):
                    act.wait_ge(less2_ready, 2 * i + j + 1)
                    act.activation(gate_parts[:, j, :, 2, :], tied[:, j, :, :].rearrange("p s (a m) -> p (s a) m", a=2),
                                   ACT.Copy).then_inc(g3_ready, 1)
                for j in range(2):
                    act.wait_ge(gT_ps, 2 * i + j + 1)
                    act.activation(gT[:, j, :, :].rearrange("p a n -> p (a n)"), ps[:, j, 0, 0:4 * L], ACT.Copy)\
                       .then_inc(gT_ready, 1)
                for j in range(2):
                    act.wait_ge(gs_ps, 2 * i + j + 1)
                    for n in range(2):
                        last = act.activation(gs[:, 8 * n:8 * n + 8, ds(2 * i + j, 1), :],
                                              parts_bank(j, n).unsqueeze(2), ACT.Copy)
                    last.then_inc(gs_ready, 1)

        @block.gpsimd
        def _(pool):
            with pool.Fori(0, HALF // 2) as i:
                norm.pool(pool, i)
                for j in range(2):
                    pool.wait_ge(g1_ready, 2 * i + j + 1)
                    pool.tensor_tensor(expo[:, j, :, :].rearrange("p s (a m) -> p (s a) m", a=2), gate[:, j, :, :],
                                       gate_parts[:, j, :, 0, :], ALU.subtract).then_inc(less1_ready, 1)
                for j in range(2):
                    pool.wait_ge(g2_ready, 2 * i + j + 1)
                    pool.tensor_tensor(tied[:, j, :, :].rearrange("p s (a m) -> p (s a) m", a=2),
                                       expo[:, j, :, :].rearrange("p s (a m) -> p (s a) m", a=2),
                                       gate_parts[:, j, :, 1, :], ALU.subtract).then_inc(less2_ready, 1)

        @block.vector
        def _(dve):
            dve.tensor_copy(ident_bf[:, :], ident[0:L, 0:L]).then_inc(ident_ready, 1)
            own = 4 + 2 * 11
            with dve.Fori(0, HALF // 2) as i:
                steps = Steps(dve, dve_steps, own * i)
                for ins in norm.vector(dve, i, steps, [h[:, ds(2 * i + j + base, 1), :] for j in range(2)],
                                       [z[:, j:j + 1, :] for j in range(2)]):
                    ins.then_inc(z_ready, 1)
                for j in range(2):
                    dve.wait_ge(score_ready, 2 * i + j + 1)
                    dve.memset(pause[:, :], 0.0)
                    for n in range(NS):
                        last = dve.max(best[:, j, n, :], score[:, j, n, :])
                    steps.done(last)
                    steps.wait()
                    dve.tensor_tensor(expo[:, j, :, :], score[:, j, :, :],
                                      best[:, j, :, 0:1].broadcast_to([L, NS, NM]), ALU.subtract).then_inc(below, 1)
                    dve.tensor_tensor(few[:, j, :, :], best[:, j, :, 0:KEEP],
                                      best[:, j, :, 0:1].broadcast_to([L, NS, KEEP]), ALU.subtract)\
                       .then_inc(few_ready, 1)
                    for n in range(NS):
                        last = dve.max_index(place[:, j, n, :], best[:, j, n, :], score[:, j, n, :])
                    steps.done(last)
                    dve.wait_ge(z1_ready, 2 * i + j + 1)
                    dve.scalar_tensor_tensor(z_rest[:, j, :, :], z_part[:, j, :, :], less[:, 0:1],
                                             ps[:, j, 2:4, 0:4 * L], ALU.mult, ALU.add).then_inc(z_rest_ready, 1)
                    fourth = best[:, j, :, KEEP - 1:KEEP].broadcast_to([L, NS, NM])
                    steps.done(dve.tensor_tensor(above[:, j, :, :], score[:, j, :, :], fourth, ALU.is_gt))
                    steps.done(dve.tensor_tensor(tied[:, j, :, :], score[:, j, :, :], fourth, ALU.is_equal))
                    steps.wait()
                    steps.done(dve.tensor_copy(last_place[:, j, :], place[:, j, :, KEEP - 1]))
                    steps.wait()
                    steps.done(dve.tensor_tensor(early[:, j, :, :], iota.unsqueeze(1).broadcast_to([L, NS, NM]),
                                                 last_place[:, j, :].unsqueeze(2).broadcast_to([L, NS, NM]),
                                                 ALU.is_le))
                    dve.wait_ge(few_exp, 2 * i + j + 1)
                    steps.done(dve.tensor_reduce(share[:, j, :], few[:, j, :, :], AX.X, ALU.add))
                    steps.wait()
                    steps.done(dve.tensor_tensor(tied[:, j, :, :], tied[:, j, :, :], early[:, j, :, :], ALU.mult))
                    steps.wait()
                    steps.done(dve.reciprocal(share[:, j, :], share[:, j, :]))
                    steps.done(dve.tensor_tensor(above[:, j, :, :], above[:, j, :, :], tied[:, j, :, :], ALU.add))
                    dve.wait_ge(below_exp, 2 * i + j + 1)
                    steps.wait()
                    steps.done(dve.tensor_tensor(above[:, j, :, :], above[:, j, :, :], expo[:, j, :, :], ALU.mult))
                    steps.wait()
                    dve.tensor_tensor(gate[:, j, :, :].rearrange("p (s a) m -> p s (a m)", a=2), above[:, j, :, :],
                                      share[:, j, :].unsqueeze(2).broadcast_to([L, NS, NM]), ALU.mult)\
                       .then_inc(gate_ready, 1)
                    dve.wait_ge(z2_ready, 2 * i + j + 1)
                    for n in range(2):
                        last = dve.scalar_tensor_tensor(
                            zs[:, 4 * n:4 * n + 4, ds(2 * i + j, 1), :].rearrange("p s a n -> p (s a) n"),
                            z_part[:, j, n, :].rearrange("p (s n) -> p s n", s=4), less[:, 1:2],
                            z_rest[:, j, n, :].rearrange("p (s n) -> p s n", s=4), ALU.mult, ALU.add)
                    last.then_inc(zs_ready, 1)
                for j in range(2):
                    dve.wait_ge(b2_ps, 2 * i + j + 1)
                    dve.tensor_copy(comb[:, :, ds(2 * i + j + base, 1), :],
                                    ps[:, j, 3, 0:2 * L].rearrange("p (c a n) -> p c a n", c=2, a=1))
                dve.wait_ge(gs_ready, 2 * i + 2)
                assert steps.n == own, (steps.n, own)


def sub_experts(nc, g, sub, base):
    w = g["l2f"]
    ps, comb = g["ps"], sub["comb"]
    zs, gs, up_parts, down, spread = sub["zs"], sub["gs"], sub["up"], sub["down"], sub["spread"]
    chunks = HALF // GB
    tiles = NS * MT
    deep = 3
    order = [(2 * r + half, t, r) for half in range(2) for t in range(MT) for r in range(RG)]
    with ExitStack() as stack:
        m = Memory(nc, g, stack, f"l2s{base}")
        hidden = m.sb("hidden", [128, deep, NG])
        gated = m.sb("gated", [128, 2 * RG, NG])
        tile_ps, hid_ready, gated_ready = m.sem("tile_ps"), m.sem("hid_ready"), m.sem("gated_ready")
        comb_ps, comb_ready = m.sem("comb_ps"), m.sem("comb_ready")
        block = stack.enter_context(nc.Block())

        def bank(kind, n):
            at = 3 * kind + n % deep
            return ps[:, at // 4, at % 4, 0:NG]

        sums = [ps[:, 1, 2 + half, 0:NG] for half in range(2)]

        @block.tensor
        def _(pe):
            def second(n, q):
                pe.wait_ge(gated_ready, deep + tiles * q + n + RG)
                for at in range(n, n + RG):
                    s, t, r = order[at]
                    last = pe.matmul(sums[at // (tiles // 2)][HP * r:HP * (r + 1)], down[:, s, t, :],
                                     gated[:, at % (2 * RG), :], start=(t == 0), stop=(t == MT - 1))
                if n + RG == tiles:
                    last.then_inc(comb_ps, 1)

            with pe.Fori(0, chunks) as q:
                for n, (s, t, r) in enumerate(order):
                    before = n - deep if n >= deep else max(a for a in range(tiles) if a % deep == n) - tiles
                    pe.wait_ge(gated_ready, tiles * q + before + 1 + deep)
                    pe.matmul(bank(1, n), spread[:, t % 8, :], gs[:, 2 * s + t // 8, ds(q * GB, GB), :],
                              start=True, stop=True)
                    pe.matmul(bank(0, n), up_parts[:, s, t * 128:(t + 1) * 128], zs[:, s, ds(q * GB, GB), :],
                              start=True, stop=True).then_inc(tile_ps, 1)
                    if n == RG - 1:
                        pe.wait_ge(comb_ready, q + 1)
                    if n % RG == RG - 1 and n > RG:
                        second(n - 2 * RG + 1, q)
                second(tiles - RG, q)

        @block.scalar
        def _(act):
            with act.Fori(0, chunks) as q:
                for n, (s, t, r) in enumerate(order):
                    act.wait_ge(tile_ps, tiles * q + n + 1)
                    act.activation(hidden[:, n % deep, :], bank(0, n), ACT.Gelu_apprx_tanh,
                                   bias=w.at("b1")[:, s * MT + t:s * MT + t + 1]).then_inc(hid_ready, 1)

        @block.vector
        def _(dve):
            dve.sem_inc(gated_ready, deep)
            dve.sem_inc(comb_ready, 1)
            with dve.Fori(0, chunks) as q:
                for n in range(tiles):
                    dve.wait_ge(hid_ready, tiles * q + n + 1)
                    dve.tensor_tensor(gated[:, n % (2 * RG), :], hidden[:, n % deep, :], bank(1, n), ALU.mult)\
                       .then_inc(gated_ready, 1)
                dve.wait_ge(comb_ps, q + 1)
                for half in range(2):
                    part = comb[:, half, ds(q * GB + base, GB), :]
                    last = dve.tensor_tensor(part, part, sums[half].rearrange("p (a n) -> p a n", a=GB), ALU.add)
                last.then_inc(comb_ready, 1)


def sub_output(nc, g, sub):
    w = g["l2f"]
    ps, h, comb = g["ps"], g["h"], sub["comb"]
    with ExitStack() as stack:
        m = Memory(nc, g, stack, "l2o")
        hT = m.sb("hT", [64, 2, L])
        y = m.sb("y", [L, 2, D])
        h_ps, h_ready, y_ps, y_ready, added = m.sem("h_ps"), m.sem("h_ready"), m.sem("y_ps"), m.sem("y_ready"), m.sem("added")
        block = stack.enter_context(nc.Block())

        @block.tensor
        def _(pe):
            with pe.Fori(0, B // 2) as i:
                for j in range(2):
                    pe.wait_ge(h_ready, 2 * i + j + 1)
                    for half in range(2):
                        last = pe.matmul(ps[0:64, j, 1, 0:L], w.at("g1", 2)[:, half, :], comb[:, half, ds(2 * i + j, 1), :],
                                         start=(half == 0), stop=(half == 1))
                    last.then_inc(h_ps, 1)
                for j in range(2):
                    pe.wait_ge(h_ready, 2 + 2 * i + j + 1)
                    pe.wait_ge(y_ready, 2 * i + j + 1)
                    pe.matmul(ps[0:L, j, 2, 0:D], hT[:, j, :], w.at("g2"), start=True, stop=True).then_inc(y_ps, 1)

        @block.scalar
        def _(act):
            act.sem_inc(h_ready, 2)
            with act.Fori(0, B // 2) as i:
                for j in range(2):
                    act.wait_ge(h_ps, 2 * i + j + 1)
                    act.activation(hT[:, j, :], ps[0:64, j, 1, 0:L], ACT.Gelu_apprx_tanh, bias=w.at("g1b"))\
                       .then_inc(h_ready, 1)

        @block.vector
        def _(dve):
            dve.sem_inc(y_ready, 2)
            with dve.Fori(0, B // 2) as i:
                for j in range(2):
                    dve.wait_ge(y_ps, 2 * i + j + 1)
                    dve.tensor_tensor(y[:, j, :], ps[0:L, j, 2, 0:D], w.at("g2b"), ALU.add).then_inc(y_ready, 1)
                for j in range(2):
                    tile = ds(2 * i + j, 1)
                    dve.wait_ge(y_ready, 2 + 2 * i + j + 1)
                    dve.tensor_tensor(h[:, tile, :], h[:, tile, :], y[:, j:j + 1, :], ALU.add).then_inc(added, 1)
                dve.wait_ge(added, 2 * i + 2)


def sub_feed_forward(nc, g, dram):
    with ExitStack() as stack:
        def sb(name, shape, dt=F32):
            return stack.enter_context(nc.sbuf_tensor("sub_" + name, shape, dt))[:]

        sub = {"comb": sb("comb", [128, 2, B, L]), "up": sb("up", [128, NS, NM * 32], BF16),
               "down": sb("down", [128, NS, MT, HP]), "spread": sb("spread", [96, 8, 128], BF16)}
        sub_weights(nc, g, dram, sub)
        with ExitStack() as inner:
            sub["zs"] = inner.enter_context(nc.sbuf_tensor("sub_zs", [128, NS, HALF, L], BF16))[:]
            sub["gs"] = inner.enter_context(nc.sbuf_tensor("sub_gs", [96, 2 * NS, HALF, L], BF16))[:]
            for base in (0, HALF):
                sub_gates(nc, g, sub, base)
                sub_experts(nc, g, sub, base)
        sub_output(nc, g, sub)


def normalise(nc, g):
    ident = g["const"].at("ident")
    ps, h, x, xT_all = g["ps"], g["h"], g["x"], g["xT"]
    with ExitStack() as stack:
        m = Memory(nc, g, stack, "l3n")
        norm = Norm(m, g, "norm")
        z = m.sb("z", [L, 2, D])
        dve_steps = m.sem("dve_steps")
        z_ready, z_kept, xT_ps, xT_ready = m.sem("z_ready"), m.sem("z_kept"), m.sem("xT_ps"), m.sem("xT_ready")
        block = stack.enter_context(nc.Block())

        @block.tensor
        def _(pe):
            with pe.Fori(0, B // 2) as i:
                for j in range(2):
                    pe.wait_ge(z_ready, 2 * i + j + 1)
                    pe.wait_ge(xT_ready, 2 * i + j + 1)
                    for c in range(C):
                        last = pe.transpose(ps[0:K, j, 3, c * L:(c + 1) * L], z[:, j, c * K:(c + 1) * K],
                                            ident[0:L, 0:L])
                    last.then_inc(xT_ps, 1)

        @block.scalar
        def _(act):
            act.sem_inc(xT_ready, 2)
            with act.Fori(0, B // 2) as i:
                for j in range(2):
                    act.wait_ge(xT_ps, 2 * i + j + 1)
                    act.activation(xT_all[:, :, ds(2 * i + j, 1), :],
                                   ps[0:K, j, 3, 0:C * L].rearrange("p (c a n) -> p c a n", c=C, a=1),
                                   ACT.Copy).then_inc(xT_ready, 1)

        @block.gpsimd
        def _(pool):
            with pool.Fori(0, B // 2) as i:
                norm.pool(pool, i)
                for j in range(2):
                    pool.wait_ge(z_ready, 2 * i + j + 1)
                    pool.tensor_copy(x[:, ds(2 * i + j, 1), :], z[:, j:j + 1, :]).then_inc(z_kept, 1)

        @block.vector
        def _(dve):
            with dve.Fori(0, B // 2) as i:
                steps = Steps(dve, dve_steps, 4 * i)
                for ins in norm.vector(dve, i, steps, [h[:, ds(2 * i + j, 1), :] for j in range(2)],
                                       [z[:, j:j + 1, :] for j in range(2)]):
                    ins.then_inc(z_ready, 1)
                dve.wait_ge(z_kept, 2 * i + 2)
                dve.wait_ge(xT_ps, 2 * i + 2)


def choose(nc, g, dram, chosen, xln, out):
    w = g["l3f"]
    ident = g["const"].at("ident")
    ps, h, xT_all = g["ps"], g["h"], g["xT"]
    with ExitStack() as stack:
        m = Memory(nc, g, stack, "l3c")
        score = m.sb("score", [E3, T])
        value = m.sb("value", [E3, ROUNDS * 8])
        place = m.sb("place", [E3, ROUNDS * 8], U32)
        placef = m.sb("placef", [E3, ROUNDS * 8])
        act_gate = m.sb("act_gate", [128, 2, SM, NG])
        act_up = m.sb("act_up", [128, 2, SM, NG])
        hidden = m.sb("hidden", [128, 2, SM, NG])
        y = m.sb("y", [L, B, D])
        x_stored, out_stored = m.sem("x_stored"), m.sem("out_stored")
        score_ps, score_ready, rounds, placef_ready = m.sem("score_ps"), m.sem("score_ready"), m.sem("rounds"), m.sem("placef_ready")
        list_ps = m.sem("list_ps")
        gu_ps, gu_ready, hidden_ready, y_ps, y_ready, h_ready = (
            m.sem("gu_ps"), m.sem("gu_ready"), m.sem("hidden_ready"), m.sem("y_ps"), m.sem("y_ready"), m.sem("h_ready"))
        block = stack.enter_context(nc.Block())

        @block.sync
        def _(sp):
            sp.dma_start(xln.rearrange("(b t) d -> t b d", b=B), g["x"][:, :, :]).then_inc(x_stored, 16)
            sp.wait_ge(h_ready, G)
            sp.dma_start(out.rearrange("b t d -> t b d"), h[:, 0:B, :]).then_inc(out_stored, 16)
            sp.wait_ge(x_stored, 16)
            sp.wait_ge(out_stored, 16)

        @block.tensor
        def _(pe):
            for q in range(G):
                for c in range(C):
                    last = pe.matmul(ps[0:E3, 0, q, 0:NG], w.at("choose", C)[:, c, :],
                                     xT_all[:, c, q * GB:(q + 1) * GB, :], start=(c == 0), stop=(c == C - 1))
                last.then_inc(score_ps, 1)
            for q in range(G):
                for t in range(SM):
                    n = q * SM + t
                    if n < 2:
                        pe.wait_ge(score_ready, 2 * n + 2)
                    else:
                        pe.wait_ge(gu_ready, n - 1)
                    for u, name in ((0, "ws_g"), (1, "ws_u")):
                        for c in range(C):
                            last = pe.matmul(ps[:, 0, 2 * (n % 2) + u, 0:NG],
                                             w.at(name, C)[:, c, t * 128:(t + 1) * 128],
                                             xT_all[:, c, q * GB:(q + 1) * GB, :], start=(c == 0), stop=(c == C - 1))
                    last.then_inc(gu_ps, 1)
                pe.wait_ge(hidden_ready, (q + 1) * SM)
                if q:
                    pe.wait_ge(y_ready, q)
                for b in range(GB):
                    for t in range(SM):
                        last = pe.matmul(ps[0:L, 1, b, 0:D], hidden[:, q % 2, t, b * L:(b + 1) * L],
                                         w.at("ws_d", SM)[:, t, :], start=(t == 0), stop=(t == SM - 1))
                last.then_inc(y_ps, 1)
            pe.wait_ge(placef_ready, 1)
            pe.wait_ge(gu_ready, G * SM)
            for half in range(2):
                for n, src in ((0, placef), (1, value)):
                    last = pe.transpose(ps[0:L, 0, n, half * E3:(half + 1) * E3],
                                        src[:, half * L:(half + 1) * L], ident[0:E3, 0:E3])
            last.then_inc(list_ps, 1)

        @block.scalar
        def _(act):
            for q in range(G):
                act.wait_ge(score_ps, q + 1)
                act.activation(score[:, q * NG:(q + 1) * NG], ps[0:E3, 0, q, 0:NG], ACT.Sigmoid)\
                   .then_inc(score_ready, 1)
            for q in range(G):
                for t in range(SM):
                    n = q * SM + t
                    act.wait_ge(gu_ps, n + 1)
                    if q >= 2:
                        act.wait_ge(hidden_ready, (q - 1) * SM)
                    act.activation(act_gate[:, q % 2, t, :], ps[:, 0, 2 * (n % 2), 0:NG], ACT.Silu)
                    act.activation(act_up[:, q % 2, t, :], ps[:, 0, 2 * (n % 2) + 1, 0:NG], ACT.Copy)\
                       .then_inc(gu_ready, 1)
                act.wait_ge(y_ps, q + 1)
                act.activation(y[:, q * GB:(q + 1) * GB, :], ps[0:L, 1, :, 0:D], ACT.Copy).then_inc(y_ready, 1)

        @block.gpsimd
        def _(pool):
            for q in range(G):
                for t in range(SM):
                    pool.wait_ge(gu_ready, q * SM + t + 1)
                    if q >= 2:
                        pool.wait_ge(y_ps, q - 1)
                    pool.tensor_tensor(hidden[:, q % 2, t, :], act_gate[:, q % 2, t, :], act_up[:, q % 2, t, :],
                                       ALU.mult).then_inc(hidden_ready, 1)
                pool.wait_ge(y_ready, q + 1)
                pool.tensor_tensor(h[:, q * GB:(q + 1) * GB, :], h[:, q * GB:(q + 1) * GB, :],
                                   y[:, q * GB:(q + 1) * GB, :], ALU.add).then_inc(h_ready, 1)

        @block.vector
        def _(dve):
            dve.wait_ge(score_ready, G)
            for n in range(ROUNDS):
                eight = slice(n * 8, n * 8 + 8)
                if n:
                    dve.wait_ge(rounds, 2 * n)
                dve.max(value[:, eight], score[:, :]).then_inc(rounds, 1)
                dve.wait_ge(rounds, 2 * n + 1)
                dve.max_index(place[:, eight], value[:, eight], score[:, :])
                if n < ROUNDS - 1:
                    dve.match_replace(score[:, :], value[:, eight], score[:, :], -1.0).then_inc(rounds, 1)
                else:
                    dve.memset(chosen["pause"][:, :], 0.0).then_inc(rounds, 1)
            dve.drain()
            dve.tensor_copy(placef[:, :], place[:, :]).then_inc(placef_ready, 1)
            dve.wait_ge(list_ps, 1)
            dve.memset(chosen["place"][:, :, E3:E3 + 2], 0)
            dve.tensor_copy(chosen["place"][:, :, 0:E3], ps[0:L, 0, 0, 0:2 * E3].rearrange("p (a e) -> p a e", a=2))
            dve.tensor_copy(chosen["score"][:, :, :], ps[0:L, 0, 1, 0:2 * E3].rearrange("p (a e) -> p a e", a=2))


def chosen_experts(nc, g, dram, chosen, xln, out):
    ident = g["const"].at("ident")
    ps = g["ps"]
    table = out.rearrange("b t d -> (b t) d")
    with ExitStack() as stack:
        m = Memory(nc, g, stack, "l3e")
        wg = m.sb("wg", [K, 2, C, F])
        wu = m.sb("wu", [K, 2, C, F])
        wd = m.sb("wd", [128, 2, FM, D])
        rows_in = [[m.sb(f"rows_in{j}{a}", [L, 1], U32) for a in range(2)] for j in range(2)]
        rows_out = [[m.sb(f"rows_out{j}{a}", [L, 1], U32) for a in range(2)] for j in range(2)]
        xg = [[m.sb(f"xg{j}{a}", [L, D]) for a in range(2)] for j in range(2)]
        xgT = m.sb("xgT", [K, 2, C, 2, L])
        pause = m.sb("pause", [1, 6])
        held, pair_added = m.sem("held"), m.sem("pair_added")
        act_gate = m.sb("act_gate", [128, 2, FM, 2 * L])
        hidden = m.sb("hidden", [128, 2, FM, 2, L])
        y = [[m.sb(f"y{j}{a}", [L, D]) for a in range(2)] for j in range(2)]
        loaded = [m.sem(f"loaded{j}") for j in range(2)]
        rows_ready, gathered, xgT_ps, xgT_ready = m.sem("rows_ready"), [m.sem(f"gathered{j}") for j in range(2)], m.sem("xgT_ps"), m.sem("xgT_ready")
        hid_ps, gate_ready, hid_ready, y_ps, y_ready, added = (
            m.sem("hid_ps"), m.sem("gate_ready"), m.sem("hid_ready"), m.sem("y_ps"), m.sem("y_ready"), m.sem("added"))
        block = stack.enter_context(nc.Block())

        @block.sync
        def _(sp):
            def load(e, j):
                for dst, name in ((wg, "l3_gate"), (wu, "l3_up"), (wd, "l3_down")):
                    sp.dma_start(dst[:, j, :, :], dram[name][e].rearrange("e p (c n) -> p (e c) n", n=dst.shape[3]))\
                      .then_inc(loaded[j], 16)
            for j in range(2):
                load(slice(j, j + 1), j)
            with sp.Fori(1, E3 // 2) as i:
                for j in range(2):
                    sp.wait_ge(y_ps, 2 * i + j - 1)
                    load(ds(2 * i + j, 1), j)

        @block.gpsimd
        def _(pool):
            neg = g["const"].at("neg_half")

            def hold(n):
                pool.tensor_tensor(pause[:, n:n + 1], neg[0:1, 0:1], neg[0:1, 1:2], ALU.mult).then_inc(held, 1)

            def gather(j):
                hold(j)
                for a in range(2):
                    pool.indirect_dma_start(xg[j][a][:, :], None, xln,
                                            bass.IndirectOffsetOnAxis(ap=rows_in[j][a][:, :], axis=0))\
                        .then_inc(gathered[j], 16)

            for j in range(2):
                pool.wait_ge(rows_ready, j + 1)
                gather(j)
            pool.wait_ge(held, 2)
            with pool.Fori(0, E3 // 2) as i:
                for j in range(2):
                    pool.wait_ge(rows_ready, 2 * i + 2 + j + 1)
                    gather(j)
                for j in range(2):
                    pool.wait_ge(y_ready, 2 * i + j + 1)
                    for a in range(2):
                        hold(2 + 2 * j + a)
                        pool.indirect_dma_start(table, bass.IndirectOffsetOnAxis(ap=rows_out[j][a][:, :], axis=0),
                                                y[j][a][:, :], None, compute_op=ALU.add).then_inc(added, 16)
                        pool.wait_ge(added, 16 * (2 * (2 * i + j) + a + 1))
                pool.sem_inc(pair_added, 1)
                pool.wait_ge(held, 2 + 6 * (i + 1))
            for j in range(2):
                pool.wait_ge(gathered[j], 32 * (E3 // 2 + 1))

        @block.tensor
        def _(pe):
            def transposes(n, j):
                pe.wait_ge(gathered[j], 32 * (n + 1))
                for a in range(2):
                    for c in range(C):
                        last = pe.transpose(ps[0:K, j, 3, (c * 2 + a) * L:(c * 2 + a + 1) * L],
                                            xg[j][a][:, c * K:(c + 1) * K], ident[0:L, 0:L])
                last.then_inc(xgT_ps, 1)

            for j in range(2):
                transposes(0, j)
            with pe.Fori(0, E3 // 2) as i:
                for j in range(2):
                    pe.wait_ge(xgT_ready, 2 * i + j + 1)
                    pe.wait_ge(loaded[j], 48 * (i + 1))
                    for t in range(FM):
                        n = FM * (2 * i + j) + t
                        pe.wait_ge(hid_ready, n + 1)
                        for u, wt in ((0, wg), (1, wu)):
                            for c in range(C):
                                last = pe.matmul(ps[:, j, t % 3, u * 2 * L:(u + 1) * 2 * L],
                                                 wt[:, j, c, t * 128:(t + 1) * 128],
                                                 xgT[:, j, c, :, :], start=(c == 0), stop=(c == C - 1))
                        last.then_inc(hid_ps, 1)
                for j in range(2):
                    pe.wait_ge(hid_ready, 3 + FM * (2 * i + j + 1))
                    for a in range(2):
                        for t in range(FM):
                            last = pe.matmul(ps[0:L, j, 3, a * D:(a + 1) * D], hidden[:, j, t, a, :],
                                             wd[:, j, t, :], start=(t == 0), stop=(t == FM - 1))
                    last.then_inc(y_ps, 1)
                for j in range(2):
                    pe.wait_ge(y_ready, 2 * i + j + 1)
                    transposes(i + 1, j)

        @block.scalar
        def _(act):
            def xgT_copies(n, j):
                act.wait_ge(xgT_ps, 2 * n + j + 1)
                act.activation(xgT[:, j, :, :, :].rearrange("p c a n -> p (c a n)"), ps[0:K, j, 3, 0:4 * L],
                               ACT.Copy).then_inc(xgT_ready, 1)

            for j in range(2):
                xgT_copies(0, j)
            with act.Fori(0, E3 // 2) as i:
                for j in range(2):
                    for t in range(FM):
                        n = FM * (2 * i + j) + t
                        act.wait_ge(hid_ps, n + 1)
                        act.activation(act_gate[:, j, t, :], ps[:, j, t % 3, 0:2 * L], ACT.Silu)\
                           .then_inc(gate_ready, 1)
                for j in range(2):
                    xgT_copies(i + 1, j)

        @block.vector
        def _(dve):
            dve.sem_inc(hid_ready, 3)
            dve.sem_inc(pair_added, 1)

            def next_rows(n, j):
                for a in range(2):
                    last = dve.tensor_copy(rows_in[j][a][:, :], chosen["place"][:, a, ds(2 * n + j, 1)])
                last.then_inc(rows_ready, 1)

            for j in range(2):
                next_rows(0, j)
            with dve.Fori(0, E3 // 2) as i:
                for j in range(2):
                    dve.wait_ge(xgT_ps, 2 * i + j + 1)
                    next_rows(i + 1, j)
                for j in range(2):
                    for t in range(FM):
                        n = FM * (2 * i + j) + t
                        dve.wait_ge(gate_ready, n + 1)
                        dve.tensor_tensor(hidden[:, j, t, :, :].rearrange("p a n -> p (a n)"), act_gate[:, j, t, :],
                                          ps[:, j, t % 3, 2 * L:4 * L], ALU.mult).then_inc(hid_ready, 1)
                dve.wait_ge(pair_added, i + 1)
                for j in range(2):
                    for a in range(2):
                        dve.tensor_copy(rows_out[j][a][:, :], chosen["place"][:, a, ds(2 * i + j, 1)])
                for j in range(2):
                    dve.wait_ge(y_ps, 2 * i + j + 1)
                    for a in range(2):
                        last = dve.tensor_scalar(y[j][a][:, :], ps[0:L, j, 3, a * D:(a + 1) * D],
                                                 chosen["score"][:, a, ds(2 * i + j, 1)], None, ALU.mult)
                    last.then_inc(y_ready, 1)


def chosen_feed_forward(nc, g, dram, out):
    xln = nc.dram_tensor("xln", [T, D], F32).ap()
    with ExitStack() as stack:
        g["x"] = stack.enter_context(nc.sbuf_tensor("x3", [L, B, D], F32))
        g["xT"] = stack.enter_context(nc.sbuf_tensor("x3T", [K, C, B, L], F32))
        chosen = {"place": stack.enter_context(nc.sbuf_tensor("chosen_place", [L, 2, E3 + 2], U32)),
                  "score": stack.enter_context(nc.sbuf_tensor("chosen_score", [L, 2, E3], F32)),
                  "pause": stack.enter_context(nc.sbuf_tensor("chosen_pause", [1, 1], F32))}
        normalise(nc, g)
        choose(nc, g, dram, chosen, xln, out)
        chosen_experts(nc, g, dram, chosen, xln, out)


def build(nc, dram, out):
    with ExitStack() as stack, ExitStack() as to_layer_2, ExitStack() as to_layer_1:
        g = {"h": stack.enter_context(nc.sbuf_tensor("h", [L, B + 4, D], F32)),
             "ps": stack.enter_context(nc.psum_tensor("ps", [128, 2, 4, 512], F32)),
             "packs_loaded": stack.enter_context(nc.semaphore("packs_loaded"))}
        first = min(nc.free_semaphores)
        g["sem_banks"] = [range(first + n * SEM_BANK, first + (n + 1) * SEM_BANK) for n in range(2)]
        g["phases"] = 0
        for scope, names in ((stack, ("const", "l3a", "l3f")), (to_layer_2, ("l2f", "l2a")),
                             (to_layer_1, ("l0a", "l0f", "l0r", "l1a", "l1r"))):
            for name in names:
                if name == "l2a":
                    continue
                g["pack_" + name] = scope.enter_context(
                    nc.sbuf_tensor("pack_" + name, [128, offsets(name)[1]], F32))
                g[name] = Fields(g["pack_" + name], name)
        l2a = to_layer_1.enter_context(nc.sbuf_tensor("pack_l2a", [128, offsets("l2a")[1]], F32))
        g["pack_l2a"], g["l2a"] = l2a, Fields(l2a, "l2a")
        g["x"] = to_layer_1.enter_context(nc.sbuf_tensor("x", [L, B + 4, D], F32))
        g["xT"] = to_layer_1.enter_context(nc.sbuf_tensor("xT", [K, C, B, L], F32))
        g["gates"] = to_layer_1.enter_context(nc.sbuf_tensor("gates", [L, B, E01], F32))

        embed(nc, g, dram)
        layers = [lambda: retention(nc, g),
                  lambda: (softmax_attention(nc, g, "l0f", "normed"), route(nc, g, "l0r", False),
                           experts(nc, g, dram, "l0", ACT.Gelu)),
                  lambda: softmax_attention(nc, g, "l1a", "both", conv=True, project=False),
                  lambda: (route(nc, g, "l1r", True), experts(nc, g, dram, "l1", ACT.Silu)),
                  lambda: softmax_attention(nc, g, "l2a", "gated", mask="band"),
                  lambda: (to_layer_1.close(), sub_feed_forward(nc, g, dram)),
                  lambda: (to_layer_1.close(), to_layer_2.close(),
                           softmax_attention(nc, g, "l3a", "plain", mask="causal")),
                  lambda: (to_layer_1.close(), to_layer_2.close(), chosen_feed_forward(nc, g, dram, out))]
        for layer in layers:
            layer()



def lay_rows(w):
    n = w.shape[1]
    return w.reshape(C, K, n).transpose(1, 0, 2).reshape(K, C * n)


def kernel(**inputs):
    import numpy as np
    import concourse.bacc as bacc
    from concourse.bass_utils import run_bass_kernel_spmd

    a = {k: np.asarray(v) for k, v in inputs.items()}
    f32 = np.float32

    def heads(w, twice=False):
        p = np.zeros((w.shape[0], HT, RG, HP), f32)
        s = w.reshape(w.shape[0], RG, HT, HD).transpose(0, 2, 1, 3)
        p[:, :, :, :HD] = s
        if twice:
            p[:, :, :, HD:] = s
        return p.reshape(w.shape[0], HT * 128)

    def head_bias(b, twice=False):
        return heads(b.reshape(1, D), twice).reshape(HT, 128).T

    def rows(b, n=L):
        return np.broadcast_to(b, (n, b.shape[0]))

    def col(b):
        return b.reshape(C, K).T

    side, nb = 32, 84 // 16
    edges = np.arange(1.0 / side, 1.0, 1.0 / side, dtype=f32)
    frac = np.arange(0.0, 1.0 - 1e-6, 1.0 / nb, dtype=f32)
    bins = np.searchsorted(edges, frac, side="right")
    pos = a["L0_tok_pos_table"][(bins[:, None] * side + bins).reshape(-1)]
    px = a["x"][:, :, :80, :80].reshape(B, 3, nb, 16, nb, 16).transpose(1, 3, 5, 0, 2, 4).reshape(CONV_K, 128, B * NP)
    conv_w = a["L0_tok_conv_w"].reshape(D, CONV_K, 128).transpose(2, 1, 0)
    steps = np.arange(L)
    ahead = steps[None, :] - steps[:, None]
    decay = np.where(ahead >= 0, f32(0.99) ** ahead.astype(f32), 0.0) / f32(np.sqrt(f32(D)))
    wqkv0 = a["L0_attn_W_qkv"].T
    b0 = a["L0_attn_b_qkv"]
    wqf, bqf = a["L0_ffn_qkv_w"], a["L0_ffn_qkv_b"]
    fields = {
        "tok": {"conv_w": conv_w.reshape(128, -1), "patches": px.transpose(1, 0, 2).reshape(128, -1),
                "pos": np.tile(pos, (GB, 1)), "conv_b": rows(a["L0_tok_conv_b"], GB * NP)},
        "const": {"ident": np.eye(128, dtype=f32), "neg_half": np.full((L, 2), -0.5, f32), "iota": rows(np.arange(64, dtype=f32))},
        "l0a": {"wq": lay_rows(wqkv0[:, :D]), "wk": lay_rows(wqkv0[:, D:2 * D]), "wv": lay_rows(wqkv0[:, 2 * D:]),
                "bq": col(b0[:D]), "bk": col(b0[D:2 * D]), "bv": rows(b0[2 * D:]), "decay": decay},
        "l0f": {"wq": lay_rows(heads(wqf[:, :D])), "wk": lay_rows(heads(wqf[:, D:2 * D])),
                "wv": lay_rows(wqf[:, 2 * D:]), "bq": head_bias(bqf[:D]), "bk": head_bias(bqf[D:2 * D]),
                "bv": rows(bqf[2 * D:]), "g": col(a["L0_ffn_ln1_g"]), "b": col(a["L0_ffn_ln1_b"]),
                "wo": lay_rows(a["L0_ffn_proj_w"]), "bo": rows(a["L0_ffn_proj_b"])},
    }
    w1a, b1a = a["L1_attn_qkv_w"].T, a["L1_attn_qkv_b"]
    half = np.arange(128) % HP < HD
    mix = np.stack([np.ones(128), 1.0 - half, np.where(half, 1.2, -0.2), np.where(half, 0.0, -0.2)], 1)
    fields["l1a"] = {"wq": lay_rows(heads(w1a[:, :D], True)), "wk": lay_rows(heads(w1a[:, D:2 * D], True)),
                     "wv": lay_rows(w1a[:, 2 * D:]), "bq": head_bias(b1a[:D], True),
                     "bk": head_bias(b1a[D:2 * D], True), "bv": rows(b1a[2 * D:]), "g": col(a["L1_attn_ln_g"]),
                     "b": col(a["L1_attn_ln_b"]), "mix": mix.astype(f32)}
    fields["l0r"] = {"g": col(a["L0_ffn_ln2_g"]), "b": col(a["L0_ffn_ln2_b"]), "gate": lay_rows(a["L0_ffn_gate_w"]),
                     "b2": a["L0_ffn_b2"]}
    fields["l1r"] = {"g": col(a["L1_ffn_ln_gamma"]), "b": col(a["L1_ffn_ln_beta"]),
                     "gate": lay_rows(a["L1_ffn_router_w"])}

    def up(w):
        return w.reshape(-1, C, K, F).transpose(0, 2, 1, 3).reshape(-1, K, C * F)

    def down(w):
        return w.reshape(-1, FM, 128, D).transpose(0, 2, 1, 3).reshape(-1, 128, FM * D)

    w2 = {n: a["L2_attn_W_" + n] for n in ("q_lin", "k_lin", "v_lin", "q_loc", "k_loc", "v_loc", "out", "g1", "g2")}
    b2 = {n: a["L2_attn_b_" + n] for n in w2}
    apart = np.abs(ahead)
    fields["l2a"] = {"wq": lay_rows(heads(w2["q_loc"])), "wk": lay_rows(heads(w2["k_loc"])),
                     "wv": lay_rows(w2["v_loc"]), "bq": head_bias(b2["q_loc"]), "bk": head_bias(b2["k_loc"]),
                     "bv": rows(b2["v_loc"]), "g": col(a["L2_attn_gamma1"]), "b": col(a["L2_attn_beta1"]),
                     "band": np.where(apart <= 32, 0.0, NEG).astype(f32), "lin_wq": lay_rows(w2["q_lin"]),
                     "lin_wk": lay_rows(w2["k_lin"]), "lin_wv": lay_rows(w2["v_lin"]), "lin_bq": col(b2["q_lin"]),
                     "lin_bk": col(b2["k_lin"]), "lin_bv": rows(b2["v_lin"]),
                     "wg1": w2["g1"].reshape(3 * C, K, D).transpose(1, 0, 2).reshape(K, -1), "bg1": col(b2["g1"]),
                     "wg2": lay_rows(w2["g2"]), "bg2": rows(b2["g2"]), "wo": lay_rows(w2["out"]),
                     "bo": rows(b2["out"])}
    sub_up = np.tile(a["L2_ffn_W1"].transpose(0, 2, 1, 3).reshape(NS, NR, NM * 32), (1, len(PAIRS), 1))
    sub_down = np.zeros((4, 32, NS, MT, HP), f32)
    sub_down[..., :NR] = a["L2_ffn_W2"].reshape(NS, MT, 4, 32, NR).transpose(2, 3, 0, 1, 4)
    spread = np.zeros((3, 32, 8, 4, 32), f32)
    for n in range(32):
        spread[:, n, n // 4, n % 4] = 1.0
    centres = np.zeros((NS, NR, NS, NM), f32)
    for n in range(NS):
        centres[n, :, n] = a["L2_ffn_C"][n].T
    b2s = np.zeros((2, NM, RG, 2, HP), f32)
    for half in range(2):
        b2s[half, :, :, half, :NR] = a["L2_ffn_b2"][half::2].transpose(1, 0, 2)
    g1s = np.zeros((RG, HP, 2, 64), f32)
    g1s[:, :NR] = a["L2_ffn_G1"].reshape(RG, 2, NR, 64).transpose(0, 2, 1, 3)
    less = np.array([[-(p > 1), -(p > 2), -(q > 1), -(q > 2)] for p, q in PAIRS], f32).repeat(NR, 0)
    sub_p = a["L2_ffn_P"].transpose(1, 0, 2)
    fields["l2f"] = {"p": lay_rows(sub_p.reshape(D, 128)),
                     "p8": lay_rows(np.tile(sub_p[:, :, None, :], (1, 1, len(PAIRS), 1)).reshape(D, NS * 128)),
                     "centres": centres.reshape(128, -1), "b2": b2s.reshape(128, -1), "parts": less,
                     "b1": a["L2_ffn_b1"].reshape(NS * MT, 128).T, "g1": g1s.reshape(128, -1),
                     "g1b": a["L2_ffn_g1b"][:, None], "g2": a["L2_ffn_G2"], "g2b": rows(a["L2_ffn_g2b"])}
    fields["l3f"] = {"choose": lay_rows(a["L3_ffn_gate_weight"].T), "ws_g": lay_rows(a["L3_ffn_Ws_g"].T),
                     "ws_u": lay_rows(a["L3_ffn_Ws_u"].T),
                     "ws_d": a["L3_ffn_Ws_d"].T.reshape(SM, 128, D).transpose(1, 0, 2)}
    w3 = a["L3_attn_w_attn"]
    fields["l3a"] = {"wq": lay_rows(heads(w3[:, :D])), "wk": lay_rows(heads(w3[:, D:2 * D])),
                     "wv": lay_rows(w3[:, 2 * D:]), "causal": np.where(ahead <= 0, 0.0, NEG).astype(f32),
                     "wo": lay_rows(a["L3_attn_w_proj"]), "bo": rows(a["L3_attn_b_proj"])}

    arrays = {"txt": a["txt"], "l3_gate": up(a["L3_ffn_Wg"].transpose(0, 2, 1)),
              "l3_up": up(a["L3_ffn_Wu"].transpose(0, 2, 1)), "l3_down": down(a["L3_ffn_Wd"].transpose(0, 2, 1)),
              "sub_up": sub_up, "sub_down": sub_down.reshape(128, -1), "sub_spread": spread.reshape(96, -1),
              "l0_up": up(a["L0_ffn_w1"]), "l0_down": down(a["L0_ffn_w2"]),
              "l0_b1": a["L0_ffn_b1"].reshape(E01, FM, 128).transpose(0, 2, 1),
              "l1_up": up(a["L1_ffn_w1"]), "l1_down": down(a["L1_ffn_w2"])}
    for pack in PACKS:
        where, width = offsets(pack)
        arr = np.zeros((128, width), f32)
        for name, (n, start, cols) in where.items():
            arr[:n, start:start + cols] = fields[pack][name].reshape(n, cols)
        arrays["pack_" + pack] = arr

    nc = bacc.Bacc("TRN2", target_bir_lowering=False, num_devices=1)
    feed, dram = {}, {}
    for name, arr in arrays.items():
        feed["in_" + name] = np.ascontiguousarray(arr)
        dram[name] = nc.dram_tensor("in_" + name, arr.shape, mybir.dt.from_np(arr.dtype), kind="ExternalInput").ap()
    out = nc.dram_tensor("out", (B, L, D), F32, kind="ExternalOutput").ap()
    build(nc, dram, out)
    r = run_bass_kernel_spmd(nc, [feed], core_ids=[0])
    return r.results[0]["out"]
```
